# Optimizing a Trainium2 kernel written in Bass

```python
import numpy as np
import jax
import jax.numpy as jnp

def _softmax(x, axis=-1):
    return jax.nn.softmax(x, axis=axis)

def _gelu(x):
    return jax.nn.gelu(x, approximate=True)

def _silu(x):
    return jax.nn.silu(x)

def _sigmoid(x):
    return jax.nn.sigmoid(x)

def _layernorm(x, axis=-1, eps=1e-05):
    m = jnp.mean(x, axis=axis, keepdims=True)
    v = jnp.var(x, axis=axis, keepdims=True)
    return (x - m) / jnp.sqrt(v + eps)

def _scatter_add(tgt, idx, src, axis=0):
    return tgt.at[idx].add(src)

def _segment_sum(src, seg, n):
    return jax.ops.segment_sum(src, seg, n)
kernel_name = 'mk_adaln_d1_jaxref_r8_60881f'

def setup_inputs(seed: int=0):
    np.random.seed(seed)
    _w = jnp.asarray

    def _L0_attn_setup():
        import jax, jax.numpy as jnp
        import numpy as np
        B, S, E, H = (2, 256, 128, 16)
        D = E // H
        TRIL = D * (D + 1) // 2
        key = jax.random.key(seed)
        ks = jax.random.split(key, 6)
        return {'x': jax.random.normal(ks[0], (B, S, E), dtype=jnp.float32), 'params': jax.random.normal(ks[1], (H, TRIL), dtype=jnp.float32), 'Wv': jax.random.normal(ks[2], (E, E), dtype=jnp.float32) * 0.02, 'bv': jax.random.normal(ks[3], (E,), dtype=jnp.float32) * 0.02, 'Wo': jax.random.normal(ks[4], (E, E), dtype=jnp.float32) * 0.02, 'bo': jax.random.normal(ks[5], (E,), dtype=jnp.float32) * 0.02}
    _L0_attn_in = _L0_attn_setup()

    def _L0_ffn_setup():
        import jax, jax.numpy as jnp
        import numpy as np
        B, S, D, H, L, E, K = (4, 128, 128, 16, 2, 8, 2)
        DFF = 4 * D

        def _ln(x, w, b):
            m = x.mean(-1, keepdims=True)
            v = x.var(-1, keepdims=True)
            return (x - m) / jnp.sqrt(v + 1e-05) * w + b

        def _attn(x, wq, wk, wv, wo, bq, bk, bv, bo):
            Bb, T, C = x.shape
            hd = C // H
            q = (x @ wq + bq).reshape(Bb, T, H, hd).transpose(0, 2, 1, 3)
            k = (x @ wk + bk).reshape(Bb, T, H, hd).transpose(0, 2, 1, 3)
            v = (x @ wv + bv).reshape(Bb, T, H, hd).transpose(0, 2, 1, 3)
            att = jnp.einsum('bhqd,bhkd->bhqk', q, k) * hd ** (-0.5)
            causal = jnp.tril(jnp.ones((T, T), bool))
            att = jnp.where(causal, att, -jnp.inf)
            att = jax.nn.softmax(att, axis=-1)
            y = jnp.einsum('bhqk,bhkd->bhqd', att, v).transpose(0, 2, 1, 3).reshape(Bb, T, C)
            return y @ wo + bo

        def _ffn(h, w1, b1, w2, b2):
            return jax.nn.gelu(h @ w1 + b1, approximate=False) @ w2 + b2

        def _combine_weights(logits):
            vals, idx = jax.lax.top_k(logits, K)
            w = jax.nn.softmax(vals, axis=-1)
            onehot = (idx[..., None] == jnp.arange(E)).astype(w.dtype)
            return jnp.sum(w[..., None] * onehot, axis=-2)

        def _token_moe(h, gw, gb, w1, b1, w2, b2):
            cw = _combine_weights(h @ gw + gb)
            out = jnp.zeros_like(h)
            for e in range(E):
                out = out + _ffn(h, w1[e], b1[e], w2[e], b2[e]) * cw[..., e:e + 1]
            return out

        def _seq_moe(h, gw, gb, w1, b1, w2, b2):
            cw = _combine_weights(h.mean(axis=1) @ gw + gb)
            out = jnp.zeros_like(h)
            for e in range(E):
                out = out + _ffn(h, w1[e], b1[e], w2[e], b2[e]) * cw[:, e, None, None]
            return out
        key = jax.random.key(seed)
        ks = jax.random.split(key, 9)
        n = lambda k, shp: jax.random.normal(k, shp, dtype=jnp.float32) * 0.02
        return {'x': jax.random.normal(ks[0], (B, S, D), dtype=jnp.float32), 'ln1_w': jnp.ones((L, D), jnp.float32), 'ln1_b': jnp.zeros((L, D), jnp.float32), 'ln2_w': jnp.ones((L, D), jnp.float32), 'ln2_b': jnp.zeros((L, D), jnp.float32), 'wq': n(ks[1], (L, D, D)), 'wk': n(ks[2], (L, D, D)), 'wv': n(ks[3], (L, D, D)), 'wo': n(ks[4], (L, D, D)), 'bq': jnp.zeros((L, D), jnp.float32), 'bk': jnp.zeros((L, D), jnp.float32), 'bv': jnp.zeros((L, D), jnp.float32), 'bo': jnp.zeros((L, D), jnp.float32), 'gate_w': n(ks[5], (L, D, E)), 'gate_b': jnp.zeros((L, E), jnp.float32), 'e_w1': n(ks[6], (L, E, D, DFF)), 'e_b1': jnp.zeros((L, E, DFF), jnp.float32), 'e_w2': n(ks[7], (L, E, DFF, D)), 'e_b2': jnp.zeros((L, E, D), jnp.float32)}
    _L0_ffn_in = _L0_ffn_setup()
    _L0_c = _w((lambda *s: np.random.randn(*s).astype(np.float32) * 0.05)(8, 128))
    _L0_wmod = _w((lambda *s: np.random.randn(*s).astype(np.float32) * 0.05)(128, 6 * 128) * 128 ** (-0.5))
    _d = {'L0_attn_x': _L0_attn_in['x'], 'L0_attn_params': _L0_attn_in['params'], 'L0_attn_Wv': _L0_attn_in['Wv'], 'L0_attn_bv': _L0_attn_in['bv'], 'L0_attn_Wo': _L0_attn_in['Wo'], 'L0_attn_bo': _L0_attn_in['bo'], 'L0_ffn_ln1_w': _L0_ffn_in['ln1_w'], 'L0_ffn_ln1_b': _L0_ffn_in['ln1_b'], 'L0_ffn_ln2_w': _L0_ffn_in['ln2_w'], 'L0_ffn_ln2_b': _L0_ffn_in['ln2_b'], 'L0_ffn_wq': _L0_ffn_in['wq'], 'L0_ffn_wk': _L0_ffn_in['wk'], 'L0_ffn_wv': _L0_ffn_in['wv'], 'L0_ffn_wo': _L0_ffn_in['wo'], 'L0_ffn_bq': _L0_ffn_in['bq'], 'L0_ffn_bk': _L0_ffn_in['bk'], 'L0_ffn_bv': _L0_ffn_in['bv'], 'L0_ffn_bo': _L0_ffn_in['bo'], 'L0_ffn_gate_w': _L0_ffn_in['gate_w'], 'L0_ffn_gate_b': _L0_ffn_in['gate_b'], 'L0_ffn_e_w1': _L0_ffn_in['e_w1'], 'L0_ffn_e_b1': _L0_ffn_in['e_b1'], 'L0_ffn_e_w2': _L0_ffn_in['e_w2'], 'L0_ffn_e_b2': _L0_ffn_in['e_b2'], 'L0_c': _L0_c, 'L0_wmod': _L0_wmod}
    _x0 = _d['L0_attn_x']
    _d['L0_attn_x'] = jax.random.normal(jax.random.fold_in(jax.random.key(seed), 1), (8, 512, 128), dtype=_x0.dtype)
    del _x0
    return _d

def reference(L0_attn_x, L0_attn_params, L0_attn_Wv, L0_attn_bv, L0_attn_Wo, L0_attn_bo, L0_ffn_ln1_w, L0_ffn_ln1_b, L0_ffn_ln2_w, L0_ffn_ln2_b, L0_ffn_wq, L0_ffn_wk, L0_ffn_wv, L0_ffn_wo, L0_ffn_bq, L0_ffn_bk, L0_ffn_bv, L0_ffn_bo, L0_ffn_gate_w, L0_ffn_gate_b, L0_ffn_e_w1, L0_ffn_e_b1, L0_ffn_e_w2, L0_ffn_e_b2, L0_c, L0_wmod):

    def _L0_attn_ref(x, params, Wv, bv, Wo, bo):
        import jax, jax.numpy as jnp
        import numpy as np
        B, S, E, H = (2, 256, 128, 16)
        D = E // H
        TRIL = D * (D + 1) // 2
        bs, seq_len, emb_dim = x.shape
        d = D
        rows, cols = jnp.tril_indices(d)
        tril = jnp.zeros((H, d, d), dtype=x.dtype).at[:, rows, cols].set(params)
        Wqk = jnp.einsum('hij,hkj->hik', tril, tril)
        xh = x.reshape(bs, seq_len, H, d)
        t = jnp.einsum('bshd,hde->bshe', xh, Wqk)
        scores = jnp.einsum('bshe,bthe->bhst', t, xh) / jnp.sqrt(jnp.asarray(d, x.dtype))
        attn = jax.nn.softmax(scores, axis=-1)
        Vh = (x @ Wv.T + bv).reshape(bs, seq_len, H, d)
        out = jnp.einsum('bhst,bthd->bshd', attn, Vh).reshape(bs, seq_len, emb_dim)
        return out @ Wo.T + bo

    def _L0_ffn_ref(x, ln1_w, ln1_b, ln2_w, ln2_b, wq, wk, wv, wo, bq, bk, bv, bo, gate_w, gate_b, e_w1, e_b1, e_w2, e_b2):
        import jax, jax.numpy as jnp
        import numpy as np
        B, S, D, H, L, E, K = (4, 128, 128, 16, 2, 8, 2)
        DFF = 4 * D

        def _ln(x, w, b):
            m = x.mean(-1, keepdims=True)
            v = x.var(-1, keepdims=True)
            return (x - m) / jnp.sqrt(v + 1e-05) * w + b

        def _attn(x, wq, wk, wv, wo, bq, bk, bv, bo):
            Bb, T, C = x.shape
            hd = C // H
            q = (x @ wq + bq).reshape(Bb, T, H, hd).transpose(0, 2, 1, 3)
            k = (x @ wk + bk).reshape(Bb, T, H, hd).transpose(0, 2, 1, 3)
            v = (x @ wv + bv).reshape(Bb, T, H, hd).transpose(0, 2, 1, 3)
            att = jnp.einsum('bhqd,bhkd->bhqk', q, k) * hd ** (-0.5)
            causal = jnp.tril(jnp.ones((T, T), bool))
            att = jnp.where(causal, att, -jnp.inf)
            att = jax.nn.softmax(att, axis=-1)
            y = jnp.einsum('bhqk,bhkd->bhqd', att, v).transpose(0, 2, 1, 3).reshape(Bb, T, C)
            return y @ wo + bo

        def _ffn(h, w1, b1, w2, b2):
            return jax.nn.gelu(h @ w1 + b1, approximate=False) @ w2 + b2

        def _combine_weights(logits):
            vals, idx = jax.lax.top_k(logits, K)
            w = jax.nn.softmax(vals, axis=-1)
            onehot = (idx[..., None] == jnp.arange(E)).astype(w.dtype)
            return jnp.sum(w[..., None] * onehot, axis=-2)

        def _token_moe(h, gw, gb, w1, b1, w2, b2):
            cw = _combine_weights(h @ gw + gb)
            out = jnp.zeros_like(h)
            for e in range(E):
                out = out + _ffn(h, w1[e], b1[e], w2[e], b2[e]) * cw[..., e:e + 1]
            return out

        def _seq_moe(h, gw, gb, w1, b1, w2, b2):
            cw = _combine_weights(h.mean(axis=1) @ gw + gb)
            out = jnp.zeros_like(h)
            for e in range(E):
                out = out + _ffn(h, w1[e], b1[e], w2[e], b2[e]) * cw[:, e, None, None]
            return out
        for l in range(L):
            x = x + _attn(_ln(x, ln1_w[l], ln1_b[l]), wq[l], wk[l], wv[l], wo[l], bq[l], bk[l], bv[l], bo[l])
            h = _ln(x, ln2_w[l], ln2_b[l])
            moe = _token_moe if l % 2 == 0 else _seq_moe
            x = x + moe(h, gate_w[l], gate_b[l], e_w1[l], e_b1[l], e_w2[l], e_b2[l])
        return x
    x = L0_attn_x
    mod = (_silu(L0_c) @ L0_wmod).reshape(L0_c.shape[0], 6, 1, -1)
    sa, ca, ga, sb, cb, gb = (mod[:, 0], mod[:, 1], mod[:, 2], mod[:, 3], mod[:, 4], mod[:, 5])
    ga = (2 * (ga >= 0) - 1) * jnp.maximum(jnp.abs(ga), 0.25)
    gb = (2 * (gb >= 0) - 1) * jnp.maximum(jnp.abs(gb), 0.25)
    h = _layernorm(x, axis=-1) * (1 + ca) + sa
    x = x + ga * _L0_attn_ref(h, L0_attn_params, L0_attn_Wv, L0_attn_bv, L0_attn_Wo, L0_attn_bo)
    h = _layernorm(x, axis=-1) * (1 + cb) + sb
    x = x + gb * _L0_ffn_ref(h, L0_ffn_ln1_w, L0_ffn_ln1_b, L0_ffn_ln2_w, L0_ffn_ln2_b, L0_ffn_wq, L0_ffn_wk, L0_ffn_wv, L0_ffn_wo, L0_ffn_bq, L0_ffn_bk, L0_ffn_bv, L0_ffn_bo, L0_ffn_gate_w, L0_ffn_gate_b, L0_ffn_e_w1, L0_ffn_e_b1, L0_ffn_e_w2, L0_ffn_e_b2)
    return x

_drawn_inputs = setup_inputs


def setup_inputs(seed=0):
    import zlib

    import numpy as np

    out = dict(_drawn_inputs(seed))
    spreads = {'L0_ffn_ln1_w': (1.0, 0.6),
     'L0_ffn_ln1_b': (0.0, 0.8),
     'L0_ffn_ln2_w': (1.0, 0.6),
     'L0_ffn_ln2_b': (0.0, 0.8),
     'L0_ffn_bq': (0.0, 0.8),
     'L0_ffn_bk': (0.0, 0.8),
     'L0_ffn_bv': (0.0, 0.8),
     'L0_ffn_bo': (0.0, 0.1),
     'L0_ffn_gate_b': (0.0, 0.446),
     'L0_ffn_e_b1': (0.0, 0.8),
     'L0_ffn_e_b2': (0.0, 0.341)}
    factors = {'L0_attn_params': 6.849,
     'L0_attn_Wv': 6.098,
     'L0_attn_bv': 8.0,
     'L0_attn_Wo': 6.047,
     'L0_attn_bo': 8.0,
     'L0_ffn_wq': 8.0,
     'L0_ffn_wk': 8.0,
     'L0_ffn_wv': 8.0,
     'L0_ffn_wo': 6.262,
     'L0_ffn_gate_w': 2.847,
     'L0_ffn_e_w1': 4.103,
     'L0_ffn_e_w2': 3.763}
    for name, (base, spread) in spreads.items():
        noise = np.random.default_rng([zlib.crc32(name.encode()), seed]).standard_normal(out[name].shape)
        drawn = base * np.exp(spread * noise) if base else spread * noise
        out[name] = jnp.asarray(drawn.astype(out[name].dtype))
    for name, factor in factors.items():
        out[name] = (out[name] * factor).astype(out[name].dtype)
    return out
```

```python
from contextlib import ExitStack

import concourse.bass as bass
from concourse import mybir

F32 = mybir.dt.float32
BF16 = mybir.dt.bfloat16
U32 = mybir.dt.uint32
I32 = mybir.dt.int32
ALU = mybir.AluOpType
ACT = mybir.ActivationFunctionType
AX_X = mybir.AxisListType.X

P = 128
EPS = 1e-5
NEG = -1e30
E_CONST = 2.718281828459045


class Phase:

    def __init__(self, s, first_batch, causal, own_k, stream, wq, wk, wv, bq, bk, bv, hw, hb, n):
        self.s, self.first_batch, self.causal, self.own_k, self.stream = s, first_batch, causal, own_k, stream
        self.wq, self.wk, self.wv, self.bq, self.bk, self.bv = wq, wk, wv, bq, bk, bv
        self.hw, self.hb, self.n = hw, hb, n


def wait(eng, sem, value):
    if isinstance(value, int) and value <= 0:
        return
    eng.wait_ge(sem, value)


def adaln_block(nc, x_in, params, Wv, bv, Wo, bo, ln1_w, ln1_b, ln2_w, ln2_b, wq, wk, wv, wo, bq, bk, bv2, bo2,
                gate_w, gate_b, e_w1, e_b1, e_w2, e_b2, c_in, wmod, out):
    NB, S, D = x_in.shape
    H = params.shape[0]
    HD = D // H
    TC = S // P
    E = gate_w.shape[2]
    FF = e_w1.shape[3]
    FC = FF // P
    L = gate_w.shape[0]
    HG = 4
    G = H // HG
    PAIRS = H // 2
    STEPS = G * TC
    UNITS = STEPS * HG
    LAG = 8
    SEL = 1
    SCALE = float(HD) ** -0.5
    assert D == P and HD == 8 and NB == 8 and STEPS == 16 and E == 8 and L == 2

    Q_PARTS = (0, 0, 0, 1, 1, 2)
    K_PARTS = (0, 1, 2, 0, 1, 0)
    NPROD = len(Q_PARTS)
    KROWS = NPROD * HD
    SHIFT_ROW = 64 + KROWS
    STACK_DMAS = NPROD * 2
    SHIFT_DMAS = 4

    with ExitStack() as ctx:
        def sb(name, shape, dt=F32):
            return ctx.enter_context(nc.sbuf_tensor(name, shape, dt))

        def psum(name, shape=(P, 512), dt=F32):
            return ctx.enter_context(nc.psum_tensor(name, list(shape), dt))

        def sem(name):
            return ctx.enter_context(nc.semaphore(name))

        xr = sb("xr", [P, NB * S])
        yr = sb("yr", [P, NB * S])

        ident = sb("ident", [P, P])
        identb = sb("identb", [P, P], BF16)
        mask_q = sb("mask_q", [P, P], BF16)
        mask_k = sb("mask_k", [P, P], BF16)
        head_sel = sb("head_sel", [P, 36])
        ones8 = sb("ones8", [E, P])
        blockdiag = sb("blockdiag", [P, H])
        iota8 = sb("iota8", [P, E])
        minus_half = sb("minus_half", [P, NB * TC])
        e_const = sb("e_const", [P, TC])

        NROW = 12 + 2 * E * FC + 1 + L
        rows = sb("rows", [NROW, P])
        cols = sb("cols", [P, NROW])
        LN1W, LN1B, LN2W, LN2B, BQ, BK, B1, BV = 0, 2, 4, 6, 8, 10, 12, NROW - 1 - L
        bias_row = sb("bias_row", [P, 1 + L, P])
        gate_bias = sb("gate_bias", [P, L, E])
        gate_sb = sb("gate_sb", [P, L, E])
        wq_sb = sb("wq_sb", [P, L, P])
        wk_sb = sb("wk_sb", [P, L, P])
        wv_sb = sb("wv_sb", [P, L, P])
        wo_sb = sb("wo_sb", [P, L, P])
        w_outer = sb("w_outer", [P, 2, P])
        wo_gated = sb("wo_gated", [P, P])
        tril_rows = sb("tril_rows", [P, HD])
        tril_block = sb("tril_block", [P, P])
        w1_sb = sb("w1_sb", [P, E, FF])
        w2_sb = sb("w2_sb", [P, E, FC, P])
        b2_sb = sb("b2_sb", [E, P])
        cond = sb("cond", [NB, P])
        cond_a = sb("cond_a", [NB, P])
        cond_b = sb("cond_b", [NB, P])
        condT = sb("condT", [P, NB])
        mod_cols = sb("mod_cols", [P, 2, NB])
        modB = sb("modB", [P, NB, 4, P])

        stats = sb("stats", [P, TC, 6])
        mean_var = sb("mean_var", [P, TC, 2])
        var_eps = sb("var_eps", [P, TC])
        rstd = sb("rstd", [P, TC])
        xn = sb("xn", [P, TC, P])
        hT = sb("hT", [P, S])
        q_f = sb("q_f", [P, S])
        k_f = sb("k_f", [P, S])
        q_parts = sb("q_parts", [P, 3, S], BF16)
        k_parts = sb("k_parts", [P, 3, S], BF16)
        stacks = sb("stacks", [P, 6, PAIRS, S], BF16)
        Qs = [[stacks[:, 2 * n + a] for a in range(2)] for n in range(2)]
        Ks = [stacks[:, 4 + n] for n in range(2)]
        Vt = [sb(f"Vt{n}", [P, TC, H, 32]) for n in range(2)]
        NPB = 2 * TC
        work = sb("work", [P, NPB, S])
        probs = [work[:, n, :] for n in range(NPB)]
        flat = work[:, :, :].rearrange("p n s -> p (n s)")
        wmod_sb = flat[:, 0:6 * P]
        w_raw = flat[:, 6 * P:8 * P].rearrange("p (n d) -> p n d", n=2)
        batch_row = flat[0:NB, 8 * P:16 * P].rearrange("p (b d) -> p b d", b=NB)
        mod_row = flat[0:NB, 16 * P:20 * P].rearrange("p (n d) -> p n d", n=4)
        mod_tmp = flat[0:NB, 20 * P:22 * P].rearrange("p (n d) -> p n d", n=2)
        mod_tmp2 = flat[0:NB, 22 * P:24 * P].rearrange("p (n d) -> p n d", n=2)
        row_max = sb("row_max", [P, UNITS])
        shift_tok = [sb(f"shift_tok{n}", [P, TC, 2, HG], BF16) for n in range(2)]
        shift = [sb(f"shift{n}", [2 * HG, S], BF16) for n in range(2)]
        av_sb = [sb(f"av_sb{n}", [P, S]) for n in range(2)]
        recip = sb("recip", [P, TC, HG])
        y_sb = sb("y_sb", [P, TC, P])
        yT = sb("yT", [P, S])
        bias_gated = sb("bias_gated", [P, P])
        stats2 = sb("stats2", [P, TC, 6])
        mean_var2 = sb("mean_var2", [P, TC, 2])
        var_eps2 = sb("var_eps2", [P, TC])
        rstd2 = sb("rstd2", [P, TC])

        hid = [work[:, n * FC:(n + 1) * FC, :] for n in range(2)]
        logits = sb("logits", [P, TC, E])
        top8 = sb("top8", [P, TC, 8])
        top_idx = sb("top_idx", [P, TC, 8], U32)
        top_idxf = sb("top_idxf", [P, TC, 2])
        gap = sb("gap", [P, TC])
        gap_exp = sb("gap_exp", [P, TC])
        denom = sb("denom", [P, TC])
        weight = sb("weight", [P, TC, 2])
        pick = [sb(f"pick{n}", [P, TC, E]) for n in range(4)]
        combine = sb("combine", [P, TC, E])
        combineT = av_sb[0][0:E, :]
        seq_xn = [xn, y_sb]
        stats_all = sb("stats_all", [P, NB * TC, 6])
        mv_all = sb("mv_all", [P, NB * TC, 2])
        ve_all = sb("ve_all", [P, NB * TC])
        rstd_all = sb("rstd_all", [P, NB * TC])
        hsum = sb("hsum", [P, NB])
        seq_both = sb("seq_both", [NB, 2, NB, 2])
        seqB = sb("seqB", [P, 2 * NB])
        seq_idx = sb("seq_idx", [P, 2 * NB], I32)
        NSLOT = 4
        w1_slot = [w1_sb[:, n, :] for n in range(NSLOT)]
        w2_slot = [w2_sb[:, n, :, :] for n in range(NSLOT)]
        b1_slot = [sb(f"b1_slot{n}", [P, FC]) for n in range(NSLOT)]
        b2_slot = [Vt[0][:, 0, 4 * n:4 * n + 4, :].rearrange("p h d -> p (h d)") for n in range(NSLOT)]
        hT_all = stacks[:, 0:2].rearrange("p a b s -> p (a b s)").bitcast(F32)

        q_dram = nc.dram_tensor("q_parts_dram", [P, 3, S], BF16, kind="Internal").ap()
        k_dram = nc.dram_tensor("k_parts_dram", [P, 3, S], BF16, kind="Internal").ap()

        banks = [psum(f"bank{n}") for n in range(8)]
        SA = banks[0:2]
        ST = banks[2:5]
        AV = banks[5]
        MA, MB = banks[6], banks[7]
        HB = banks[0:4]
        YB = banks[4:6]

        ALL_SMALL = 16 * (4 + HD + 9 + 1 + 2 * L + 6)
        DVE_SILU = 2 * len(Vt) + 2 * len(Ks) + 3
        DVE_CONDT = DVE_SILU + 2
        DVE_MODROW = DVE_CONDT + 13
        DVE_SETUP = DVE_MODROW + 1
        s_ld = sem("small_loaded")
        s_x0 = sem("x_first_loaded")
        s_x = sem("x_loaded")
        s_w = sem("expert_weights_loaded")
        s_pool0 = sem("pool_setup_chain")
        s_const = sem("constants_built")
        s_dve0 = sem("dve_setup_chain")
        s_pe0 = sem("pe_setup")
        s_act0 = sem("act_setup")
        s_own_pool = sem("pool_own")
        s_own_dve = sem("dve_own")
        s_own_sp = sem("sp_own")

        def attention_names(tag, more=()):
            names = ("stats_done", "rstd_chain", "xn_ready", "xT_ready", "hT_ready", "q_proj", "k_proj", "v_proj",
                     "qf_ready", "q_copied", "kf_ready", "k_copied", "q_split_chain", "k_split_chain", "q_split",
                     "k_split", "q_stacked", "k_stacked", "q_spilled", "k_spilled", "v_ready", "scores_q", "max_done", "max_T", "shift_half",
                     "shift_split", "shift_copied", "shift_rows0", "shift_rows1", "scores_k", "exp_done", "av_done", "av_copied", "heads_sel",
                     "recip_done", "y_ready", "yT_done", "yT_copied", "out_proj", "bias_added", "residual_done",
                     "mv_chain") + more
            return {n: sem(f"{tag}_{n}") for n in names}

        outer = Phase(attention_names("o", ("wo_gated", "bias_gated", "stats2_done", "tail_chain", "tail_normed",
                                                       "tail_scaled", "tail_done", "mv2_chain")), first_batch=0, causal=False, own_k=False, stream=xr,
                      wq=tril_block[:, :], wk=None, wv=w_outer[:, 0, :], bq=None, bk=None, bv=cols[:, BV:BV + 1],
                      hw=None, hb=None, n=None)
        layer_sems = attention_names("l")
        layer = [Phase(layer_sems, first_batch=n * NB, causal=True, own_k=True, stream=yr,
                       wq=wq_sb[:, n, :], wk=wk_sb[:, n, :], wv=wv_sb[:, n, :],
                       bq=cols[:, BQ + n:BQ + n + 1], bk=cols[:, BK + n:BK + n + 1], bv=cols[:, BV + 1 + n:BV + 2 + n],
                       hw=cols[:, LN1W + n:LN1W + n + 1], hb=cols[:, LN1B + n:LN1B + n + 1], n=n) for n in range(2)]
        tok = {n: sem(f"t_{n}") for n in (
            "stats_done", "mv_chain", "rstd_chain", "xn_ready", "xT_ready", "hT_ready", "logits_ready", "logits_copied",
            "gap_ready", "gap_exp", "gate_chain", "combine_ready", "combine_T", "combineT_copied", "b2_ready",
            "b2_added", "hidden", "gelu_done", "expert_out", "accumulated")}
        seq = {n: sem(f"s_{n}") for n in (
            "mv_chain", "aggregated", "rstd_chain", "rstd_ready", "xn_ready", "xT_ready", "hT_ready", "logits_ready", "gate_chain",
            "gap_ready", "gap_exp", "both_ready", "both_B", "picked", "loaded0", "loaded1", "loaded2", "loaded3", "hidden", "gelu_done", "expert_out",
            "b2_added", "accumulated", "gated", "added", "stored")}

        seq_loaded = [seq["loaded0"], seq["loaded1"], seq["loaded2"], seq["loaded3"]]
        SLOT_DMAS = 4

        def rows_shifted(ph, g):
            return (ph.s["shift_rows0"], ph.s["shift_rows1"])[g % 2]

        def tokens(stream, b, c=None):
            if c is None:
                return stream[:, bass.ds(b * S, S)].rearrange("p (c d) -> p c d", c=TC)
            return stream[:, bass.ds(b * S + c * P, P)]

        def batches(eng, ph, body):
            n = ph.first_batch
            body(n, 0, False, True, True)
            with eng.Fori(0, (NB - 2) // 2) as j:
                body(j * 2 + (n + 1), 1, True, True, True)
                body(j * 2 + (n + 2), 0, True, True, True)
            body(n + NB - 1, 1, True, True, False)
            body(n + NB, 0, True, False, False)

        def second_pass(i, q, prev, cur, k, lag):
            if k < lag:
                return i - 1, 1 - q, k + STEPS - lag, prev
            return i, q, k - lag, cur

        def first_width(ph, c):
            return (c + 1) * P if ph.causal else S

        def second_low(ph, c):
            return c * P if ph.causal else 0

        block = ctx.enter_context(nc.Block())

        @block.sync
        def _(sp):
            def load(dst, src, **kw):
                sp.dma_start(dst, src, **kw).then_inc(s_ld, 16)

            def load_x(b, s):
                sp.dma_start(xr[:, b * S:(b + 1) * S].rearrange("p (c d) -> p c d", c=TC),
                             x_in[b].rearrange("(c p) d -> p c d", p=P)).then_inc(s, 16)

            load_x(0, s_x0)
            load(cond[:, :], c_in)
            load(wmod_sb[:, :], wmod)
            load(w_raw[:, 0, :], Wv)
            load(w_raw[:, 1, :], Wo)
            sp.wait_ge(s_const, 1)
            for r in range(HD):
                load(tril_rows[r::HD, 0:r + 1],
                     params[:, r * (r + 1) // 2:r * (r + 1) // 2 + r + 1], allow_slow_non_contiguous=(r == 0))
            for n, v in enumerate((ln1_w, ln1_b, ln2_w, ln2_b, bq, bk)):
                load(rows[2 * n:2 * n + 2, :], v)
            load(rows[B1:BV, :], e_b1.rearrange("l e (f p) -> (l e f) p", p=P))
            load(rows[BV:BV + 1, :], bv.unsqueeze(0))
            load(rows[BV + 1:NROW, :], bv2)
            load(bias_row[:, 0, :], bo.partition_broadcast(P))
            for n in range(L):
                load(bias_row[:, 1 + n, :], bo2[n].partition_broadcast(P))
                load(gate_bias[:, n, :], gate_b[n].partition_broadcast(P))
            load(gate_sb[:, :, :], gate_w.rearrange("l d e -> d l e"))
            load(wq_sb[:, :, :], wq.rearrange("l d e -> d l e"))
            load(wk_sb[:, :, :], wk.rearrange("l d e -> d l e"))
            load(wv_sb[:, :, :], wv.rearrange("l d e -> d l e"))
            load(wo_sb[:, :, :], wo.rearrange("l d e -> d l e"))
            load(b2_sb[:, :], e_b2[0])
            for b in range(1, NB):
                load_x(b, s_x)
            sp.dma_start(w1_sb[:, :, :], e_w1[0].rearrange("e d f -> d e f")).then_inc(s_w, 16)
            sp.dma_start(w2_sb[:, :, :, :], e_w2[0].rearrange("e (f p) d -> p e f d", p=P)).then_inc(s_w, 16)

            def stack(ph, b, dst, dram, order, spilled, done):
                sp.wait_ge(spilled, (b + 1) * 16)
                sp.sem_inc(s_own_sp, 1)
                wait(sp, ph.s["scores_k"], (b - 1) * UNITS)
                heads = dram.rearrange("(p a d) r n -> a r d p n", a=2, d=HD)
                for a in range(2):
                    for r, part in enumerate(order):
                        sp.dma_start(dst[a][64 * a + HD * r:64 * a + HD * (r + 1), :, :], heads[a, part]).then_inc(done, 16)

            def spill_q(ph, b):
                sp.wait_ge(ph.s["q_split"], b + 1)
                sp.dma_start(q_dram, q_parts[:, :, :]).then_inc(ph.s["q_spilled"], 16)

            def spill_k(ph, b):
                if ph.own_k:
                    sp.wait_ge(ph.s["k_split"], b + 1)
                    sp.dma_start(k_dram, k_parts[:, :, :]).then_inc(ph.s["k_spilled"], 16)

            def stack_q(ph, b, q):
                stack(ph, b, Qs[q], q_dram, Q_PARTS, ph.s["q_spilled"], ph.s["q_stacked"])

            def stack_k(ph, b, q):
                if ph.own_k:
                    stack(ph, b, [Ks[q]] * 2, k_dram, K_PARTS, ph.s["k_spilled"], ph.s["k_stacked"])
                else:
                    stack(ph, b, [Ks[q]] * 2, q_dram, K_PARTS, ph.s["q_spilled"], ph.s["k_stacked"])

            def shift_rows(ph, b, q, g):
                sp.wait_ge(ph.s["shift_copied"], b * G + g + 1)
                sp.sem_inc(s_own_sp, 1)
                for n in range(HG):
                    sp.dma_start(Qs[q][n % 2][SHIFT_ROW:SHIFT_ROW + 2, 2 * g + n // 2, :], shift[g % 2][n::HG, :]).then_inc(rows_shifted(ph, g), 16)

            def attention(ph):
                n = ph.first_batch
                spill_q(ph, n)
                spill_k(ph, n)
                stack_q(ph, n, 0)
                stack_k(ph, n, 0)

                def body(i, q, prev, cur, nxt):
                    if prev:
                        shift_rows(ph, i - 1, 1 - q, 3)
                    if cur:
                        shift_rows(ph, i, q, 0)
                    if nxt:
                        spill_q(ph, i + 1)
                        spill_k(ph, i + 1)
                    if cur:
                        shift_rows(ph, i, q, 1)
                    if nxt:
                        stack_q(ph, i + 1, 1 - q)
                    if cur:
                        shift_rows(ph, i, q, 2)
                    if nxt:
                        stack_k(ph, i + 1, 1 - q)
                batches(sp, ph, body)

            attention(outer)
            attention(layer[0])
            attention(layer[1])

            sp.wait_ge(seq["picked"], 1)

            def fill_slots(j):
                for slot in range(NSLOT):
                    n = j * NSLOT + slot
                    sp.sem_inc(s_own_sp, 1)
                    e = sp.value_load(seq_idx[0:1, bass.ds(n, 1)], min_val=0, max_val=E - 1)
                    wait(sp, seq["accumulated"], n - NSLOT + 1)
                    sp.wait_ge(seq["picked"], 1)
                    for dst, src in (
                        (w1_slot[slot], e_w1[1, bass.ds(e, 1), :, :].rearrange("o d f -> (o d) f")),
                        (w2_slot[slot], e_w2[1, bass.ds(e, 1), :, :].rearrange("o (f p) d -> p (o f) d", p=P)),
                        (b1_slot[slot][:, :], cols[:, bass.ds(e * FC + (B1 + E * FC), FC)]),
                        (b2_slot[slot], e_b2[1, bass.ds(e, 1), :].rearrange("o d -> (o d)").partition_broadcast(P)),
                    ):
                        sp.dma_start(dst, src).then_inc(seq_loaded[slot], 16)

            fill_slots(0)
            with sp.Fori(1, NB // 2) as j:
                fill_slots(j)

        @block.gpsimd
        def _(pool):
            chain = [0]

            def link(ins):
                chain[0] += 1
                ins.then_inc(s_pool0, 1)
                pool.wait_ge(s_pool0, chain[0])

            link(pool.memset(tril_rows[:, :], 0.0))
            pool.memset(ones8[:, :], 1.0).then_inc(s_const, 1)
            for t in (ident, identb, mask_q, mask_k, head_sel, batch_row):
                link(pool.memset(t[:], 0.0))
            link(pool.memset(blockdiag[:, :], 1.0))

            def select(t, pattern, op, fill, base, mult):
                link(pool.affine_select(out=t, in_=t, compare_op=op, fill=fill, base=base, pattern=pattern,
                                        channel_multiplier=mult))

            select(ident[:, :], [[-1, P]], ALU.not_equal, 1.0, 0, 1)
            select(blockdiag[:, :], [[-HD, H]], ALU.is_ge, 0.0, 0, 1)
            select(blockdiag[:, :], [[HD, H]], ALU.is_ge, 0.0, HD - 1, -1)
            select(batch_row[:, :, :], [[-1, NB], [0, P]], ALU.not_equal, 1.0, 0, 1)
            select(identb[:, :], [[-1, P]], ALU.not_equal, 1.0, 0, 1)
            select(mask_q[:, :], [[-1, P]], ALU.is_ge, NEG, 0, 1)
            select(mask_k[:, :], [[1, P]], ALU.is_ge, NEG, 0, -1)
            select(head_sel[:, 0:32].rearrange("p (j d) -> p j d", j=HG), [[-32, HG], [-1, HD]], ALU.not_equal, 1.0, 0, 1)
            select(head_sel[:, 32:36], [[-32, HG]], ALU.not_equal, 1.0, -HD, 1)
            link(pool.memset(minus_half[:, :], -0.5))
            link(pool.memset(e_const[:, :], E_CONST))
            link(pool.memset(wo_gated[:, :], 0.0))
            pool.memset(rstd2[:, :], 0.0).then_inc(outer.s["tail_done"], 1)
            pool.iota(iota8[:, :], pattern=[[1, E]], base=0, channel_multiplier=0,
                      allow_small_or_imprecise_dtypes=True).then_inc(s_const, 1)
            pool.wait_ge(s_const, 2)
            pool.wait_ge(s_dve0, DVE_SETUP)

            def wait(eng, sem_, value):
                if isinstance(value, int):
                    if value > 0:
                        eng.wait_ge(sem_, value)
                    return
                eng.wait_ge(sem_, value)
                eng.sem_inc(s_own_pool, 1)

            def normalise(dst, src, mv, s_stats, s_chain, done, ve, rs, n):
                wait(pool, s_stats, n + 1)
                pool.tensor_scalar(ve[:, :], mv[:, :, 1], EPS, None, ALU.add).then_inc(s_chain, 1)
                wait(pool, s_chain, n * 3 + 1)
                pool.tensor_tensor(rs[:, :], ve[:, :], minus_half[:, 0:TC], ALU.pow).then_inc(s_chain, 1)
                pool.tensor_tensor(dst, src, mv[:, :, 0:1].to_broadcast([P, TC, P]), ALU.subtract).then_inc(s_chain, 1)
                wait(pool, s_chain, n * 3 + 3)
                pool.tensor_tensor(dst, dst, rs[:, :].unsqueeze(2).to_broadcast([P, TC, P]), ALU.mult).then_inc(done, 1)

            def split(full, parts, s_full, s_high, s_chain, done, b):
                wait(pool, s_full, b + 1)
                wait(pool, s_high, b + 1)
                pool.tensor_tensor(full[:, :], full[:, :], parts[:, 0, :], ALU.subtract).then_inc(s_chain, 1)
                wait(pool, s_chain, b * 2 + 1)
                pool.tensor_scalar(parts[:, 1, :], full[:, :], 1.0, None, ALU.mult).then_inc(s_chain, 1)
                wait(pool, s_chain, b * 2 + 2)
                pool.tensor_tensor(parts[:, 2, :], full[:, :], parts[:, 1, :], ALU.subtract).then_inc(done, 1)

            def attention(ph):
                s = ph.s

                def prep(b):
                    wait(pool, s["xT_ready"], b)
                    normalise(xn[:, :, :], tokens(ph.stream, b - ph.first_batch), mean_var, s["stats_done"], s["rstd_chain"],
                              s["xn_ready"], var_eps, rstd, b)

                def bias(b, q):
                    wait(pool, s["xn_ready"], b + 1)
                    if ph is outer:
                        ga = modB[:, bass.ds(b, 1), 0, :]
                        wait(pool, s["bias_added"], b)
                        pool.tensor_tensor(bias_gated[:, :].unsqueeze(1), bias_row[:, 0, :].unsqueeze(1), ga,
                                           ALU.mult).then_inc(s["bias_gated"], 1)
                        wait(pool, s["bias_gated"], b + 1)
                        row = bias_gated[:, :]
                    else:
                        row = bias_row[:, 1 + ph.n, :]
                    t = tokens(ph.stream, b - ph.first_batch)
                    pool.tensor_tensor(t, t, row.unsqueeze(1).to_broadcast([P, TC, P]), ALU.add).then_inc(s["bias_added"], 1)

                def gate_wo(b):
                    wait(pool, s["out_proj"], b)
                    pool.tensor_tensor(wo_gated[:, :].unsqueeze(1), w_outer[:, 1, :].unsqueeze(1),
                                       modB[:, bass.ds(b, 1), 0, :], ALU.mult).then_inc(s["wo_gated"], 1)

                def tail(b):
                    t = tokens(yr, b)
                    normalise(t, tokens(xr, b), mean_var2, s["stats2_done"], s["tail_chain"], s["tail_normed"], var_eps2, rstd2, b)
                    wait(pool, s["tail_normed"], b + 1)
                    pool.tensor_tensor(t, t, modB[:, bass.ds(b, 1), 2, :].to_broadcast([P, TC, P]), ALU.mult)\
                        .then_inc(s["tail_scaled"], 1)
                    wait(pool, s["tail_scaled"], b + 1)
                    pool.tensor_tensor(t, t, modB[:, bass.ds(b, 1), 1, :].to_broadcast([P, TC, P]), ALU.add)\
                        .then_inc(s["tail_done"], 1)

                def splits(b):
                    split(q_f, q_parts, s["qf_ready"], s["q_copied"], s["q_split_chain"], s["q_split"], b)
                    if ph.own_k:
                        split(k_f, k_parts, s["kf_ready"], s["k_copied"], s["k_split_chain"], s["k_split"], b)

                prep(ph.first_batch)
                splits(ph.first_batch)

                def body(i, q, prev, cur, nxt):
                    if nxt:
                        prep(i + 1)
                    if cur:
                        bias(i, q)
                    if nxt:
                        splits(i + 1)
                    if prev and ph is outer:
                        tail(i - 1)
                    if cur and ph is outer:
                        gate_wo(i)
                batches(pool, ph, body)

            attention(outer)
            wait(pool, outer.s["residual_done"], NB)
            attention(layer[0])
            wait(pool, layer[0].s["residual_done"], NB)

            def tok_prep(b):
                wait(pool, tok["xT_ready"], b)
                normalise(xn[:, :, :], tokens(yr, b), mean_var, tok["stats_done"], tok["rstd_chain"], tok["xn_ready"], var_eps,
                          rstd, b)

            def tok_gap(b):
                wait(pool, tok["gap_ready"], b + 1)
                pool.tensor_tensor(gap_exp[:, :], e_const[:, :], gap[:, :], ALU.pow).then_inc(tok["gap_exp"], 1)

            tok_prep(0)
            tok_gap(0)
            with pool.Fori(0, NB - 1) as i:
                tok_prep(i + 1)
                tok_gap(i + 1)
            wait(pool, tok["accumulated"], NB * E)
            attention(layer[1])
            wait(pool, layer[1].s["residual_done"], 2 * NB)

            wait(pool, seq["aggregated"], NB * TC)
            pool.tensor_scalar(ve_all[:, :], mv_all[:, :, 1], EPS, None, ALU.add).then_inc(seq["rstd_chain"], 1)
            wait(pool, seq["rstd_chain"], 1)
            pool.tensor_tensor(rstd_all[:, :], ve_all[:, :], minus_half[:, :], ALU.pow).then_inc(seq["rstd_ready"], 1)
            wait(pool, seq["gap_ready"], 1)
            pool.tensor_tensor(gap_exp[0:NB, 0:1], e_const[0:NB, 0:1], gap[0:NB, 0:1], ALU.pow).then_inc(seq["gap_exp"], 1)

            def finish(b):
                wait(pool, seq["accumulated"], b * 2 + 2)
                t = tokens(yr, b)
                pool.tensor_tensor(t, t, modB[:, bass.ds(b, 1), 3, :].to_broadcast([P, TC, P]), ALU.mult)\
                    .then_inc(seq["gated"], 1)
                wait(pool, seq["gated"], b + 1)
                o = q_f[:, :].rearrange("p (c d) -> p c d", c=TC)
                wait(pool, seq["stored"], b * 16)
                pool.tensor_tensor(o, t, tokens(xr, b), ALU.add).then_inc(seq["added"], 1)
                wait(pool, seq["added"], b + 1)
                pool.dma_start(out[bass.ds(b, 1), :, :].rearrange("o (c p) d -> p (o c) d", p=P), o).then_inc(seq["stored"], 16)

            finish(0)
            with pool.Fori(1, NB) as b:
                finish(b)
            wait(pool, seq["stored"], NB * 16)

        @block.scalar
        def _(act):
            act.wait_ge(s_ld, ALL_SMALL)
            act.activation(cond_a[:, :], cond[:, :], ACT.Exp, scale=-1.0).then_inc(s_act0, 1)
            for n in range(2):
                act.wait_ge(s_pe0, 3 + n)
                act.activation(w_outer[:, n, :], (MA, MB)[n][:, 0:P], ACT.Copy).then_inc(s_act0, 1)
            for b in range(NB):
                act.wait_ge(s_pe0, 7 + b)
                act.activation(modB[:, b, :, :].rearrange("p a d -> p (a d)"), (MA, MB)[b % 2][:, :], ACT.Copy)\
                    .then_inc(s_act0, 1)

            def attention(ph):
                s = ph.s

                def copy_hT(b):
                    act.wait_ge(s["xT_ready"], b + 1)
                    wait(act, s["v_proj"], b)
                    if ph is outer:
                        sc = mod_cols[:, 1, bass.ds(b, 1)]
                        bi = mod_cols[:, 0, bass.ds(b, 1)]
                    else:
                        sc, bi = ph.hw, ph.hb
                    act.activation(hT[:, :], MB[:, :], ACT.Identity, bias=bi, scale=sc).then_inc(s["hT_ready"], 1)

                def copy_proj(b, bank, full, parts, bias, s_proj, s_full, s_high, s_split, done):
                    act.wait_ge(s_proj, b + 1)
                    wait(act, s_split, b)
                    for sem_, n in done:
                        wait(act, sem_, b * n)
                    kw = {} if bias is None else {"bias": bias}
                    fn = ACT.Copy if bias is None else ACT.Identity
                    act.activation(full[:, :], bank[:, :], fn, **kw).then_inc(s_full, 1)
                    act.activation(parts[:, 0, :], bank[:, :], fn, **kw).then_inc(s_high, 1)

                def copy_q(b):
                    done = [(s["q_stacked"], 16 * STACK_DMAS)] + ([] if ph.own_k else [(s["k_stacked"], 16 * STACK_DMAS)])
                    copy_proj(b, MA, q_f, q_parts, ph.bq, s["q_proj"], s["qf_ready"], s["q_copied"], s["q_split"], done)

                def copy_k(b):
                    copy_proj(b, MB, k_f, k_parts, ph.bk, s["k_proj"], s["kf_ready"], s["k_copied"], s["k_split"],
                              [(s["k_stacked"], 16 * STACK_DMAS)])

                def exp(b, step, n):
                    u = step * HG + n
                    act.wait_ge(s["scores_k"], b * UNITS + u + 1)
                    wait(act, s["av_done"], b * STEPS + step - 1)
                    w = S - second_low(ph, step % TC)
                    act.activation(probs[u % NPB][:, 0:w], ST[u % 3][:, 0:w], ACT.Exp, scale=SCALE).then_inc(s["exp_done"], 1)

                def copy_av(b, g):
                    act.wait_ge(s["av_done"], b * STEPS + TC * (g + 1))
                    wait(act, s["heads_sel"], b * G + g - 1)
                    act.activation(av_sb[g % 2][:, :], AV[:, :], ACT.Copy).then_inc(s["av_copied"], 1)

                def copy_v(b, q):
                    act.wait_ge(s["v_proj"], b + 1)
                    wait(act, s["av_done"], (b - 1) * STEPS)
                    act.activation(Vt[q][:, :, :, 0:HD].rearrange("p c h d -> p (c h) d"),
                                   MA[:, :].rearrange("p (n d) -> p n d", d=HD), ACT.Copy).then_inc(s["v_ready"], 1)

                def copy_yT(b):
                    act.wait_ge(s["yT_done"], b + 1)
                    act.activation(yT[:, :], MB[:, :], ACT.Identity, bias=ph.bv).then_inc(s["yT_copied"], 1)

                copy_hT(ph.first_batch)
                copy_q(ph.first_batch)
                if ph.own_k:
                    copy_k(ph.first_batch)
                copy_v(ph.first_batch, 0)

                def body(i, q, prev, cur, nxt):
                    for k in range(STEPS):
                        b, _, step, on = second_pass(i, q, prev, cur, k, LAG)
                        if on:
                            for n in range(HG):
                                exp(b, step, n)
                        b, _, step, on = second_pass(i, q, prev, cur, k, LAG + 1)
                        if on and step % TC == TC - 1:
                            copy_av(b, step // TC)
                        if k == 2 and nxt:
                            copy_hT(i + 1)
                        if k == 3 and nxt:
                            copy_q(i + 1)
                        if k == 5 and nxt and ph.own_k:
                            copy_k(i + 1)
                        if k == LAG + 1 and nxt:
                            copy_v(i + 1, 1 - q)
                        if k == LAG + 2 and prev:
                            copy_yT(i - 1)
                batches(act, ph, body)

            attention(outer)
            act.wait_ge(outer.s["residual_done"], NB)
            attention(layer[0])
            act.wait_ge(layer[0].s["residual_done"], NB)

            def tok_hT(b):
                act.wait_ge(tok["xT_ready"], b + 1)
                wait(act, tok["hidden"], b * E * FC)
                act.activation(hT[:, :], MA[:, :], ACT.Identity, bias=cols[:, LN2B:LN2B + 1],
                               scale=cols[:, LN2W:LN2W + 1]).then_inc(tok["hT_ready"], 1)

            def tok_experts(b):
                for e in range(E):
                    for f in range(FC):
                        u = e * FC + f
                        act.wait_ge(tok["hidden"], b * (E * FC) + u + 1)
                        if f == 0:
                            wait(act, tok["expert_out"], b * E + e - 1)
                        act.activation(hid[e % 2][:, f, :], HB[f][:, :], ACT.Gelu,
                                       bias=cols[:, B1 + u:B1 + u + 1]).then_inc(tok["gelu_done"], 1)

            tok_hT(0)
            tok_experts(0)
            tok_hT(1)
            with act.Fori(1, NB - 1) as i:
                tok_experts(i)
                tok_hT(i + 1)
            tok_experts(NB - 1)
            act.wait_ge(tok["accumulated"], NB * E)
            attention(layer[1])
            act.wait_ge(layer[1].s["residual_done"], 2 * NB)

            for b in range(NB):
                act.wait_ge(seq["xT_ready"], b + 1)
                act.activation(hT_all[:, b * S:(b + 1) * S], (MA, MB)[b % 2][:, :], ACT.Identity, bias=cols[:, LN2B + 1:LN2B + 2],
                               scale=cols[:, LN2W + 1:LN2W + 2], accum_out=hsum[:, b:b + 1]).then_inc(seq["hT_ready"], 1)

            def seq_experts(j):
                for slot in range(NSLOT):
                    n = j * NSLOT + slot
                    act.wait_ge(seq_loaded[slot], (j + 1) * (16 * SLOT_DMAS))
                    wait(act, seq["expert_out"], n - 1)
                    for f in range(FC):
                        act.wait_ge(seq["hidden"], n * FC + f + 1)
                        act.activation(hid[slot % 2][:, f, :], HB[f][:, :], ACT.Gelu,
                                       bias=b1_slot[slot][:, f:f + 1]).then_inc(seq["gelu_done"], 1)

            seq_experts(0)
            with act.Fori(1, NB // 2) as j:
                seq_experts(j)

        @block.vector
        def _(dve):
            chain = [0]

            def link(ins):
                chain[0] += 1
                ins.then_inc(s_dve0, 1)
                dve.wait_ge(s_dve0, chain[0])

            for t in Vt:
                link(dve.memset(t[:], 0.0))
                link(dve.memset(t[:, :, :, HD:HD + 1], 1.0))
            for n in range(2):
                link(dve.memset(stacks[:, 2 * n:2 * n + 2], 0.0))
                link(dve.memset(Ks[n][:], 1.0))
            dve.wait_ge(s_ld, ALL_SMALL)
            dve.wait_ge(s_act0, 1)
            link(dve.tensor_scalar(cond_b[:, :], cond_a[:, :], 1.0, None, ALU.add))
            link(dve.reciprocal(cond_a[:, :], cond_b[:, :]))
            link(dve.tensor_tensor(cond_b[:, :], cond_a[:, :], cond[:, :], ALU.mult))
            assert chain[0] == DVE_SILU
            dve.wait_ge(s_const, 2)
            link(dve.tensor_tensor(tril_block[:, :].rearrange("p (h j) -> p h j", h=H),
                                   tril_rows[:, :].unsqueeze(1).to_broadcast([P, H, HD]),
                                   blockdiag[:, :].unsqueeze(2).to_broadcast([P, H, HD]), ALU.mult))
            dve.wait_ge(s_pe0, 1)
            link(dve.tensor_copy(condT[:, :], MA[:, 0:NB]))
            assert chain[0] == DVE_CONDT
            dve.wait_ge(s_pe0, 2)
            link(dve.tensor_copy(cols[:, :], MB[:, 0:NROW]))
            dve.wait_ge(s_pe0, 5)
            link(dve.tensor_copy(mod_cols[:, 0, :], MA[:, 256:256 + NB]))
            link(dve.tensor_scalar(mod_cols[:, 1, :], MA[:, 256 + NB:256 + 2 * NB], 1.0, None, ALU.add))
            dve.wait_ge(s_pe0, 6)
            link(dve.tensor_copy(mod_row[:, 1:3, :].rearrange("b a d -> b (a d)"), MB[0:NB, P:3 * P]))
            for n in range(2):
                src = MB[0:NB, 0:P] if n == 0 else MB[0:NB, 3 * P:4 * P]
                link(dve.tensor_scalar(mod_tmp[:, n, :], src, 0.0, 2.0, ALU.is_ge, ALU.mult))
                link(dve.tensor_scalar(mod_tmp2[:, n, :], src, -1.0, None, ALU.mult))
                link(dve.scalar_tensor_tensor(mod_tmp2[:, n, :], src, 0.25, mod_tmp2[:, n, :], ALU.max, ALU.max))
                link(dve.scalar_tensor_tensor(mod_row[:, 3 * n, :], mod_tmp[:, n, :], 1.0, mod_tmp2[:, n, :],
                                              ALU.subtract, ALU.mult))
            link(dve.tensor_scalar(mod_row[:, 2, :], mod_row[:, 2, :], 1.0, None, ALU.add))
            assert chain[0] == DVE_MODROW
            dve.wait_ge(s_act0, 3 + NB)
            link(dve.memset(denom[:, :], 1.0))
            assert chain[0] == DVE_SETUP

            def settled(sem_, value):
                dve.wait_ge(sem_, value)
                dve.sem_inc(s_own_dve, 1)

            def statistics(stream, b, st, mv, s_chain, done, n):
                if not (isinstance(n, int) and n == 0):
                    settled(done, n)
                for c in range(TC):
                    ins = dve.bn_stats(st[:, c, :], tokens(stream, b, c))
                ins.then_inc(s_chain, 1)
                settled(s_chain, n + 1)
                for c in range(TC):
                    ins = dve.bn_aggr(mv[:, c, :], st[:, c, :])
                ins.then_inc(done, 1)

            def attention(ph):
                s = ph.s

                def stats_of(b):
                    if ph is outer:
                        if isinstance(b, int) and b == 0:
                            dve.wait_ge(s_x0, 16)
                        else:
                            dve.wait_ge(s_x, 16 * (NB - 1))
                    wait(dve, s["xn_ready"], b)
                    statistics(ph.stream, b - ph.first_batch, stats, mean_var, s["mv_chain"], s["stats_done"], b)

                def maxima(i, k, n):
                    v = k * HG + n
                    dve.wait_ge(s["scores_q"], i * UNITS + v + 1)
                    if v % 16 == 0:
                        wait(dve, s["shift_split"], i * G + k // TC - G + 1)
                    w = first_width(ph, k % TC)
                    dve.tensor_reduce(row_max[:, v:v + 1], SA[v % 2][:, 0:w], AX_X, ALU.max).then_inc(s["max_done"], 1)

                def split_max(b, g):
                    m = b * G + g
                    dve.wait_ge(s["max_done"], b * UNITS + 16 * (g + 1))
                    wait(dve, s["max_T"], m - 1)
                    t = shift_tok[g % 2]
                    rm = row_max[:, 16 * g:16 * g + 16].rearrange("p (c h) -> p c h", h=HG)
                    dve.tensor_scalar(t[:, :, 0, :], rm, -1.0, None, ALU.mult).then_inc(s["shift_half"], 1)
                    dve.wait_ge(s["shift_half"], m + 1)
                    dve.scalar_tensor_tensor(t[:, :, 1, :], rm, -1.0, t[:, :, 0, :], ALU.mult, ALU.subtract)\
                        .then_inc(s["shift_split"], 1)

                def copy_shift(b, g):
                    dve.wait_ge(s["max_T"], b * G + g + 1)
                    wait(dve, rows_shifted(ph, g), (b * (G // 2) + g // 2) * (16 * SHIFT_DMAS))
                    dve.tensor_copy(shift[g % 2][:, :], MA[:, :].bitcast(BF16)[0:2 * HG, 0:S]).then_inc(s["shift_copied"], 1)

                def normalise_heads(b, g):
                    dve.wait_ge(s["heads_sel"], b * G + g + 1)
                    m = MB[:, 0:TC * 36].rearrange("p (c n) -> p c n", c=TC)
                    dve.reciprocal(recip[:, :, :], m[:, :, 32:36]).then_inc(s["recip_done"], 1)
                    dve.wait_ge(s["recip_done"], b * G + g + 1)
                    if g == 0:
                        wait(dve, s["yT_done"], b)
                    dve.tensor_tensor(y_sb[:, :, 32 * g:32 * g + 32].rearrange("p c (h d) -> p c h d", d=HD),
                                      m[:, :, 0:32].rearrange("p c (h d) -> p c h d", d=HD),
                                      recip[:, :, :].unsqueeze(3).to_broadcast([P, TC, HG, HD]), ALU.mult)\
                        .then_inc(s["y_ready"], 1)

                def residual(b):
                    dve.wait_ge(s["out_proj"], b + 1)
                    dve.wait_ge(s["bias_added"], b + 1)
                    t = tokens(ph.stream, b - ph.first_batch)
                    dve.tensor_tensor(t, MA[:, :].rearrange("p (c d) -> p c d", c=TC), t, ALU.add)\
                        .then_inc(s["residual_done"], 1)

                def tail_stats(b):
                    dve.wait_ge(s["residual_done"], b + 1)
                    wait(dve, s["tail_done"], b + 1)
                    statistics(xr, b, stats2, mean_var2, s["mv2_chain"], s["stats2_done"], b)

                stats_of(ph.first_batch)

                def body(i, q, prev, cur, nxt):
                    for k in range(STEPS):
                        if k == 0 and prev:
                            split_max(i - 1, G - 1)
                        elif k and k % TC == 0 and cur:
                            split_max(i, k // TC - 1)
                        for n in range(HG):
                            if cur:
                                maxima(i, k, n)
                            if n == 1 and k == 0 and prev:
                                copy_shift(i - 1, G - 1)
                            elif n == 1 and k and k % TC == 0 and cur:
                                copy_shift(i, k // TC - 1)
                        if k == 0 and nxt:
                            stats_of(i + 1)
                        if prev and k % TC == SEL and k <= SEL + 2 * TC:
                            normalise_heads(i - 1, k // TC + 1)
                        if k == LAG + 3 and prev:
                            residual(i - 1)
                        if k == LAG + 4 and prev and ph is outer:
                            tail_stats(i - 1)
                        if k == LAG + TC + SEL and cur:
                            normalise_heads(i, 0)
                batches(dve, ph, body)

            attention(outer)
            dve.wait_ge(outer.s["tail_done"], NB + 1)
            attention(layer[0])
            dve.wait_ge(layer[0].s["residual_done"], NB)

            def top_two(lg, t8, ti, tif, gp, s_chain, n0, rows_, nc_):
                dve.sem_inc(s_own_dve, 1)
                for c in range(nc_):
                    dve.max(t8[0:rows_, c, :], lg[0:rows_, c, :]).then_inc(s_chain, 1)
                settled(s_chain, n0 + nc_)
                for c in range(nc_):
                    dve.max_index(ti[0:rows_, c, :], t8[0:rows_, c, :], lg[0:rows_, c, :]).then_inc(s_chain, 1)

            def tok_stats(b):
                wait(dve, tok["xn_ready"], b)
                statistics(yr, b, stats, mean_var, tok["mv_chain"], tok["stats_done"], b)

            GC = 2 * TC + 8

            def tok_gate_a(b):
                dve.wait_ge(tok["logits_ready"], b + 1)
                lg = logits[:, :, :]
                dve.tensor_tensor(lg, MB[:, 0:TC * E].rearrange("p (c e) -> p c e", c=TC),
                                  gate_bias[:, 0, :].unsqueeze(1).to_broadcast([P, TC, E]), ALU.add)\
                    .then_inc(tok["logits_copied"], 1)
                dve.wait_ge(tok["logits_copied"], b + 1)
                top_two(logits, top8, top_idx, top_idxf, gap, tok["gate_chain"], b * GC, P, TC)
                dve.tensor_tensor(gap[:, :], top8[:, :, 1], top8[:, :, 0], ALU.subtract).then_inc(tok["gap_ready"], 1)

            def tok_gate_b(b):
                s_, n = tok["gate_chain"], [b * GC + 2 * TC]

                def step(ins):
                    n[0] = n[0] + 1
                    ins.then_inc(s_, 1)
                    dve.wait_ge(s_, n[0])

                dve.wait_ge(s_, n[0])
                step(dve.tensor_copy(top_idxf[:, :, :], top_idx[:, :, 0:2]))
                dve.wait_ge(tok["gap_exp"], b + 1)
                step(dve.tensor_scalar(denom[:, :], gap_exp[:, :], 1.0, None, ALU.add))
                step(dve.reciprocal(weight[:, :, 0], denom[:, :]))
                step(dve.tensor_tensor(weight[:, :, 1], weight[:, :, 0], gap_exp[:, :], ALU.mult))
                for m in range(2):
                    step(dve.tensor_tensor(pick[m][:, :, :], iota8[:, :].unsqueeze(1).to_broadcast([P, TC, E]),
                                           top_idxf[:, :, m:m + 1].to_broadcast([P, TC, E]), ALU.is_equal))
                    step(dve.tensor_tensor(pick[2 + m][:, :, :], pick[m][:, :, :],
                                           weight[:, :, m:m + 1].to_broadcast([P, TC, E]), ALU.mult))
                wait(dve, tok["combine_T"], b)
                wait(dve, tok["accumulated"], b * E)
                dve.tensor_tensor(combine[:, :, :], pick[2][:, :, :], pick[3][:, :, :], ALU.add)\
                    .then_inc(tok["combine_ready"], 1)
                dve.wait_ge(tok["combine_ready"], b + 1)

            def tok_combineT(b):
                dve.wait_ge(tok["combine_T"], b + 1)
                wait(dve, tok["b2_ready"], b)
                dve.tensor_copy(combineT[:, :], MA[0:E, :]).then_inc(tok["combineT_copied"], 1)

            def tok_b2(b):
                dve.wait_ge(tok["b2_ready"], b + 1)
                dve.wait_ge(tok["accumulated"], b * E + 3)
                t = tokens(yr, b)
                dve.tensor_tensor(t, MB[:, :].rearrange("p (c d) -> p c d", c=TC), t, ALU.add).then_inc(tok["b2_added"], 1)

            def tok_accumulate(b, e):
                dve.wait_ge(tok["expert_out"], b * E + e + 1)
                if e > 0:
                    dve.wait_ge(tok["accumulated"], b * E + e)
                if e == 3:
                    dve.wait_ge(tok["b2_added"], b + 1)
                for c in range(TC):
                    t = tokens(yr, b, c)
                    ins = dve.scalar_tensor_tensor(t, YB[e % 2][:, c * P:(c + 1) * P], combine[:, c, e:e + 1], t,
                                                   ALU.mult, ALU.add)
                ins.then_inc(tok["accumulated"], 1)

            def tok_body(i, prev, nxt):
                if prev:
                    tok_accumulate(i - 1, E - 1)
                tok_gate_b(i)
                tok_combineT(i)
                for e in range(1, E):
                    tok_accumulate(i, e - 1)
                    if e == 1 and nxt:
                        tok_stats(i + 1)
                    if e == 3:
                        tok_b2(i)
                if nxt:
                    tok_gate_a(i + 1)

            tok_stats(0)
            tok_gate_a(0)
            tok_body(0, False, True)
            with dve.Fori(1, NB - 1) as i:
                tok_body(i, True, True)
            tok_body(NB - 1, True, False)
            tok_accumulate(NB - 1, E - 1)
            dve.wait_ge(tok["accumulated"], NB * E)
            attention(layer[1])
            dve.wait_ge(layer[1].s["residual_done"], 2 * NB)

            for n in range(NB * TC):
                dve.bn_stats(stats_all[:, n, :], yr[:, n * P:(n + 1) * P]).then_inc(seq["mv_chain"], 1)
            dve.wait_ge(seq["mv_chain"], NB * TC)
            for n in range(NB * TC):
                dve.bn_aggr(mv_all[:, n, :], stats_all[:, n, :]).then_inc(seq["aggregated"], 1)
            dve.wait_ge(seq["rstd_ready"], 1)
            for b in range(NB):
                wait(dve, seq["xT_ready"], b - 1)
                for c in range(TC):
                    n = b * TC + c
                    ins = dve.tensor_scalar(seq_xn[b % 2][:, c, :], yr[:, n * P:(n + 1) * P], mv_all[:, n, 0:1],
                                            rstd_all[:, n:n + 1], ALU.subtract, ALU.mult)
                ins.then_inc(seq["xn_ready"], 1)
            dve.wait_ge(seq["logits_ready"], 1)
            lg = logits[0:NB, 0:1, :]
            dve.scalar_tensor_tensor(logits[0:NB, 0, :], MA[0:NB, 0:E], 1.0 / S, gate_bias[0:NB, 1, :], ALU.mult, ALU.add)\
                .then_inc(seq["gate_chain"], 1)
            dve.wait_ge(seq["gate_chain"], 1)
            dve.max(top8[0:NB, 0, :], logits[0:NB, 0, :]).then_inc(seq["gate_chain"], 1)
            dve.wait_ge(seq["gate_chain"], 2)
            dve.max_index(top_idx[0:NB, 0, :], top8[0:NB, 0, :], logits[0:NB, 0, :]).then_inc(seq["gate_chain"], 1)
            dve.tensor_tensor(gap[0:NB, 0:1], top8[0:NB, 0, 1:2], top8[0:NB, 0, 0:1], ALU.subtract).then_inc(seq["gap_ready"], 1)
            dve.wait_ge(seq["gate_chain"], 3)
            dve.tensor_copy(top_idxf[0:NB, 0, :], top_idx[0:NB, 0, 0:2]).then_inc(seq["gate_chain"], 1)
            dve.wait_ge(seq["gap_exp"], 1)
            dve.tensor_scalar(denom[0:NB, 0:1], gap_exp[0:NB, 0:1], 1.0, None, ALU.add).then_inc(seq["gate_chain"], 1)
            dve.wait_ge(seq["gate_chain"], 5)
            dve.reciprocal(weight[0:NB, 0, 0:1], denom[0:NB, 0:1]).then_inc(seq["gate_chain"], 1)
            dve.wait_ge(seq["gate_chain"], 6)
            dve.tensor_tensor(weight[0:NB, 0, 1:2], weight[0:NB, 0, 0:1], gap_exp[0:NB, 0:1], ALU.mult)\
                .then_inc(seq["gate_chain"], 1)
            dve.wait_ge(seq["gate_chain"], 7)
            for m, src in enumerate((weight, top_idxf)):
                dve.tensor_tensor(seq_both[:, m, :, :], src[0:NB, 0, :].unsqueeze(1).to_broadcast([NB, NB, 2]),
                                  ident[0:NB, 0:NB].unsqueeze(2).to_broadcast([NB, NB, 2]), ALU.mult).then_inc(seq["both_ready"], 1)
            dve.wait_ge(seq["both_B"], 1)
            dve.tensor_copy(seq_idx[0:1, :], MB[0:1, 2 * NB:4 * NB]).then_inc(seq["picked"], 1)
            dve.tensor_copy(seqB[:, :], MB[:, 0:2 * NB]).then_inc(seq["gate_chain"], 1)
            dve.wait_ge(seq["gate_chain"], 8)

            def seq_apply(j):
                for slot in range(NSLOT):
                    n = j * NSLOT + slot
                    b = j * 2 + slot // 2
                    w = seqB[:, bass.ds(n, 1)]
                    dve.wait_ge(seq_loaded[slot], (j + 1) * (16 * SLOT_DMAS))
                    wait(dve, seq["accumulated"], n)
                    for c in range(TC):
                        t = tokens(yr, b, c)
                        ins = dve.scalar_tensor_tensor(t, b2_slot[slot][:, :], w, t, ALU.mult, ALU.add)
                    ins.then_inc(seq["b2_added"], 1)
                    dve.wait_ge(seq["b2_added"], n + 1)
                    dve.wait_ge(seq["expert_out"], n + 1)
                    for c in range(TC):
                        t = tokens(yr, b, c)
                        ins = dve.scalar_tensor_tensor(t, YB[slot % 2][:, c * P:(c + 1) * P], w, t, ALU.mult, ALU.add)
                    ins.then_inc(seq["accumulated"], 1)

            seq_apply(0)
            with dve.Fori(1, NB // 2) as j:
                seq_apply(j)

        @block.tensor
        def _(pe):
            pe.wait_ge(s_ld, ALL_SMALL)
            pe.wait_ge(s_const, 2)
            pe.wait_ge(s_dve0, DVE_SILU)
            pe.transpose(MA[:, 0:NB], cond_b[:, :], ident[0:NB, 0:NB]).then_inc(s_pe0, 1)
            pe.transpose(MB[:, 0:NROW], rows[:, :], ident[0:NROW, 0:NROW]).then_inc(s_pe0, 1)
            pe.wait_ge(s_dve0, DVE_CONDT)
            pe.transpose(MA[:, 0:P], w_raw[:, 0, :], ident[:, :]).then_inc(s_pe0, 1)
            pe.wait_ge(s_dve0, DVE_CONDT + 1)
            pe.transpose(MB[:, 0:P], w_raw[:, 1, :], ident[:, :]).then_inc(s_pe0, 1)
            pe.wait_ge(s_act0, 2)
            for m in range(2):
                ins = pe.matmul(MA[:, 256 + m * NB:256 + (m + 1) * NB], wmod_sb[:, m * P:(m + 1) * P], condT[:, :],
                                start=True, stop=True)
            ins.then_inc(s_pe0, 1)
            pe.wait_ge(s_act0, 3)
            pe.matmul(MB[0:NB, :], condT[:, :], wmod_sb[:, 2 * P:6 * P], start=True, stop=True).then_inc(s_pe0, 1)
            pe.wait_ge(s_dve0, DVE_MODROW)
            for b in range(NB):
                if b >= 2:
                    pe.wait_ge(s_act0, 3 + b - 1)
                pe.matmul((MA, MB)[b % 2][:, :], batch_row[:, b, :], mod_row[:, :, :].rearrange("b a d -> b (a d)"),
                          start=True, stop=True).then_inc(s_pe0, 1)
            pe.wait_ge(s_dve0, DVE_SETUP)

            def transposed(bank, src, chunks=TC, rows_=P):
                for c in range(chunks):
                    ins = pe.transpose(bank[0:rows_, c * P:(c + 1) * P], src[:, c, :], ident[:, :])
                return ins

            def attention(ph):
                s = ph.s
                freed = {}

                def take(bank):
                    wait(pe, *freed[bank])

                def max_T(b, g):
                    take("A")
                    pe.wait_ge(s["shift_split"], b * G + g + 1)
                    for c in range(TC):
                        ins = pe.transpose(MA[:, :].bitcast(BF16)[0:2 * HG, c * P:(c + 1) * P],
                                           shift_tok[g % 2][:, c, :, :].rearrange("p a h -> p (a h)"), identb[:, :])
                    ins.then_inc(s["max_T"], 1)
                    freed["A"] = (s["shift_copied"], b * G + g + 1)

                def normed_T(b):
                    take("B")
                    pe.wait_ge(s["xn_ready"], b + 1)
                    transposed(MB, xn).then_inc(s["xT_ready"], 1)
                    freed["B"] = (s["hT_ready"], b + 1)

                def project_q(b):
                    take("A")
                    pe.wait_ge(s["hT_ready"], b + 1)
                    pe.matmul(MA[:, :], ph.wq, hT[:, :], start=True, stop=True).then_inc(s["q_proj"], 1)
                    freed["A"] = (s["q_copied"], b + 1)

                def project_k(b):
                    take("B")
                    pe.wait_ge(s["hT_ready"], b + 1)
                    pe.matmul(MB[:, :], ph.wk, hT[:, :], start=True, stop=True).then_inc(s["k_proj"], 1)
                    freed["B"] = (s["k_copied"], b + 1)

                def project_v(b):
                    take("A")
                    pe.wait_ge(s["hT_ready"], b + 1)
                    for c in range(TC):
                        ins = pe.matmul(MA[:, c * P:(c + 1) * P], hT[:, c * P:(c + 1) * P], ph.wv, start=True, stop=True)
                    ins.then_inc(s["v_proj"], 1)
                    freed["A"] = (s["v_ready"], b + 1)

                def select_heads(b, g):
                    take("B")
                    pe.wait_ge(s["av_copied"], b * G + g + 1)
                    for c in range(TC):
                        ins = pe.matmul(MB[:, c * 36:(c + 1) * 36], av_sb[g % 2][:, c * P:(c + 1) * P], head_sel[:, :],
                                        start=True, stop=True)
                    ins.then_inc(s["heads_sel"], 1)
                    freed["B"] = (s["y_ready"], b * G + g + 1)

                def heads_T(b):
                    take("B")
                    pe.wait_ge(s["y_ready"], b * G + G)
                    transposed(MB, y_sb).then_inc(s["yT_done"], 1)
                    freed["B"] = (s["yT_copied"], b + 1)

                def project_out(b, q):
                    take("A")
                    pe.wait_ge(s["yT_copied"], b + 1)
                    if ph is outer:
                        pe.wait_ge(s["wo_gated"], b + 1)
                        w = wo_gated[:, :]
                    else:
                        w = wo_sb[:, ph.n, :]
                    for c in range(TC):
                        ins = pe.matmul(MA[:, c * P:(c + 1) * P], yT[:, c * P:(c + 1) * P], w, start=True, stop=True)
                    ins.then_inc(s["out_proj"], 1)
                    freed["A"] = (s["residual_done"], b + 1)

                def first(i, q, k, n):
                    g, c = k // TC, k % TC
                    v, h = k * HG + n, g * HG + n
                    w = first_width(ph, c)
                    if v == 0:
                        pe.wait_ge(s["q_stacked"], (i + 1) * (16 * STACK_DMAS))
                        pe.wait_ge(s["k_stacked"], (i + 1) * (16 * STACK_DMAS))
                    wait(pe, s["max_done"], i * UNITS + v - 1)
                    ins = pe.matmul(SA[v % 2][:, 0:w], Qs[q][h % 2][0:SHIFT_ROW, h // 2, c * P:(c + 1) * P],
                                    Ks[q][0:SHIFT_ROW, h // 2, 0:w], start=True, stop=not ph.causal)
                    if ph.causal:
                        ins = pe.matmul(SA[v % 2][:, w - P:w], identb[:, :], mask_q[:, :], start=False, stop=True)
                    ins.then_inc(s["scores_q"], 1)

                def second(b, q, step, n):
                    g, c = step // TC, step % TC
                    u, h = step * HG + n, g * HG + n
                    lo = second_low(ph, c)
                    if c == 0 and n == 0:
                        pe.wait_ge(rows_shifted(ph, g), (b * (G // 2) + g // 2 + 1) * (16 * SHIFT_DMAS))
                    wait(pe, s["exp_done"], b * UNITS + u - 2 if u else b * UNITS)
                    ins = pe.matmul(ST[u % 3][:, 0:S - lo], Ks[q][:, h // 2, c * P:(c + 1) * P],
                                    Qs[q][h % 2][:, h // 2, lo:S], start=True, stop=not ph.causal)
                    if ph.causal:
                        ins = pe.matmul(ST[u % 3][:, 0:P], identb[:, :], mask_k[:, :], start=False, stop=True)
                    ins.then_inc(s["scores_k"], 1)

                def weigh(b, q, step):
                    g, c = step // TC, step % TC
                    lo = second_low(ph, c)
                    pe.wait_ge(s["exp_done"], b * UNITS + (step + 1) * HG)
                    if step == 0:
                        pe.wait_ge(s["v_ready"], b + 1)
                    if c == 0:
                        wait(pe, s["av_copied"], b * G + g)
                    for n in range(HG):
                        ins = pe.matmul(AV[32 * n:32 * n + 32, lo:S], Vt[q][:, c, g * HG + n, :],
                                        probs[(step * HG + n) % NPB][:, 0:S - lo], start=(c == 0), stop=(c == TC - 1))
                    ins.then_inc(s["av_done"], 1)

                freed["A"] = freed["B"] = (None, 0)
                normed_T(ph.first_batch)
                project_q(ph.first_batch)
                if ph.own_k:
                    project_k(ph.first_batch)
                project_v(ph.first_batch)

                def body(i, q, prev, cur, nxt):
                    if prev:
                        freed["A"] = (s["shift_copied"], (i - 1) * G + G - 1)
                        freed["B"] = (s["y_ready"], (i - 1) * G + 1)
                    for k in range(STEPS):
                        b2, q2, step2, on2 = second_pass(i, q, prev, cur, k, LAG)
                        b3, q3, step3, on3 = second_pass(i, q, prev, cur, k, LAG + 1)
                        for n in range(HG):
                            if on2:
                                second(b2, q2, step2, n)
                            if cur:
                                first(i, q, k, n)
                            if n == 1:
                                if on3:
                                    weigh(b3, q3, step3)
                                if k == 0 and prev:
                                    max_T(i - 1, G - 1)
                                elif k and k % TC == 0 and cur:
                                    max_T(i, k // TC - 1)
                        if k == 2 and nxt:
                            normed_T(i + 1)
                        if k == 3 and nxt:
                            project_q(i + 1)
                        if prev and k % TC == SEL and k <= SEL + 2 * TC:
                            select_heads(i - 1, k // TC + 1)
                        if k == 5 and nxt and ph.own_k:
                            project_k(i + 1)
                        if k == LAG + 1 and nxt:
                            project_v(i + 1)
                        if k == LAG + 2 and prev:
                            heads_T(i - 1)
                        if k == LAG + 3 and prev:
                            project_out(i - 1, 1 - q)
                        if k == LAG + TC + SEL and cur:
                            select_heads(i, 0)
                batches(pe, ph, body)

            attention(outer)
            pe.wait_ge(outer.s["residual_done"], NB)
            attention(layer[0])
            pe.wait_ge(layer[0].s["residual_done"], NB)
            pe.wait_ge(s_w, 32)

            def tok_normed_T(b):
                pe.wait_ge(tok["xn_ready"], b + 1)
                wait(pe, tok["combineT_copied"], b)
                transposed(MA, xn).then_inc(tok["xT_ready"], 1)

            def tok_logits(b):
                pe.wait_ge(tok["hT_ready"], b + 1)
                wait(pe, tok["b2_added"], b)
                for c in range(TC):
                    ins = pe.matmul(MB[:, c * E:(c + 1) * E], hT[:, c * P:(c + 1) * P], gate_sb[:, 0, :],
                                    start=True, stop=True)
                ins.then_inc(tok["logits_ready"], 1)

            def expert_up(sems, n, w1, x):
                for f in range(FC):
                    wait(pe, sems["gelu_done"], n * FC + f - FC + 1)
                    pe.matmul(HB[f][:, :], w1[:, f * P:(f + 1) * P], x, start=True, stop=True).then_inc(sems["hidden"], 1)

            def expert_down(sems, n, par, w2):
                pe.wait_ge(sems["gelu_done"], n * FC + FC)
                wait(pe, sems["accumulated"], n - 1)
                for c in range(TC):
                    for f in range(FC):
                        ins = pe.matmul(YB[par][:, c * P:(c + 1) * P], hid[par][:, f, c * P:(c + 1) * P], w2[:, f, :],
                                        start=(f == 0), stop=(f == FC - 1))
                ins.then_inc(sems["expert_out"], 1)

            def tok_body(i, prev, nxt):
                for e in range(E):
                    if e == 0:
                        pe.wait_ge(tok["hT_ready"], i + 1)
                    expert_up(tok, i * E + e, w1_sb[:, e, :], hT[:, :])
                    if e == 1:
                        pe.wait_ge(tok["combine_ready"], i + 1)
                        transposed(MA, combine, rows_=E).then_inc(tok["combine_T"], 1)
                    if e == 2:
                        pe.wait_ge(tok["combineT_copied"], i + 1)
                        pe.wait_ge(tok["logits_copied"], i + 1)
                        for c in range(TC):
                            ins = pe.matmul(MB[:, c * P:(c + 1) * P], combineT[:, c * P:(c + 1) * P], b2_sb[:, :],
                                            start=True, stop=True)
                        ins.then_inc(tok["b2_ready"], 1)
                    if e == E - 1 and nxt:
                        tok_normed_T(i + 1)
                    if e:
                        expert_down(tok, i * E + e - 1, (e - 1) % 2, w2_sb[:, e - 1, :, :])
                    elif prev:
                        expert_down(tok, i * E - 1, (E - 1) % 2, w2_sb[:, E - 1, :, :])
                if nxt:
                    tok_logits(i + 1)

            tok_normed_T(0)
            tok_logits(0)
            tok_body(0, False, True)
            with pe.Fori(1, NB - 1) as i:
                tok_body(i, True, True)
            tok_body(NB - 1, True, False)
            expert_down(tok, NB * E - 1, (E - 1) % 2, w2_sb[:, E - 1, :, :])
            pe.wait_ge(tok["accumulated"], NB * E)
            attention(layer[1])
            pe.wait_ge(layer[1].s["residual_done"], 2 * NB)

            for b in range(NB):
                pe.wait_ge(seq["xn_ready"], b + 1)
                wait(pe, seq["hT_ready"], b - 1)
                transposed((MA, MB)[b % 2], seq_xn[b % 2]).then_inc(seq["xT_ready"], 1)
            pe.wait_ge(seq["hT_ready"], NB)
            pe.matmul(MA[0:NB, 0:E], hsum[:, :], gate_sb[:, 1, :], start=True, stop=True).then_inc(seq["logits_ready"], 1)
            pe.wait_ge(seq["both_ready"], 2)
            pe.matmul(MB[:, 0:4 * NB], ones8[:, :], seq_both[:, :, :, :].rearrange("p m b k -> p (m b k)"),
                      start=True, stop=True).then_inc(seq["both_B"], 1)

            def seq_body(j):
                for slot in range(NSLOT):
                    n = j * NSLOT + slot
                    pe.wait_ge(seq_loaded[slot], (j + 1) * (16 * SLOT_DMAS))
                    expert_up(seq, n, w1_slot[slot], hT_all[:, bass.ds((j * 2 + slot // 2) * S, S)])
                    if slot or not isinstance(j, int):
                        expert_down(seq, n - 1, (slot - 1) % 2, w2_slot[(slot - 1) % NSLOT])

            seq_body(0)
            with pe.Fori(1, NB // 2) as j:
                seq_body(j)
            expert_down(seq, 2 * NB - 1, (NSLOT - 1) % 2, w2_slot[NSLOT - 1])


_INS = ['L0_attn_x', 'L0_attn_params', 'L0_attn_Wv', 'L0_attn_bv', 'L0_attn_Wo', 'L0_attn_bo', 'L0_ffn_ln1_w',
        'L0_ffn_ln1_b', 'L0_ffn_ln2_w', 'L0_ffn_ln2_b', 'L0_ffn_wq', 'L0_ffn_wk', 'L0_ffn_wv', 'L0_ffn_wo',
        'L0_ffn_bq', 'L0_ffn_bk', 'L0_ffn_bv', 'L0_ffn_bo', 'L0_ffn_gate_w', 'L0_ffn_gate_b', 'L0_ffn_e_w1',
        'L0_ffn_e_b1', 'L0_ffn_e_w2', 'L0_ffn_e_b2', 'L0_c', 'L0_wmod']
_OUTS = [((8, 512, 128), 'float32')]


def kernel(**inputs):
    import numpy as _np
    import concourse.bacc as _bacc
    from concourse import mybir as _mybir
    from concourse.bass_utils import run_bass_kernel_spmd as _run

    nc = _bacc.Bacc("TRN2", target_bir_lowering=False, num_devices=1)
    arrays, args = {}, []
    for name in _INS:
        a = _np.ascontiguousarray(inputs[name])
        arrays[f"in_{name}_dram"] = a
        args.append(nc.dram_tensor(f"in_{name}_dram", a.shape, _mybir.dt.from_np(a.dtype), kind="ExternalInput").ap())
    for i, (shape, dtype) in enumerate(_OUTS):
        dt = _mybir.dt.from_np(_np.dtype(dtype))
        args.append(nc.dram_tensor(f"out_{i}_dram", shape, dt, kind="ExternalOutput").ap())
    adaln_block(nc, *args)
    r = _run(nc, [arrays], core_ids=[0])
    got = tuple(r.results[0][f"out_{i}_dram"] for i in range(len(_OUTS)))
    return got[0]
```

```python
from contextlib import ExitStack

import concourse.bass as bass
from concourse import mybir

F32 = mybir.dt.float32
BF16 = mybir.dt.bfloat16
U32 = mybir.dt.uint32
I32 = mybir.dt.int32
ALU = mybir.AluOpType
ACT = mybir.ActivationFunctionType
AX_X = mybir.AxisListType.X

P = 128
EPS = 1e-5
NEG = -1e30
E_CONST = 2.718281828459045


class Phase:

    def __init__(self, s, first_batch, causal, own_k, stream, wq, wk, wv, bq, bk, bv, hw, hb, n):
        self.s, self.first_batch, self.causal, self.own_k, self.stream = s, first_batch, causal, own_k, stream
        self.wq, self.wk, self.wv, self.bq, self.bk, self.bv = wq, wk, wv, bq, bk, bv
        self.hw, self.hb, self.n = hw, hb, n


def wait(eng, sem, value):
    if isinstance(value, int) and value <= 0:
        return
    eng.wait_ge(sem, value)


def adaln_block(nc, x_in, params, Wv, bv, Wo, bo, ln1_w, ln1_b, ln2_w, ln2_b, wq, wk, wv, wo, bq, bk, bv2, bo2,
                gate_w, gate_b, e_w1, e_b1, e_w2, e_b2, c_in, wmod, out):
    NB, S, D = x_in.shape
    H = params.shape[0]
    HD = D // H
    TC = S // P
    E = gate_w.shape[2]
    FF = e_w1.shape[3]
    FC = FF // P
    L = gate_w.shape[0]
    HG = 4
    G = H // HG
    PAIRS = H // 2
    STEPS = G * TC
    UNITS = STEPS * HG
    LAG = 8
    SCALE = float(HD) ** -0.5
    assert D == P and HD == 8 and NB == 8 and STEPS == 16 and E == 8 and L == 2

    Q_PARTS = (0, 0, 0, 1, 1, 2)
    K_PARTS = (0, 1, 2, 0, 1, 0)
    NPROD = len(Q_PARTS)
    KROWS = NPROD * HD
    SHIFT_ROW = 64 + KROWS
    Q_RUNS = ((0, 0, 3, True), (3, 1, 2, True), (5, 2, 1, False))
    K_RUNS = ((0, 0, 3, False), (3, 0, 2, False), (5, 0, 1, False))
    SPILL_DMAS = 2 * len(Q_RUNS)
    STACK_DMAS = 2
    SHIFT_DMAS = 4

    with ExitStack() as ctx:
        def sb(name, shape, dt=F32):
            return ctx.enter_context(nc.sbuf_tensor(name, shape, dt))

        def psum(name, shape=(P, 512), dt=F32):
            return ctx.enter_context(nc.psum_tensor(name, list(shape), dt))

        def sem(name):
            return ctx.enter_context(nc.semaphore(name))

        xr = sb("xr", [P, NB * S])
        yr = sb("yr", [P, NB * S])

        ident = sb("ident", [P, P])
        identb = sb("identb", [P, P], BF16)
        mask_q = sb("mask_q", [P, S])
        head_sel = sb("head_sel", [P, 36])
        ones8 = sb("ones8", [E, P])
        blockdiag = sb("blockdiag", [P, H])
        iota8 = sb("iota8", [P, E])
        minus_half = sb("minus_half", [P, NB * TC])
        e_const = sb("e_const", [P, TC])

        NROW = 12 + 2 * E * FC + 1 + L
        rows = sb("rows", [NROW, P])
        cols = sb("cols", [P, NROW])
        cols_regrouped = sb("cols_regrouped", [P, NROW])
        LN1W, LN1B, LN2W, LN2B, BQ, BK, B1, BV = 0, 2, 4, 6, 8, 10, 12, NROW - 1 - L
        bias_row = sb("bias_row", [P, 1 + L, P])
        gate_bias = sb("gate_bias", [P, L, E])
        gate_sb = sb("gate_sb", [P, L, E])
        wq_sb = sb("wq_sb", [P, L, P])
        wk_sb = sb("wk_sb", [P, L, P])
        wv_sb = sb("wv_sb", [P, L, P])
        wo_sb = sb("wo_sb", [P, L, P])
        w_outer = sb("w_outer", [P, 2, P])
        wo_gated = sb("wo_gated", [P, P])
        tril_rows = sb("tril_rows", [P, HD])
        tril_block = sb("tril_block", [P, P])
        w1_sb = sb("w1_sb", [P, E, FF])
        w2_sb = sb("w2_sb", [P, E, FC, P])
        b2_sb = sb("b2_sb", [E, P])
        cond = sb("cond", [NB, P])
        cond_a = sb("cond_a", [NB, P])
        cond_b = sb("cond_b", [NB, P])
        condT = sb("condT", [P, NB])
        mod_cols = sb("mod_cols", [P, 2, NB])
        modB = sb("modB", [P, NB, 4, P])

        stats = sb("stats", [P, TC, 6])
        mean_var = sb("mean_var", [P, TC, 2])
        var_eps = sb("var_eps", [P, TC])
        rstd = sb("rstd", [P, TC])
        xn = sb("xn", [P, TC, P])
        hT = sb("hT", [P, S])
        q_f = sb("q_f", [P, S])
        k_f = sb("k_f", [P, S])
        q_parts = sb("q_parts", [P, 3, S], BF16)
        k_parts = sb("k_parts", [P, 3, S], BF16)
        stacks = sb("stacks", [P, 6, PAIRS, S], BF16)
        Qs = [[stacks[:, 2 * n + a] for a in range(2)] for n in range(2)]
        Ks = [stacks[:, 4 + n] for n in range(2)]
        Vt = [sb(f"Vt{n}", [P, TC, H, 32]) for n in range(2)]
        CAUSAL_AT = [HG * sum(S - P * j for j in range(c)) for c in range(TC + 1)]
        work_all = sb("work", [P, CAUSAL_AT[TC]])
        work = work_all[:, 0:2 * HG * S].rearrange("p (n s) -> p n s", s=S)

        def probs(ph, step):
            c = step % TC
            if ph.causal:
                return work_all[:, CAUSAL_AT[c]:CAUSAL_AT[c + 1]].rearrange("p (h s) -> p h s", h=HG)
            return work[:, step % 2 * HG:(step % 2 + 1) * HG, :]

        flat = work_all
        wmod_sb = flat[:, 0:6 * P]
        w_raw = flat[:, 6 * P:8 * P].rearrange("p (n d) -> p n d", n=2)
        batch_row = flat[0:NB, 8 * P:16 * P].rearrange("p (b d) -> p b d", b=NB)
        mod_row = flat[0:NB, 16 * P:20 * P].rearrange("p (n d) -> p n d", n=4)
        mod_tmp = flat[0:NB, 20 * P:22 * P].rearrange("p (n d) -> p n d", n=2)
        mod_tmp2 = flat[0:NB, 22 * P:24 * P].rearrange("p (n d) -> p n d", n=2)
        wqk_raw = flat[:, 24 * P:28 * P].rearrange("p (n d) -> p n d", n=4)
        tril_raw = flat[:, 28 * P:29 * P]
        rows_regrouped = flat[0:NROW, 29 * P:30 * P]
        row_max = sb("row_max", [P, UNITS])
        shift_tok = [sb(f"shift_tok{n}", [P, TC, 2, HG], BF16) for n in range(2)]
        shift = [sb(f"shift{n}", [2 * HG, S], BF16) for n in range(2)]
        av_sb = [sb(f"av_sb{n}", [P, S]) for n in range(2)]
        recip = sb("recip", [P, TC, HG])
        y_sb = sb("y_sb", [P, TC, P])
        yT = sb("yT", [P, S])
        bias_gated = sb("bias_gated", [P, P])
        stats2 = sb("stats2", [P, TC, 6])
        mean_var2 = sb("mean_var2", [P, TC, 2])
        var_eps2 = sb("var_eps2", [P, TC])
        rstd2 = sb("rstd2", [P, TC])

        hid = [work[:, n * FC:(n + 1) * FC, :] for n in range(2)]
        logits = sb("logits", [P, TC, E])
        top8 = sb("top8", [P, TC, 8])
        top_idx = sb("top_idx", [P, TC, 8], U32)
        top_idxf = sb("top_idxf", [P, TC, 2])
        gap = sb("gap", [P, TC])
        gap_exp = sb("gap_exp", [P, TC])
        denom = sb("denom", [P, TC])
        weight = sb("weight", [P, TC, 2])
        pick = [sb(f"pick{n}", [P, TC, E]) for n in range(4)]
        combine = sb("combine", [P, TC, E])
        combineT = av_sb[0][0:E, :]
        seq_xn = [xn, y_sb]
        stats_all = sb("stats_all", [P, NB * TC, 6])
        mv_all = sb("mv_all", [P, NB * TC, 2])
        ve_all = sb("ve_all", [P, NB * TC])
        rstd_all = sb("rstd_all", [P, NB * TC])
        hsum = sb("hsum", [P, NB])
        seq_both = sb("seq_both", [NB, 2, NB, 2])
        seqB = sb("seqB", [P, 2 * NB])
        seq_idx = sb("seq_idx", [P, 2 * NB], I32)
        NSLOT = 4
        w1_slot = [w1_sb[:, n, :] for n in range(NSLOT)]
        w2_slot = [w2_sb[:, n, :, :] for n in range(NSLOT)]
        b1_slot = [sb(f"b1_slot{n}", [P, FC]) for n in range(NSLOT)]
        b2_slot = [Vt[0][:, 0, 4 * n:4 * n + 4, :].rearrange("p h d -> p (h d)") for n in range(NSLOT)]
        hT_all = stacks[:, 0:2].rearrange("p a b s -> p (a b s)").bitcast(F32)

        q_dram = nc.dram_tensor("q_parts_dram", [2, NPROD, P // 2, S], BF16, kind="Internal").ap()
        k_dram = nc.dram_tensor("k_parts_dram", [2, NPROD, P // 2, S], BF16, kind="Internal").ap()

        banks = [psum(f"bank{n}") for n in range(8)]
        AV = banks[5]
        MA, MB = banks[6], banks[7]
        HB = banks[0:4]
        YB = banks[4:6]

        EARLY_LOADS = 16 * (2 + HD + 9)
        LATE_LOADS = 16 * (1 + 2 * L + 6)
        DVE_SILU = 2 * len(Vt) + 2 + 3
        DVE_CONDT = DVE_SILU + 4
        DVE_MODCOL = DVE_CONDT + 4
        DVE_MODROW = DVE_MODCOL + 10
        DVE_WEIGHTS = DVE_MODROW + 4
        ACT_MODB = 3 + NB
        s_ld = sem("early_loaded")
        s_late = sem("late_loaded")
        s_cond = sem("cond_loaded")
        s_x0 = sem("x_first_loaded")
        s_x = sem("x_loaded")
        s_w = sem("expert_weights_loaded")
        s_pool0 = sem("pool_setup_chain")
        s_const = sem("constants_built")
        s_dve0 = sem("dve_setup_chain")
        s_pe0 = sem("pe_setup")
        s_act0 = sem("act_setup")
        s_own_pool = sem("pool_own")
        s_own_dve = sem("dve_own")
        s_own_sp = sem("sp_own")

        def attention_names(tag, more=()):
            names = ("stats_done", "rstd_chain", "xn_ready", "xT_ready", "hT_ready", "q_proj", "k_proj", "v_proj",
                     "qf_ready", "q_copied", "kf_ready", "k_copied", "q_split_chain", "k_split_chain", "q_split",
                     "k_split", "q_stacked", "k_stacked", "q_spilled", "k_spilled", "v_ready", "scores_q", "max_done", "max_T", "shift_half",
                     "shift_split", "shift_copied", "shift_rows0", "shift_rows1", "scores_k", "exp_done", "masked", "av_done", "av_copied", "heads_sel",
                     "recip_done", "y_ready", "yT_done", "yT_copied", "out_proj", "bias_added", "residual_done",
                     "mv_chain") + more
            return {n: sem(f"{tag}_{n}") for n in names}

        outer = Phase(attention_names("o", ("wo_gated", "bias_gated", "stats2_done", "tail_chain", "tail_normed",
                                                       "tail_scaled", "tail_done", "mv2_chain")), first_batch=0, causal=False, own_k=False, stream=xr,
                      wq=tril_block[:, :], wk=None, wv=w_outer[:, 0, :], bq=None, bk=None, bv=cols[:, BV:BV + 1],
                      hw=None, hb=None, n=None)
        layer_sems = attention_names("l")
        layer = [Phase(layer_sems, first_batch=n * NB, causal=True, own_k=True, stream=yr,
                       wq=wq_sb[:, n, :], wk=wk_sb[:, n, :], wv=wv_sb[:, n, :],
                       bq=cols_regrouped[:, BQ + n:BQ + n + 1], bk=cols_regrouped[:, BK + n:BK + n + 1], bv=cols[:, BV + 1 + n:BV + 2 + n],
                       hw=cols[:, LN1W + n:LN1W + n + 1], hb=cols[:, LN1B + n:LN1B + n + 1], n=n) for n in range(2)]
        tok = {n: sem(f"t_{n}") for n in (
            "stats_done", "mv_chain", "rstd_chain", "xn_ready", "xT_ready", "hT_ready", "logits_ready", "logits_copied",
            "gap_ready", "gap_exp", "gate_chain", "combine_ready", "combine_T", "combineT_copied", "b2_ready",
            "b2_added", "hidden", "gelu_done", "expert_out", "accumulated")}
        seq = {n: sem(f"s_{n}") for n in (
            "mv_chain", "aggregated", "rstd_chain", "rstd_ready", "xn_ready", "xT_ready", "hT_ready", "logits_ready", "gate_chain",
            "gap_ready", "gap_exp", "both_ready", "both_B", "picked", "loaded0", "loaded1", "loaded2", "loaded3", "hidden", "gelu_done", "expert_out",
            "b2_added", "accumulated", "gated", "added", "stored")}

        seq_loaded = [seq["loaded0"], seq["loaded1"], seq["loaded2"], seq["loaded3"]]
        SLOT_DMAS = 4

        def rows_shifted(ph, g):
            return (ph.s["shift_rows0"], ph.s["shift_rows1"])[g % 2]

        def tokens(stream, b, c=None):
            if c is None:
                return stream[:, bass.ds(b * S, S)].rearrange("p (c d) -> p c d", c=TC)
            return stream[:, bass.ds(b * S + c * P, P)]

        def batches(eng, ph, body):
            n = ph.first_batch
            body(n, 0, False, True, True)
            with eng.Fori(0, (NB - 2) // 2) as j:
                body(j * 2 + (n + 1), 1, True, True, True)
                body(j * 2 + (n + 2), 0, True, True, True)
            body(n + NB - 1, 1, True, True, False)
            body(n + NB, 0, True, False, False)

        def second_pass(i, q, prev, cur, k, lag):
            if k < lag:
                return i - 1, 1 - q, k + STEPS - lag, prev
            return i, q, k - lag, cur

        def first_banks(ph):
            return 3

        def bank_q(ph, v):
            return banks[v % first_banks(ph)]

        def bank_k(ph, u):
            return banks[first_banks(ph) + u % (5 - first_banks(ph))]

        def weigh_lag(ph):
            return LAG + 2 if ph.causal else LAG + 1

        def select_step(ph):
            return weigh_lag(ph) - LAG

        def first_chunk(ph, k):
            return TC - 1 - k % TC if ph.causal else k % TC

        def first_width(ph, c):
            return (c + 1) * P if ph.causal else S

        def second_low(ph, c):
            return c * P if ph.causal else 0

        block = ctx.enter_context(nc.Block())

        @block.sync
        def _(sp):
            def load(dst, src, s=s_ld, **kw):
                sp.dma_start(dst, src, **kw).then_inc(s, 16)

            def load_x(b, s):
                sp.dma_start(xr[:, b * S:(b + 1) * S].rearrange("p (c d) -> p c d", c=TC),
                             x_in[b].rearrange("(c p) d -> p c d", p=P)).then_inc(s, 16)

            load_x(0, s_x0)
            load(cond[:, :], c_in, s_cond)
            load(wmod_sb[:, :], wmod, s_cond)
            load(w_raw[:, 0, :], Wv)
            load(w_raw[:, 1, :], Wo)
            sp.wait_ge(s_const, 1)
            for r in range(HD):
                load(tril_rows[r::HD, 0:r + 1],
                     params[:, r * (r + 1) // 2:r * (r + 1) // 2 + r + 1], allow_slow_non_contiguous=(r == 0))
            for n, v in enumerate((ln1_w, ln1_b, ln2_w, ln2_b, bq, bk)):
                load(rows[2 * n:2 * n + 2, :], v)
            load(rows[B1:BV, :], e_b1.rearrange("l e (f p) -> (l e f) p", p=P))
            load(rows[BV:BV + 1, :], bv.unsqueeze(0))
            load(rows[BV + 1:NROW, :], bv2)
            load_x(1, s_x)
            load(bias_row[:, 0, :], bo.partition_broadcast(P), s_late)
            for n in range(L):
                load(bias_row[:, 1 + n, :], bo2[n].partition_broadcast(P), s_late)
                load(gate_bias[:, n, :], gate_b[n].partition_broadcast(P), s_late)
            load(gate_sb[:, :, :], gate_w.rearrange("l d e -> d l e"), s_late)
            load(wqk_raw[:, 0:L, :], wq.rearrange("l d e -> d l e"), s_late)
            load(wqk_raw[:, L:2 * L, :], wk.rearrange("l d e -> d l e"), s_late)
            load(wv_sb[:, :, :], wv.rearrange("l d e -> d l e"), s_late)
            load(wo_sb[:, :, :], wo.rearrange("l d e -> d l e"), s_late)
            load(b2_sb[:, :], e_b2[0], s_late)
            for b in range(2, NB):
                load_x(b, s_x)
            sp.dma_start(w1_sb[:, :, :], e_w1[0].rearrange("e d f -> d e f")).then_inc(s_w, 16)
            sp.dma_start(w2_sb[:, :, :, :], e_w2[0].rearrange("e (f p) d -> p e f d", p=P)).then_inc(s_w, 16)

            def spill(ph, b, parts, dram, runs, split, spilled):
                sp.wait_ge(split, b + 1)
                sp.sem_inc(s_own_sp, 1)
                for a in range(2):
                    half = slice(64 * a, 64 * (a + 1))
                    for place, part, n, same in runs:
                        if same:
                            src = parts[half, part:part + 1, :].to_broadcast([64, n, S])
                        else:
                            src = parts[half, part:part + n, :]
                        sp.dma_start(dram[a, place:place + n].rearrange("r c n -> c r n"), src).then_inc(spilled, 16)

            def stack(ph, b, dst, dram, spilled, done):
                sp.wait_ge(spilled, (b + 1) * (16 * SPILL_DMAS))
                sp.sem_inc(s_own_sp, 1)
                wait(sp, ph.s["scores_k"], (b - 1) * UNITS)
                for a in range(2):
                    sp.dma_start(dst[a][64 * a:64 * a + KROWS, :, :],
                                 dram[a].rearrange("r (d p) n -> (r d) p n", d=HD)).then_inc(done, 16)

            def spill_q(ph, b):
                spill(ph, b, q_parts, q_dram, Q_RUNS, ph.s["q_split"], ph.s["q_spilled"])

            def spill_k(ph, b):
                if ph.own_k:
                    spill(ph, b, k_parts, k_dram, K_RUNS, ph.s["k_split"], ph.s["k_spilled"])
                else:
                    spill(ph, b, q_parts, k_dram, K_RUNS, ph.s["q_split"], ph.s["k_spilled"])

            def stack_q(ph, b, q):
                stack(ph, b, Qs[q], q_dram, ph.s["q_spilled"], ph.s["q_stacked"])

            def stack_k(ph, b, q):
                stack(ph, b, [Ks[q]] * 2, k_dram, ph.s["k_spilled"], ph.s["k_stacked"])

            def shift_rows(ph, b, q, g):
                sp.wait_ge(ph.s["shift_copied"], b * G + g + 1)
                sp.sem_inc(s_own_sp, 1)
                for n in range(HG):
                    sp.dma_start(Qs[q][n % 2][SHIFT_ROW:SHIFT_ROW + 2, 2 * g + n // 2, :], shift[g % 2][n::HG, :]).then_inc(rows_shifted(ph, g), 16)

            def attention(ph):
                n = ph.first_batch
                spill_q(ph, n)
                spill_k(ph, n)
                stack_q(ph, n, 0)
                stack_k(ph, n, 0)

                def body(i, q, prev, cur, nxt):
                    if prev:
                        shift_rows(ph, i - 1, 1 - q, 3)
                    if cur:
                        shift_rows(ph, i, q, 0)
                    if nxt:
                        spill_q(ph, i + 1)
                    if cur:
                        shift_rows(ph, i, q, 1)
                    if nxt:
                        spill_k(ph, i + 1)
                    if nxt:
                        stack_q(ph, i + 1, 1 - q)
                    if cur:
                        shift_rows(ph, i, q, 2)
                    if nxt:
                        stack_k(ph, i + 1, 1 - q)
                batches(sp, ph, body)

            attention(outer)
            attention(layer[0])
            attention(layer[1])

            sp.wait_ge(seq["picked"], 1)

            def fill_slots(j):
                for slot in range(NSLOT):
                    n = j * NSLOT + slot
                    sp.sem_inc(s_own_sp, 1)
                    e = sp.value_load(seq_idx[0:1, bass.ds(n, 1)], min_val=0, max_val=E - 1)
                    wait(sp, seq["accumulated"], n - NSLOT + 1)
                    sp.wait_ge(seq["picked"], 1)
                    for dst, src in (
                        (w1_slot[slot], e_w1[1, bass.ds(e, 1), :, :].rearrange("o d f -> (o d) f")),
                        (w2_slot[slot], e_w2[1, bass.ds(e, 1), :, :].rearrange("o (f p) d -> p (o f) d", p=P)),
                        (b1_slot[slot][:, :], cols[:, bass.ds(e * FC + (B1 + E * FC), FC)]),
                        (b2_slot[slot], e_b2[1, bass.ds(e, 1), :].rearrange("o d -> (o d)").partition_broadcast(P)),
                    ):
                        sp.dma_start(dst, src).then_inc(seq_loaded[slot], 16)

            fill_slots(0)
            with sp.Fori(1, NB // 2) as j:
                fill_slots(j)

        @block.gpsimd
        def _(pool):
            chain = [0]

            def link(ins):
                chain[0] += 1
                ins.then_inc(s_pool0, 1)
                pool.wait_ge(s_pool0, chain[0])

            link(pool.memset(tril_rows[:, :], 0.0))
            pool.memset(ones8[:, :], 1.0).then_inc(s_const, 1)
            for t in (ident, identb, mask_q, head_sel, batch_row):
                link(pool.memset(t[:], 0.0))
            link(pool.memset(blockdiag[:, :], 1.0))

            def select(t, pattern, op, fill, base, mult):
                link(pool.affine_select(out=t, in_=t, compare_op=op, fill=fill, base=base, pattern=pattern,
                                        channel_multiplier=mult))

            select(ident[:, :], [[-1, P]], ALU.not_equal, 1.0, 0, 1)
            select(blockdiag[:, :], [[-HD, H]], ALU.is_ge, 0.0, 0, 1)
            select(blockdiag[:, :], [[HD, H]], ALU.is_ge, 0.0, HD - 1, -1)
            select(batch_row[:, :, :], [[-1, NB], [0, P]], ALU.not_equal, 1.0, 0, 1)
            select(identb[:, :], [[-1, P]], ALU.not_equal, 1.0, 0, 1)
            select(mask_q[:, S - P:S], [[-1, P]], ALU.is_ge, NEG, 0, 1)
            select(head_sel[:, 0:32].rearrange("p (j d) -> p j d", j=HG), [[-32, HG], [-1, HD]], ALU.not_equal, 1.0, 0, 1)
            select(head_sel[:, 32:36], [[-32, HG]], ALU.not_equal, 1.0, -HD, 1)
            link(pool.memset(minus_half[:, :], -0.5))
            link(pool.memset(e_const[:, :], E_CONST))
            link(pool.memset(wo_gated[:, :], 0.0))
            pool.memset(rstd2[:, :], 0.0).then_inc(outer.s["tail_done"], 1)
            pool.iota(iota8[:, :], pattern=[[1, E]], base=0, channel_multiplier=0,
                      allow_small_or_imprecise_dtypes=True).then_inc(s_const, 1)
            pool.wait_ge(s_const, 2)

            def wait(eng, sem_, value):
                if isinstance(value, int):
                    if value > 0:
                        eng.wait_ge(sem_, value)
                    return
                eng.wait_ge(sem_, value)
                eng.sem_inc(s_own_pool, 1)

            def normalise(piece, dst, src, mv, s_stats, s_chain, done, ve, rs, n):
                if piece == 0:
                    wait(pool, s_stats, n + 1)
                    pool.tensor_scalar(ve[:, :], mv[:, :, 1], EPS, None, ALU.add).then_inc(s_chain, 1)
                    wait(pool, s_chain, n * 3 + 1)
                    pool.tensor_tensor(rs[:, :], ve[:, :], minus_half[:, 0:TC], ALU.pow).then_inc(s_chain, 1)
                elif piece == 1:
                    pool.tensor_tensor(dst, src, mv[:, :, 0:1].to_broadcast([P, TC, P]), ALU.subtract).then_inc(s_chain, 1)
                else:
                    wait(pool, s_chain, n * 3 + 3)
                    pool.tensor_tensor(dst, dst, rs[:, :].unsqueeze(2).to_broadcast([P, TC, P]), ALU.mult).then_inc(done, 1)

            def split(piece, full, parts, s_full, s_high, s_chain, done, b):
                if piece == 0:
                    wait(pool, s_full, b + 1)
                    wait(pool, s_high, b + 1)
                    pool.tensor_tensor(full[:, :], full[:, :], parts[:, 0, :], ALU.subtract).then_inc(s_chain, 1)
                elif piece == 1:
                    wait(pool, s_chain, b * 2 + 1)
                    pool.tensor_scalar(parts[:, 1, :], full[:, :], 1.0, None, ALU.mult).then_inc(s_chain, 1)
                else:
                    wait(pool, s_chain, b * 2 + 2)
                    pool.tensor_tensor(parts[:, 2, :], full[:, :], parts[:, 1, :], ALU.subtract).then_inc(done, 1)

            def attention(ph):
                s = ph.s

                def prep(b, piece):
                    if piece == 1:
                        wait(pool, s["xT_ready"], b)
                    normalise(piece, xn[:, :, :], tokens(ph.stream, b - ph.first_batch), mean_var, s["stats_done"],
                              s["rstd_chain"], s["xn_ready"], var_eps, rstd, b)

                def bias(b, q):
                    wait(pool, s["xn_ready"], b + 1)
                    if ph is outer:
                        ga = modB[:, bass.ds(b, 1), 0, :]
                        wait(pool, s["bias_added"], b)
                        pool.tensor_tensor(bias_gated[:, :].unsqueeze(1), bias_row[:, 0, :].unsqueeze(1), ga,
                                           ALU.mult).then_inc(s["bias_gated"], 1)
                        wait(pool, s["bias_gated"], b + 1)
                        row = bias_gated[:, :]
                    else:
                        row = bias_row[:, 1 + ph.n, :]
                    t = tokens(ph.stream, b - ph.first_batch)
                    pool.tensor_tensor(t, t, row.unsqueeze(1).to_broadcast([P, TC, P]), ALU.add).then_inc(s["bias_added"], 1)

                def gate_wo(b):
                    wait(pool, s["out_proj"], b)
                    pool.tensor_tensor(wo_gated[:, :].unsqueeze(1), w_outer[:, 1, :].unsqueeze(1),
                                       modB[:, bass.ds(b, 1), 0, :], ALU.mult).then_inc(s["wo_gated"], 1)

                def tail(b):
                    t = tokens(yr, b)
                    for piece in range(3):
                        normalise(piece, t, tokens(xr, b), mean_var2, s["stats2_done"], s["tail_chain"],
                                  s["tail_normed"], var_eps2, rstd2, b)
                    wait(pool, s["tail_normed"], b + 1)
                    pool.tensor_tensor(t, t, modB[:, bass.ds(b, 1), 2, :].to_broadcast([P, TC, P]), ALU.mult)\
                        .then_inc(s["tail_scaled"], 1)
                    wait(pool, s["tail_scaled"], b + 1)
                    pool.tensor_tensor(t, t, modB[:, bass.ds(b, 1), 1, :].to_broadcast([P, TC, P]), ALU.add)\
                        .then_inc(s["tail_done"], 1)

                def split_q(b, piece):
                    split(piece, q_f, q_parts, s["qf_ready"], s["q_copied"], s["q_split_chain"], s["q_split"], b)

                def split_k(b, piece):
                    split(piece, k_f, k_parts, s["kf_ready"], s["k_copied"], s["k_split_chain"], s["k_split"], b)

                def mask(b, step):
                    wait(pool, s["exp_done"], b * UNITS + (step + 1) * HG)
                    block_ = probs(ph, step)[:, :, 0:P]
                    pool.affine_select(out=block_, in_=block_, compare_op=ALU.is_ge, fill=0.0, base=0,
                                       pattern=[[0, HG], [1, P]], channel_multiplier=-1).then_inc(s["masked"], 1)

                for piece in range(3):
                    prep(ph.first_batch, piece)
                for piece in range(3):
                    split_q(ph.first_batch, piece)
                for piece in range(3 if ph.own_k else 0):
                    split_k(ph.first_batch, piece)
                if ph is outer:
                    link(pool.memset(stacks[:, 2:4], 0.0))
                    link(pool.memset(Ks[1][:], 1.0))
                    pool.wait_ge(s_act0, ACT_MODB)
                    pool.wait_ge(s_late, LATE_LOADS)

                def body(i, q, prev, cur, nxt):
                    for k in range(STEPS):
                        b, _, step, on = second_pass(i, q, prev, cur, k, LAG)
                        if on and ph.causal:
                            mask(b, step)
                        if k < 3 and nxt:
                            prep(i + 1, k)
                        if k == 3 and cur:
                            bias(i, q)
                        if 5 <= k < 8 and nxt:
                            split_q(i + 1, k - 5)
                        if 8 <= k < 11 and nxt and ph.own_k:
                            split_k(i + 1, k - 8)
                    if prev and ph is outer:
                        tail(i - 1)
                    if cur and ph is outer:
                        gate_wo(i)
                batches(pool, ph, body)

            attention(outer)
            wait(pool, outer.s["residual_done"], NB)
            attention(layer[0])
            wait(pool, layer[0].s["residual_done"], NB)

            def tok_prep(b):
                wait(pool, tok["xT_ready"], b)
                for piece in range(3):
                    normalise(piece, xn[:, :, :], tokens(yr, b), mean_var, tok["stats_done"], tok["rstd_chain"],
                              tok["xn_ready"], var_eps, rstd, b)

            def tok_gap(b):
                wait(pool, tok["gap_ready"], b + 1)
                pool.tensor_tensor(gap_exp[:, :], e_const[:, :], gap[:, :], ALU.pow).then_inc(tok["gap_exp"], 1)

            tok_prep(0)
            tok_gap(0)
            with pool.Fori(0, NB - 1) as i:
                tok_prep(i + 1)
                tok_gap(i + 1)
            wait(pool, tok["accumulated"], NB * E)
            attention(layer[1])
            wait(pool, layer[1].s["residual_done"], 2 * NB)

            wait(pool, seq["aggregated"], NB * TC)
            pool.tensor_scalar(ve_all[:, :], mv_all[:, :, 1], EPS, None, ALU.add).then_inc(seq["rstd_chain"], 1)
            wait(pool, seq["rstd_chain"], 1)
            pool.tensor_tensor(rstd_all[:, :], ve_all[:, :], minus_half[:, :], ALU.pow).then_inc(seq["rstd_ready"], 1)
            wait(pool, seq["gap_ready"], 1)
            pool.tensor_tensor(gap_exp[0:NB, 0:1], e_const[0:NB, 0:1], gap[0:NB, 0:1], ALU.pow).then_inc(seq["gap_exp"], 1)

            def finish(b):
                wait(pool, seq["accumulated"], b * 2 + 2)
                t = tokens(yr, b)
                pool.tensor_tensor(t, t, modB[:, bass.ds(b, 1), 3, :].to_broadcast([P, TC, P]), ALU.mult)\
                    .then_inc(seq["gated"], 1)
                wait(pool, seq["gated"], b + 1)
                o = q_f[:, :].rearrange("p (c d) -> p c d", c=TC)
                wait(pool, seq["stored"], b * 16)
                pool.tensor_tensor(o, t, tokens(xr, b), ALU.add).then_inc(seq["added"], 1)
                wait(pool, seq["added"], b + 1)
                pool.dma_start(out[bass.ds(b, 1), :, :].rearrange("o (c p) d -> p (o c) d", p=P), o).then_inc(seq["stored"], 16)

            finish(0)
            with pool.Fori(1, NB) as b:
                finish(b)
            wait(pool, seq["stored"], NB * 16)

        @block.scalar
        def _(act):
            act.wait_ge(s_cond, 32)
            act.activation(cond_a[:, :], cond[:, :], ACT.Exp, scale=-1.0).then_inc(s_act0, 1)
            for n in range(2):
                act.wait_ge(s_pe0, 3 + 2 * n)
                act.activation(w_outer[:, n, :], (MA, MB)[n][:, 0:P], ACT.Copy).then_inc(s_act0, 1)
            def attention(ph):
                s = ph.s

                def copy_hT(b):
                    act.wait_ge(s["xT_ready"], b + 1)
                    wait(act, s["v_proj"], b)
                    if ph is outer:
                        sc = mod_cols[:, 1, bass.ds(b, 1)]
                        bi = mod_cols[:, 0, bass.ds(b, 1)]
                    else:
                        sc, bi = ph.hw, ph.hb
                    act.activation(hT[:, :], MB[:, :], ACT.Identity, bias=bi, scale=sc).then_inc(s["hT_ready"], 1)

                def copy_proj(b, bank, full, parts, bias, s_proj, s_full, s_high, s_split, done):
                    act.wait_ge(s_proj, b + 1)
                    wait(act, s_split, b)
                    for sem_, n in done:
                        wait(act, sem_, b * n)
                    kw = {} if bias is None else {"bias": bias}
                    fn = ACT.Copy if bias is None else ACT.Identity
                    act.activation(full[:, :], bank[:, :], fn, **kw).then_inc(s_full, 1)
                    act.activation(parts[:, 0, :], bank[:, :], fn, **kw).then_inc(s_high, 1)

                def copy_q(b):
                    done = [(s["q_stacked"], 16 * STACK_DMAS)] + ([] if ph.own_k else [(s["k_stacked"], 16 * STACK_DMAS)])
                    copy_proj(b, MA, q_f, q_parts, ph.bq, s["q_proj"], s["qf_ready"], s["q_copied"], s["q_split"], done)

                def copy_k(b):
                    copy_proj(b, MB, k_f, k_parts, ph.bk, s["k_proj"], s["kf_ready"], s["k_copied"], s["k_split"],
                              [(s["k_stacked"], 16 * STACK_DMAS)])

                def exp(b, step, n):
                    u = step * HG + n
                    act.wait_ge(s["scores_k"], b * UNITS + u + 1)
                    wait(act, s["av_done"], b * STEPS + step + 1 - (TC if ph.causal else 2))
                    w = S - second_low(ph, step % TC)
                    act.activation(probs(ph, step)[:, n, :], bank_k(ph, u)[:, 0:w], ACT.Exp, scale=SCALE).then_inc(s["exp_done"], 1)

                def copy_av(b, g):
                    act.wait_ge(s["av_done"], b * STEPS + TC * (g + 1))
                    wait(act, s["heads_sel"], b * G + g - 1)
                    act.activation(av_sb[g % 2][:, :], AV[:, :], ACT.Copy).then_inc(s["av_copied"], 1)

                def copy_v(b, q):
                    act.wait_ge(s["v_proj"], b + 1)
                    wait(act, s["av_done"], (b - 1) * STEPS)
                    act.activation(Vt[q][:, :, :, 0:HD].rearrange("p c h d -> p (c h) d"),
                                   MA[:, :].rearrange("p (n d) -> p n d", d=HD), ACT.Copy).then_inc(s["v_ready"], 1)

                def copy_yT(b):
                    act.wait_ge(s["yT_done"], b + 1)
                    act.activation(yT[:, :], MB[:, :], ACT.Identity, bias=ph.bv).then_inc(s["yT_copied"], 1)

                if ph is outer:
                    act.wait_ge(s_dve0, DVE_MODCOL)
                copy_hT(ph.first_batch)
                copy_q(ph.first_batch)
                if ph.own_k:
                    copy_k(ph.first_batch)
                copy_v(ph.first_batch, 0)
                if ph is outer:
                    for b in range(NB):
                        act.wait_ge(s_pe0, 8 + b)
                        act.activation(modB[:, b, :, :].rearrange("p a d -> p (a d)"), banks[1 + b % 4][:, :], ACT.Copy)\
                            .then_inc(s_act0, 1)

                sel = select_step(ph)

                def body(i, q, prev, cur, nxt):
                    for k in range(STEPS):
                        b, _, step, on = second_pass(i, q, prev, cur, k, LAG)
                        if on:
                            for n in range(HG):
                                exp(b, step, n)
                        b, _, step, on = second_pass(i, q, prev, cur, k, weigh_lag(ph))
                        if on and step % TC == TC - 1:
                            copy_av(b, step // TC)
                        if k == 3 and nxt:
                            copy_hT(i + 1)
                        if k == 4 and nxt:
                            copy_q(i + 1)
                        if k == 5 and nxt and ph.own_k:
                            copy_k(i + 1)
                        if k == weigh_lag(ph) and nxt:
                            copy_v(i + 1, 1 - q)
                        if k == LAG + sel + 1 and prev:
                            copy_yT(i - 1)
                batches(act, ph, body)

            attention(outer)
            act.wait_ge(outer.s["residual_done"], NB)
            attention(layer[0])
            act.wait_ge(layer[0].s["residual_done"], NB)

            def tok_hT(b):
                act.wait_ge(tok["xT_ready"], b + 1)
                wait(act, tok["hidden"], b * E * FC)
                act.activation(hT[:, :], MA[:, :], ACT.Identity, bias=cols[:, LN2B:LN2B + 1],
                               scale=cols[:, LN2W:LN2W + 1]).then_inc(tok["hT_ready"], 1)

            def tok_experts(b):
                for e in range(E):
                    for f in range(FC):
                        u = e * FC + f
                        act.wait_ge(tok["hidden"], b * (E * FC) + u + 1)
                        if f == 0:
                            wait(act, tok["expert_out"], b * E + e - 1)
                        act.activation(hid[e % 2][:, f, :], HB[f][:, :], ACT.Gelu,
                                       bias=cols[:, B1 + u:B1 + u + 1]).then_inc(tok["gelu_done"], 1)

            tok_hT(0)
            tok_experts(0)
            tok_hT(1)
            with act.Fori(1, NB - 1) as i:
                tok_experts(i)
                tok_hT(i + 1)
            tok_experts(NB - 1)
            act.wait_ge(tok["accumulated"], NB * E)
            attention(layer[1])
            act.wait_ge(layer[1].s["residual_done"], 2 * NB)

            for b in range(NB):
                act.wait_ge(seq["xT_ready"], b + 1)
                act.activation(hT_all[:, b * S:(b + 1) * S], (MA, MB)[b % 2][:, :], ACT.Identity, bias=cols[:, LN2B + 1:LN2B + 2],
                               scale=cols[:, LN2W + 1:LN2W + 2], accum_out=hsum[:, b:b + 1]).then_inc(seq["hT_ready"], 1)

            def seq_experts(j):
                for slot in range(NSLOT):
                    n = j * NSLOT + slot
                    act.wait_ge(seq_loaded[slot], (j + 1) * (16 * SLOT_DMAS))
                    wait(act, seq["expert_out"], n - 1)
                    for f in range(FC):
                        act.wait_ge(seq["hidden"], n * FC + f + 1)
                        act.activation(hid[slot % 2][:, f, :], HB[f][:, :], ACT.Gelu,
                                       bias=b1_slot[slot][:, f:f + 1]).then_inc(seq["gelu_done"], 1)

            seq_experts(0)
            with act.Fori(1, NB // 2) as j:
                seq_experts(j)

        @block.vector
        def _(dve):
            chain = [0]

            def link(ins):
                chain[0] += 1
                ins.then_inc(s_dve0, 1)
                dve.wait_ge(s_dve0, chain[0])

            def regroup(dst, src):
                return dve.tensor_copy(dst.rearrange("x (a d p) -> x p a d", a=2, d=HD),
                                       src.rearrange("x (p a d) -> x p a d", a=2, d=HD))

            def settled(sem_, value):
                dve.wait_ge(sem_, value)
                dve.sem_inc(s_own_dve, 1)

            def statistics(stream, b, st, mv, s_chain, done, n):
                if not (isinstance(n, int) and n == 0):
                    settled(done, n)
                for c in range(TC):
                    ins = dve.bn_stats(st[:, c, :], tokens(stream, b, c))
                ins.then_inc(s_chain, 1)
                settled(s_chain, n + 1)
                for c in range(TC):
                    ins = dve.bn_aggr(mv[:, c, :], st[:, c, :])
                ins.then_inc(done, 1)

            for t in Vt:
                link(dve.memset(t[:], 0.0))
                link(dve.memset(t[:, :, :, HD:HD + 1], 1.0))
            dve.wait_ge(s_x0, 16)
            statistics(xr, 0, stats, mean_var, outer.s["mv_chain"], outer.s["stats_done"], 0)
            link(dve.memset(stacks[:, 0:2], 0.0))
            link(dve.memset(Ks[0][:], 1.0))
            dve.wait_ge(s_act0, 1)
            dve.wait_ge(s_cond, 32)
            link(dve.tensor_scalar(cond_b[:, :], cond_a[:, :], 1.0, None, ALU.add))
            link(dve.reciprocal(cond_a[:, :], cond_b[:, :]))
            link(dve.tensor_tensor(cond_b[:, :], cond_a[:, :], cond[:, :], ALU.mult))
            assert chain[0] == DVE_SILU
            dve.wait_ge(s_const, 2)
            dve.wait_ge(s_ld, EARLY_LOADS)
            link(dve.tensor_tensor(tril_raw.rearrange("p (h j) -> p h j", h=H),
                                   tril_rows[:, :].unsqueeze(1).to_broadcast([P, H, HD]),
                                   blockdiag[:, :].unsqueeze(2).to_broadcast([P, H, HD]), ALU.mult))
            dve.wait_ge(s_pe0, 1)
            link(dve.tensor_copy(condT[:, :], MA[:, 0:NB]))
            for dst, src in ((tril_block[:, :], tril_raw), (rows_regrouped, rows[:, :])):
                link(regroup(dst, src))
            assert chain[0] == DVE_CONDT
            dve.wait_ge(s_pe0, 2)
            link(dve.tensor_copy(cols[:, :], MB[:, 0:NROW]))
            dve.wait_ge(s_pe0, 4)
            link(dve.tensor_copy(cols_regrouped[:, :], MB[:, 256:256 + NROW]))
            dve.wait_ge(s_pe0, 6)
            link(dve.tensor_copy(mod_cols[:, 0, :], MA[:, 384:384 + NB]))
            link(dve.tensor_scalar(mod_cols[:, 1, :], MA[:, 384 + NB:384 + 2 * NB], 1.0, None, ALU.add))
            assert chain[0] == DVE_MODCOL
            dve.wait_ge(s_pe0, 7)
            link(dve.tensor_copy(mod_row[:, 1:3, :].rearrange("b a d -> b (a d)"), banks[0][0:NB, P:3 * P]))
            for n in range(2):
                src = banks[0][0:NB, 0:P] if n == 0 else banks[0][0:NB, 3 * P:4 * P]
                link(dve.tensor_scalar(mod_tmp[:, n, :], src, 0.0, 2.0, ALU.is_ge, ALU.mult))
                link(dve.tensor_scalar(mod_tmp2[:, n, :], src, -1.0, None, ALU.mult))
                link(dve.scalar_tensor_tensor(mod_tmp2[:, n, :], src, 0.25, mod_tmp2[:, n, :], ALU.max, ALU.max))
                link(dve.scalar_tensor_tensor(mod_row[:, 3 * n, :], mod_tmp[:, n, :], 1.0, mod_tmp2[:, n, :],
                                              ALU.subtract, ALU.mult))
            link(dve.tensor_scalar(mod_row[:, 2, :], mod_row[:, 2, :], 1.0, None, ALU.add))
            assert chain[0] == DVE_MODROW
            dve.wait_ge(s_late, LATE_LOADS)
            for dst, src in ((wq_sb[:, 0, :], wqk_raw[:, 0, :]), (wq_sb[:, 1, :], wqk_raw[:, 1, :]),
                             (wk_sb[:, 0, :], wqk_raw[:, 2, :]), (wk_sb[:, 1, :], wqk_raw[:, 3, :])):
                link(regroup(dst, src))
            assert chain[0] == DVE_WEIGHTS

            def attention(ph):
                s = ph.s

                def stats_of(b):
                    if ph is outer:
                        dve.wait_ge(s_x, 16 * (NB - 1))
                    wait(dve, s["xn_ready"], b)
                    statistics(ph.stream, b - ph.first_batch, stats, mean_var, s["mv_chain"], s["stats_done"], b)

                def maxima(i, k, n):
                    v = k * HG + n
                    if v % 16 == 0:
                        wait(dve, s["shift_split"], i * G + k // TC - G + 1)
                    dve.wait_ge(s["scores_q"], i * UNITS + v + 1)
                    c = first_chunk(ph, k)
                    w, at = first_width(ph, c), HG * (k // TC * TC + c) + n
                    if ph.causal:
                        dve.sem_inc(s_own_dve, 1)
                        dve.tensor_tensor_reduce(bank_q(ph, v)[:, 0:w], bank_q(ph, v)[:, 0:w], mask_q[:, S - w:S], 1.0, NEG,
                                                 ALU.add, ALU.max, row_max[:, at:at + 1]).then_inc(s["max_done"], 1)
                    else:
                        dve.tensor_reduce(row_max[:, at:at + 1], bank_q(ph, v)[:, 0:w], AX_X, ALU.max)\
                            .then_inc(s["max_done"], 1)

                def split_max(b, g):
                    m = b * G + g
                    dve.wait_ge(s["max_done"], b * UNITS + 16 * (g + 1))
                    wait(dve, s["max_T"], m - 1)
                    t = shift_tok[g % 2]
                    rm = row_max[:, 16 * g:16 * g + 16].rearrange("p (c h) -> p c h", h=HG)
                    dve.tensor_scalar(t[:, :, 0, :], rm, -1.0, None, ALU.mult).then_inc(s["shift_half"], 1)
                    dve.wait_ge(s["shift_half"], m + 1)
                    dve.scalar_tensor_tensor(t[:, :, 1, :], rm, -1.0, t[:, :, 0, :], ALU.mult, ALU.subtract)\
                        .then_inc(s["shift_split"], 1)

                def copy_shift(b, g):
                    dve.wait_ge(s["max_T"], b * G + g + 1)
                    wait(dve, rows_shifted(ph, g), (b * (G // 2) + g // 2) * (16 * SHIFT_DMAS))
                    dve.tensor_copy(shift[g % 2][:, :], MA[:, :].bitcast(BF16)[0:2 * HG, 0:S]).then_inc(s["shift_copied"], 1)

                def normalise_heads(b, g):
                    dve.wait_ge(s["heads_sel"], b * G + g + 1)
                    m = MB[:, 0:TC * 36].rearrange("p (c n) -> p c n", c=TC)
                    dve.reciprocal(recip[:, :, :], m[:, :, 32:36]).then_inc(s["recip_done"], 1)
                    dve.wait_ge(s["recip_done"], b * G + g + 1)
                    if g == 0:
                        wait(dve, s["yT_done"], b)
                    dve.tensor_tensor(y_sb[:, :, 32 * g:32 * g + 32].rearrange("p c (h d) -> p c h d", d=HD),
                                      m[:, :, 0:32].rearrange("p c (h d) -> p c h d", d=HD),
                                      recip[:, :, :].unsqueeze(3).to_broadcast([P, TC, HG, HD]), ALU.mult)\
                        .then_inc(s["y_ready"], 1)

                def residual(b):
                    dve.wait_ge(s["out_proj"], b + 1)
                    dve.wait_ge(s["bias_added"], b + 1)
                    t = tokens(ph.stream, b - ph.first_batch)
                    dve.tensor_tensor(t, MA[:, :].rearrange("p (c d) -> p c d", c=TC), t, ALU.add)\
                        .then_inc(s["residual_done"], 1)

                def tail_stats(b):
                    dve.wait_ge(s["residual_done"], b + 1)
                    wait(dve, s["tail_done"], b + 1)
                    statistics(xr, b, stats2, mean_var2, s["mv2_chain"], s["stats2_done"], b)

                if ph is not outer:
                    stats_of(ph.first_batch)

                sel = select_step(ph)

                def body(i, q, prev, cur, nxt):
                    for k in range(STEPS):
                        if k == 0 and prev:
                            split_max(i - 1, G - 1)
                        elif k and k % TC == 0 and cur:
                            split_max(i, k // TC - 1)
                        for n in range(HG):
                            if cur:
                                maxima(i, k, n)
                            if n == 1 and k == 0 and prev:
                                copy_shift(i - 1, G - 1)
                            elif n == 1 and k and k % TC == 0 and cur:
                                copy_shift(i, k // TC - 1)
                        if k == 0 and nxt:
                            stats_of(i + 1)
                        if prev and k % TC == sel and k <= sel + 2 * TC:
                            normalise_heads(i - 1, k // TC + 1)
                        if k == LAG + sel + 2 and prev:
                            residual(i - 1)
                        if k == LAG + sel + 3 and prev and ph is outer:
                            tail_stats(i - 1)
                        if k == sel + LAG + TC and cur:
                            normalise_heads(i, 0)
                batches(dve, ph, body)

            attention(outer)
            dve.wait_ge(outer.s["tail_done"], NB + 1)
            attention(layer[0])
            dve.wait_ge(layer[0].s["residual_done"], NB)

            def top_two(lg, t8, ti, tif, gp, s_chain, n0, rows_, nc_):
                dve.sem_inc(s_own_dve, 1)
                for c in range(nc_):
                    dve.max(t8[0:rows_, c, :], lg[0:rows_, c, :]).then_inc(s_chain, 1)
                settled(s_chain, n0 + nc_)
                for c in range(nc_):
                    dve.max_index(ti[0:rows_, c, :], t8[0:rows_, c, :], lg[0:rows_, c, :]).then_inc(s_chain, 1)

            def tok_stats(b):
                wait(dve, tok["xn_ready"], b)
                statistics(yr, b, stats, mean_var, tok["mv_chain"], tok["stats_done"], b)

            GC = 2 * TC + 8

            def tok_gate_a(b):
                dve.wait_ge(tok["logits_ready"], b + 1)
                lg = logits[:, :, :]
                dve.tensor_tensor(lg, MB[:, 0:TC * E].rearrange("p (c e) -> p c e", c=TC),
                                  gate_bias[:, 0, :].unsqueeze(1).to_broadcast([P, TC, E]), ALU.add)\
                    .then_inc(tok["logits_copied"], 1)
                dve.wait_ge(tok["logits_copied"], b + 1)
                top_two(logits, top8, top_idx, top_idxf, gap, tok["gate_chain"], b * GC, P, TC)
                dve.tensor_tensor(gap[:, :], top8[:, :, 1], top8[:, :, 0], ALU.subtract).then_inc(tok["gap_ready"], 1)

            def tok_gate_b(b):
                s_, n = tok["gate_chain"], [b * GC + 2 * TC]

                def step(ins):
                    n[0] = n[0] + 1
                    ins.then_inc(s_, 1)
                    dve.wait_ge(s_, n[0])

                dve.wait_ge(s_, n[0])
                step(dve.tensor_copy(top_idxf[:, :, :], top_idx[:, :, 0:2]))
                dve.wait_ge(tok["gap_exp"], b + 1)
                step(dve.tensor_scalar(denom[:, :], gap_exp[:, :], 1.0, None, ALU.add))
                step(dve.reciprocal(weight[:, :, 0], denom[:, :]))
                step(dve.tensor_tensor(weight[:, :, 1], weight[:, :, 0], gap_exp[:, :], ALU.mult))
                for m in range(2):
                    step(dve.tensor_tensor(pick[m][:, :, :], iota8[:, :].unsqueeze(1).to_broadcast([P, TC, E]),
                                           top_idxf[:, :, m:m + 1].to_broadcast([P, TC, E]), ALU.is_equal))
                    step(dve.tensor_tensor(pick[2 + m][:, :, :], pick[m][:, :, :],
                                           weight[:, :, m:m + 1].to_broadcast([P, TC, E]), ALU.mult))
                wait(dve, tok["combine_T"], b)
                wait(dve, tok["accumulated"], b * E)
                dve.tensor_tensor(combine[:, :, :], pick[2][:, :, :], pick[3][:, :, :], ALU.add)\
                    .then_inc(tok["combine_ready"], 1)
                dve.wait_ge(tok["combine_ready"], b + 1)

            def tok_combineT(b):
                dve.wait_ge(tok["combine_T"], b + 1)
                wait(dve, tok["b2_ready"], b)
                dve.tensor_copy(combineT[:, :], MA[0:E, :]).then_inc(tok["combineT_copied"], 1)

            def tok_b2(b):
                dve.wait_ge(tok["b2_ready"], b + 1)
                dve.wait_ge(tok["accumulated"], b * E + 3)
                t = tokens(yr, b)
                dve.tensor_tensor(t, MB[:, :].rearrange("p (c d) -> p c d", c=TC), t, ALU.add).then_inc(tok["b2_added"], 1)

            def tok_accumulate(b, e):
                dve.wait_ge(tok["expert_out"], b * E + e + 1)
                if e > 0:
                    dve.wait_ge(tok["accumulated"], b * E + e)
                if e == 3:
                    dve.wait_ge(tok["b2_added"], b + 1)
                for c in range(TC):
                    t = tokens(yr, b, c)
                    ins = dve.scalar_tensor_tensor(t, YB[e % 2][:, c * P:(c + 1) * P], combine[:, c, e:e + 1], t,
                                                   ALU.mult, ALU.add)
                ins.then_inc(tok["accumulated"], 1)

            def tok_body(i, prev, nxt):
                if prev:
                    tok_accumulate(i - 1, E - 1)
                tok_gate_b(i)
                tok_combineT(i)
                for e in range(1, E):
                    tok_accumulate(i, e - 1)
                    if e == 1 and nxt:
                        tok_stats(i + 1)
                    if e == 3:
                        tok_b2(i)
                if nxt:
                    tok_gate_a(i + 1)

            tok_stats(0)
            tok_gate_a(0)
            tok_body(0, False, True)
            with dve.Fori(1, NB - 1) as i:
                tok_body(i, True, True)
            tok_body(NB - 1, True, False)
            tok_accumulate(NB - 1, E - 1)
            dve.wait_ge(tok["accumulated"], NB * E)
            attention(layer[1])
            dve.wait_ge(layer[1].s["residual_done"], 2 * NB)

            for n in range(NB * TC):
                dve.bn_stats(stats_all[:, n, :], yr[:, n * P:(n + 1) * P]).then_inc(seq["mv_chain"], 1)
            dve.wait_ge(seq["mv_chain"], NB * TC)
            for n in range(NB * TC):
                dve.bn_aggr(mv_all[:, n, :], stats_all[:, n, :]).then_inc(seq["aggregated"], 1)
            dve.wait_ge(seq["rstd_ready"], 1)
            for b in range(NB):
                wait(dve, seq["xT_ready"], b - 1)
                for c in range(TC):
                    n = b * TC + c
                    ins = dve.tensor_scalar(seq_xn[b % 2][:, c, :], yr[:, n * P:(n + 1) * P], mv_all[:, n, 0:1],
                                            rstd_all[:, n:n + 1], ALU.subtract, ALU.mult)
                ins.then_inc(seq["xn_ready"], 1)
            dve.wait_ge(seq["logits_ready"], 1)
            lg = logits[0:NB, 0:1, :]
            dve.scalar_tensor_tensor(logits[0:NB, 0, :], MA[0:NB, 0:E], 1.0 / S, gate_bias[0:NB, 1, :], ALU.mult, ALU.add)\
                .then_inc(seq["gate_chain"], 1)
            dve.wait_ge(seq["gate_chain"], 1)
            dve.max(top8[0:NB, 0, :], logits[0:NB, 0, :]).then_inc(seq["gate_chain"], 1)
            dve.wait_ge(seq["gate_chain"], 2)
            dve.max_index(top_idx[0:NB, 0, :], top8[0:NB, 0, :], logits[0:NB, 0, :]).then_inc(seq["gate_chain"], 1)
            dve.tensor_tensor(gap[0:NB, 0:1], top8[0:NB, 0, 1:2], top8[0:NB, 0, 0:1], ALU.subtract).then_inc(seq["gap_ready"], 1)
            dve.wait_ge(seq["gate_chain"], 3)
            dve.tensor_copy(top_idxf[0:NB, 0, :], top_idx[0:NB, 0, 0:2]).then_inc(seq["gate_chain"], 1)
            dve.wait_ge(seq["gap_exp"], 1)
            dve.tensor_scalar(denom[0:NB, 0:1], gap_exp[0:NB, 0:1], 1.0, None, ALU.add).then_inc(seq["gate_chain"], 1)
            dve.wait_ge(seq["gate_chain"], 5)
            dve.reciprocal(weight[0:NB, 0, 0:1], denom[0:NB, 0:1]).then_inc(seq["gate_chain"], 1)
            dve.wait_ge(seq["gate_chain"], 6)
            dve.tensor_tensor(weight[0:NB, 0, 1:2], weight[0:NB, 0, 0:1], gap_exp[0:NB, 0:1], ALU.mult)\
                .then_inc(seq["gate_chain"], 1)
            dve.wait_ge(seq["gate_chain"], 7)
            for m, src in enumerate((weight, top_idxf)):
                dve.tensor_tensor(seq_both[:, m, :, :], src[0:NB, 0, :].unsqueeze(1).to_broadcast([NB, NB, 2]),
                                  ident[0:NB, 0:NB].unsqueeze(2).to_broadcast([NB, NB, 2]), ALU.mult).then_inc(seq["both_ready"], 1)
            dve.wait_ge(seq["both_B"], 1)
            dve.tensor_copy(seq_idx[0:1, :], MB[0:1, 2 * NB:4 * NB]).then_inc(seq["picked"], 1)
            dve.tensor_copy(seqB[:, :], MB[:, 0:2 * NB]).then_inc(seq["gate_chain"], 1)
            dve.wait_ge(seq["gate_chain"], 8)

            def seq_apply(j):
                for slot in range(NSLOT):
                    n = j * NSLOT + slot
                    b = j * 2 + slot // 2
                    w = seqB[:, bass.ds(n, 1)]
                    dve.wait_ge(seq_loaded[slot], (j + 1) * (16 * SLOT_DMAS))
                    wait(dve, seq["accumulated"], n)
                    for c in range(TC):
                        t = tokens(yr, b, c)
                        ins = dve.scalar_tensor_tensor(t, b2_slot[slot][:, :], w, t, ALU.mult, ALU.add)
                    ins.then_inc(seq["b2_added"], 1)
                    dve.wait_ge(seq["b2_added"], n + 1)
                    dve.wait_ge(seq["expert_out"], n + 1)
                    for c in range(TC):
                        t = tokens(yr, b, c)
                        ins = dve.scalar_tensor_tensor(t, YB[slot % 2][:, c * P:(c + 1) * P], w, t, ALU.mult, ALU.add)
                    ins.then_inc(seq["accumulated"], 1)

            seq_apply(0)
            with dve.Fori(1, NB // 2) as j:
                seq_apply(j)

        @block.tensor
        def _(pe):
            pe.wait_ge(s_const, 2)
            pe.wait_ge(s_dve0, DVE_SILU)
            pe.transpose(MA[:, 0:NB], cond_b[:, :], ident[0:NB, 0:NB]).then_inc(s_pe0, 1)
            pe.wait_ge(s_ld, EARLY_LOADS)
            pe.transpose(MB[:, 0:NROW], rows[:, :], ident[0:NROW, 0:NROW]).then_inc(s_pe0, 1)
            pe.wait_ge(s_dve0, DVE_CONDT)
            pe.transpose(MA[:, 0:P], w_raw[:, 0, :], ident[:, :]).then_inc(s_pe0, 1)
            pe.wait_ge(s_dve0, DVE_CONDT + 1)
            pe.transpose(MB[:, 256:256 + NROW], rows_regrouped, ident[0:NROW, 0:NROW]).then_inc(s_pe0, 1)
            pe.wait_ge(s_dve0, DVE_CONDT + 2)
            pe.transpose(MB[:, 0:P], w_raw[:, 1, :], ident[:, :]).then_inc(s_pe0, 1)
            pe.wait_ge(s_act0, 2)
            for m in range(2):
                ins = pe.matmul(MA[:, 384 + m * NB:384 + (m + 1) * NB], wmod_sb[:, m * P:(m + 1) * P], condT[:, :],
                                start=True, stop=True)
            ins.then_inc(s_pe0, 1)
            pe.matmul(banks[0][0:NB, :], condT[:, :], wmod_sb[:, 2 * P:6 * P], start=True, stop=True).then_inc(s_pe0, 1)

            def spread_modulation():
                pe.wait_ge(s_dve0, DVE_MODROW)
                for b in range(NB):
                    if b >= 4:
                        pe.wait_ge(s_act0, ACT_MODB - NB + b - 3)
                    pe.matmul(banks[1 + b % 4][:, :], batch_row[:, b, :], mod_row[:, :, :].rearrange("b a d -> b (a d)"),
                              start=True, stop=True).then_inc(s_pe0, 1)
                pe.wait_ge(s_act0, ACT_MODB)
                pe.wait_ge(s_dve0, DVE_WEIGHTS)
                pe.wait_ge(s_late, LATE_LOADS)

            def transposed(bank, src, chunks=TC, rows_=P):
                for c in range(chunks):
                    ins = pe.transpose(bank[0:rows_, c * P:(c + 1) * P], src[:, c, :], ident[:, :])
                return ins

            def attention(ph):
                s = ph.s
                freed = {}

                def take(bank):
                    wait(pe, *freed[bank])

                def max_T(b, g):
                    take("A")
                    pe.wait_ge(s["shift_split"], b * G + g + 1)
                    for c in range(TC):
                        ins = pe.transpose(MA[:, :].bitcast(BF16)[0:2 * HG, c * P:(c + 1) * P],
                                           shift_tok[g % 2][:, c, :, :].rearrange("p a h -> p (a h)"), identb[:, :])
                    ins.then_inc(s["max_T"], 1)
                    freed["A"] = (s["shift_copied"], b * G + g + 1)

                def normed_T(b):
                    take("B")
                    pe.wait_ge(s["xn_ready"], b + 1)
                    transposed(MB, xn).then_inc(s["xT_ready"], 1)
                    freed["B"] = (s["hT_ready"], b + 1)

                def project_q(b):
                    take("A")
                    pe.wait_ge(s["hT_ready"], b + 1)
                    pe.matmul(MA[:, :], ph.wq, hT[:, :], start=True, stop=True).then_inc(s["q_proj"], 1)
                    freed["A"] = (s["q_copied"], b + 1)

                def project_k(b):
                    take("B")
                    pe.wait_ge(s["hT_ready"], b + 1)
                    pe.matmul(MB[:, :], ph.wk, hT[:, :], start=True, stop=True).then_inc(s["k_proj"], 1)
                    freed["B"] = (s["k_copied"], b + 1)

                def project_v(b):
                    take("A")
                    pe.wait_ge(s["hT_ready"], b + 1)
                    for c in range(TC):
                        ins = pe.matmul(MA[:, c * P:(c + 1) * P], hT[:, c * P:(c + 1) * P], ph.wv, start=True, stop=True)
                    ins.then_inc(s["v_proj"], 1)
                    freed["A"] = (s["v_ready"], b + 1)

                def select_heads(b, g):
                    take("B")
                    pe.wait_ge(s["av_copied"], b * G + g + 1)
                    for c in range(TC):
                        ins = pe.matmul(MB[:, c * 36:(c + 1) * 36], av_sb[g % 2][:, c * P:(c + 1) * P], head_sel[:, :],
                                        start=True, stop=True)
                    ins.then_inc(s["heads_sel"], 1)
                    freed["B"] = (s["y_ready"], b * G + g + 1)

                def heads_T(b):
                    take("B")
                    pe.wait_ge(s["y_ready"], b * G + G)
                    transposed(MB, y_sb).then_inc(s["yT_done"], 1)
                    freed["B"] = (s["yT_copied"], b + 1)

                def project_out(b, q):
                    take("A")
                    pe.wait_ge(s["yT_copied"], b + 1)
                    if ph is outer:
                        pe.wait_ge(s["wo_gated"], b + 1)
                        w = wo_gated[:, :]
                    else:
                        w = wo_sb[:, ph.n, :]
                    for c in range(TC):
                        ins = pe.matmul(MA[:, c * P:(c + 1) * P], yT[:, c * P:(c + 1) * P], w, start=True, stop=True)
                    ins.then_inc(s["out_proj"], 1)
                    freed["A"] = (s["residual_done"], b + 1)

                def first(i, q, k, n):
                    g, c = k // TC, first_chunk(ph, k)
                    v, h = k * HG + n, g * HG + n
                    w = first_width(ph, c)
                    if v == 0:
                        pe.wait_ge(s["q_stacked"], (i + 1) * (16 * STACK_DMAS))
                        pe.wait_ge(s["k_stacked"], (i + 1) * (16 * STACK_DMAS))
                    wait(pe, s["max_done"], i * UNITS + max(0, v + 1 - first_banks(ph)))
                    pe.matmul(bank_q(ph, v)[:, 0:w], Qs[q][h % 2][0:SHIFT_ROW, h // 2, c * P:(c + 1) * P],
                              Ks[q][0:SHIFT_ROW, h // 2, 0:w], start=True, stop=True).then_inc(s["scores_q"], 1)

                def second(b, q, step, n):
                    g, c = step // TC, step % TC
                    u, h = step * HG + n, g * HG + n
                    lo = second_low(ph, c)
                    if c == 0 and n == 0:
                        pe.wait_ge(rows_shifted(ph, g), (b * (G // 2) + g // 2 + 1) * (16 * SHIFT_DMAS))
                    wait(pe, s["exp_done"], b * UNITS + max(0, u + 1 - (5 - first_banks(ph))))
                    pe.matmul(bank_k(ph, u)[:, 0:S - lo], Ks[q][:, h // 2, c * P:(c + 1) * P],
                              Qs[q][h % 2][:, h // 2, lo:S], start=True, stop=True).then_inc(s["scores_k"], 1)

                def weigh(b, q, step):
                    g, c = step // TC, step % TC
                    lo = second_low(ph, c)
                    pe.wait_ge(s["exp_done"], b * UNITS + (step + 1) * HG)
                    if ph.causal:
                        pe.wait_ge(s["masked"], b * STEPS + step + 1)
                    if step == 0:
                        pe.wait_ge(s["v_ready"], b + 1)
                    if c == 0:
                        wait(pe, s["av_copied"], b * G + g)
                    for n in range(HG):
                        ins = pe.matmul(AV[32 * n:32 * n + 32, lo:S], Vt[q][:, c, g * HG + n, :],
                                        probs(ph, step)[:, n, :], start=(c == 0), stop=(c == TC - 1))
                    ins.then_inc(s["av_done"], 1)

                if ph is outer:
                    freed["A"], freed["B"] = (s_dve0, DVE_MODCOL), (s_act0, 3)
                else:
                    freed["A"] = freed["B"] = (None, 0)
                normed_T(ph.first_batch)
                project_q(ph.first_batch)
                if ph.own_k:
                    project_k(ph.first_batch)
                project_v(ph.first_batch)
                if ph is outer:
                    spread_modulation()

                sel = select_step(ph)

                def body(i, q, prev, cur, nxt):
                    if prev:
                        freed["A"] = (s["shift_copied"], (i - 1) * G + G - 1)
                        freed["B"] = (s["y_ready"], (i - 1) * G + 1)
                    for k in range(STEPS):
                        b2, q2, step2, on2 = second_pass(i, q, prev, cur, k, LAG)
                        b3, q3, step3, on3 = second_pass(i, q, prev, cur, k, weigh_lag(ph))
                        for n in range(HG):
                            if on2:
                                second(b2, q2, step2, n)
                            if cur:
                                first(i, q, k, n)
                            if n == 1:
                                if on3:
                                    weigh(b3, q3, step3)
                                if k == 0 and prev:
                                    max_T(i - 1, G - 1)
                                elif k and k % TC == 0 and cur:
                                    max_T(i, k // TC - 1)
                        if k == 3 and nxt:
                            normed_T(i + 1)
                        if k == 4 and nxt:
                            project_q(i + 1)
                        if prev and k % TC == sel and k <= sel + 2 * TC:
                            select_heads(i - 1, k // TC + 1)
                        if k == 5 and nxt and ph.own_k:
                            project_k(i + 1)
                        if k == weigh_lag(ph) and nxt:
                            project_v(i + 1)
                        if k == LAG + sel + 1 and prev:
                            heads_T(i - 1)
                        if k == LAG + sel + 2 and prev:
                            project_out(i - 1, 1 - q)
                        if k == sel + LAG + TC and cur:
                            select_heads(i, 0)
                batches(pe, ph, body)

            attention(outer)
            pe.wait_ge(outer.s["residual_done"], NB)
            attention(layer[0])
            pe.wait_ge(layer[0].s["residual_done"], NB)
            pe.wait_ge(s_w, 32)

            def tok_normed_T(b):
                pe.wait_ge(tok["xn_ready"], b + 1)
                wait(pe, tok["combineT_copied"], b)
                transposed(MA, xn).then_inc(tok["xT_ready"], 1)

            def tok_logits(b):
                pe.wait_ge(tok["hT_ready"], b + 1)
                wait(pe, tok["b2_added"], b)
                for c in range(TC):
                    ins = pe.matmul(MB[:, c * E:(c + 1) * E], hT[:, c * P:(c + 1) * P], gate_sb[:, 0, :],
                                    start=True, stop=True)
                ins.then_inc(tok["logits_ready"], 1)

            def expert_up(sems, n, w1, x):
                for f in range(FC):
                    wait(pe, sems["gelu_done"], n * FC + f - FC + 1)
                    pe.matmul(HB[f][:, :], w1[:, f * P:(f + 1) * P], x, start=True, stop=True).then_inc(sems["hidden"], 1)

            def expert_down(sems, n, par, w2):
                pe.wait_ge(sems["gelu_done"], n * FC + FC)
                wait(pe, sems["accumulated"], n - 1)
                for c in range(TC):
                    for f in range(FC):
                        ins = pe.matmul(YB[par][:, c * P:(c + 1) * P], hid[par][:, f, c * P:(c + 1) * P], w2[:, f, :],
                                        start=(f == 0), stop=(f == FC - 1))
                ins.then_inc(sems["expert_out"], 1)

            def tok_body(i, prev, nxt):
                for e in range(E):
                    if e == 0:
                        pe.wait_ge(tok["hT_ready"], i + 1)
                    expert_up(tok, i * E + e, w1_sb[:, e, :], hT[:, :])
                    if e == 1:
                        pe.wait_ge(tok["combine_ready"], i + 1)
                        transposed(MA, combine, rows_=E).then_inc(tok["combine_T"], 1)
                    if e == 2:
                        pe.wait_ge(tok["combineT_copied"], i + 1)
                        pe.wait_ge(tok["logits_copied"], i + 1)
                        for c in range(TC):
                            ins = pe.matmul(MB[:, c * P:(c + 1) * P], combineT[:, c * P:(c + 1) * P], b2_sb[:, :],
                                            start=True, stop=True)
                        ins.then_inc(tok["b2_ready"], 1)
                    if e == E - 1 and nxt:
                        tok_normed_T(i + 1)
                    if e:
                        expert_down(tok, i * E + e - 1, (e - 1) % 2, w2_sb[:, e - 1, :, :])
                    elif prev:
                        expert_down(tok, i * E - 1, (E - 1) % 2, w2_sb[:, E - 1, :, :])
                if nxt:
                    tok_logits(i + 1)

            tok_normed_T(0)
            tok_logits(0)
            tok_body(0, False, True)
            with pe.Fori(1, NB - 1) as i:
                tok_body(i, True, True)
            tok_body(NB - 1, True, False)
            expert_down(tok, NB * E - 1, (E - 1) % 2, w2_sb[:, E - 1, :, :])
            pe.wait_ge(tok["accumulated"], NB * E)
            attention(layer[1])
            pe.wait_ge(layer[1].s["residual_done"], 2 * NB)

            for b in range(NB):
                pe.wait_ge(seq["xn_ready"], b + 1)
                wait(pe, seq["hT_ready"], b - 1)
                transposed((MA, MB)[b % 2], seq_xn[b % 2]).then_inc(seq["xT_ready"], 1)
            pe.wait_ge(seq["hT_ready"], NB)
            pe.matmul(MA[0:NB, 0:E], hsum[:, :], gate_sb[:, 1, :], start=True, stop=True).then_inc(seq["logits_ready"], 1)
            pe.wait_ge(seq["both_ready"], 2)
            pe.matmul(MB[:, 0:4 * NB], ones8[:, :], seq_both[:, :, :, :].rearrange("p m b k -> p (m b k)"),
                      start=True, stop=True).then_inc(seq["both_B"], 1)

            def seq_body(j):
                for slot in range(NSLOT):
                    n = j * NSLOT + slot
                    pe.wait_ge(seq_loaded[slot], (j + 1) * (16 * SLOT_DMAS))
                    expert_up(seq, n, w1_slot[slot], hT_all[:, bass.ds((j * 2 + slot // 2) * S, S)])
                    if slot or not isinstance(j, int):
                        expert_down(seq, n - 1, (slot - 1) % 2, w2_slot[(slot - 1) % NSLOT])

            seq_body(0)
            with pe.Fori(1, NB // 2) as j:
                seq_body(j)
            expert_down(seq, 2 * NB - 1, (NSLOT - 1) % 2, w2_slot[NSLOT - 1])


_INS = ['L0_attn_x', 'L0_attn_params', 'L0_attn_Wv', 'L0_attn_bv', 'L0_attn_Wo', 'L0_attn_bo', 'L0_ffn_ln1_w',
        'L0_ffn_ln1_b', 'L0_ffn_ln2_w', 'L0_ffn_ln2_b', 'L0_ffn_wq', 'L0_ffn_wk', 'L0_ffn_wv', 'L0_ffn_wo',
        'L0_ffn_bq', 'L0_ffn_bk', 'L0_ffn_bv', 'L0_ffn_bo', 'L0_ffn_gate_w', 'L0_ffn_gate_b', 'L0_ffn_e_w1',
        'L0_ffn_e_b1', 'L0_ffn_e_w2', 'L0_ffn_e_b2', 'L0_c', 'L0_wmod']
_OUTS = [((8, 512, 128), 'float32')]


def kernel(**inputs):
    import numpy as _np
    import concourse.bacc as _bacc
    from concourse import mybir as _mybir
    from concourse.bass_utils import run_bass_kernel_spmd as _run

    nc = _bacc.Bacc("TRN2", target_bir_lowering=False, num_devices=1)
    arrays, args = {}, []
    for name in _INS:
        a = _np.ascontiguousarray(inputs[name])
        arrays[f"in_{name}_dram"] = a
        args.append(nc.dram_tensor(f"in_{name}_dram", a.shape, _mybir.dt.from_np(a.dtype), kind="ExternalInput").ap())
    for i, (shape, dtype) in enumerate(_OUTS):
        dt = _mybir.dt.from_np(_np.dtype(dtype))
        args.append(nc.dram_tensor(f"out_{i}_dram", shape, dt, kind="ExternalOutput").ap())
    adaln_block(nc, *args)
    r = _run(nc, [arrays], core_ids=[0])
    got = tuple(r.results[0][f"out_{i}_dram"] for i in range(len(_OUTS)))
    return got[0]
```

```python
from contextlib import ExitStack

import concourse.bass as bass
from concourse import mybir

F32 = mybir.dt.float32
BF16 = mybir.dt.bfloat16
U32 = mybir.dt.uint32
I32 = mybir.dt.int32
ALU = mybir.AluOpType
ACT = mybir.ActivationFunctionType
AX_X = mybir.AxisListType.X

P = 128
EPS = 1e-5
NEG = -1e30
E_CONST = 2.718281828459045


class Phase:

    def __init__(self, s, first_batch, causal, own_k, stream, wq, wk, wv, bq, bk, bv, hw, hb, n):
        self.s, self.first_batch, self.causal, self.own_k, self.stream = s, first_batch, causal, own_k, stream
        self.wq, self.wk, self.wv, self.bq, self.bk, self.bv = wq, wk, wv, bq, bk, bv
        self.hw, self.hb, self.n = hw, hb, n


def wait(eng, sem, value):
    if isinstance(value, int) and value <= 0:
        return
    eng.wait_ge(sem, value)


def adaln_block(nc, x_in, params, Wv, bv, Wo, bo, ln1_w, ln1_b, ln2_w, ln2_b, wq, wk, wv, wo, bq, bk, bv2, bo2,
                gate_w, gate_b, e_w1, e_b1, e_w2, e_b2, c_in, wmod, out):
    NB, S, D = x_in.shape
    H = params.shape[0]
    HD = D // H
    TC = S // P
    E = gate_w.shape[2]
    FF = e_w1.shape[3]
    FC = FF // P
    L = gate_w.shape[0]
    HG = 4
    G = H // HG
    PAIRS = H // 2
    STEPS = G * TC
    UNITS = STEPS * HG
    LAG = 8
    SCALE = float(HD) ** -0.5
    assert D == P and HD == 8 and NB == 8 and STEPS == 16 and E == 8 and L == 2

    Q_PARTS = (0, 0, 0, 1, 1, 2)
    K_PARTS = (0, 1, 2, 0, 1, 0)
    NPROD = len(Q_PARTS)
    KROWS = NPROD * HD
    SHIFT_ROW = 64 + KROWS
    Q_RUNS = ((0, 0, 3, True), (3, 1, 2, True), (5, 2, 1, False))
    K_RUNS = ((0, 0, 3, False), (3, 0, 2, False), (5, 0, 1, False))
    SPILL_DMAS = 2 * len(Q_RUNS)
    STACK_DMAS = 2
    SHIFT_DMAS = 4

    with ExitStack() as ctx:
        def sb(name, shape, dt=F32):
            return ctx.enter_context(nc.sbuf_tensor(name, shape, dt))

        def psum(name, shape=(P, 512), dt=F32):
            return ctx.enter_context(nc.psum_tensor(name, list(shape), dt))

        def sem(name):
            return ctx.enter_context(nc.semaphore(name))

        xr = sb("xr", [P, NB * S])
        yr = sb("yr", [P, NB * S])

        ident = sb("ident", [P, P])
        identb = sb("identb", [P, P], BF16)
        mask_q = sb("mask_q", [P, S])
        head_sel = sb("head_sel", [P, 36])
        ones8 = sb("ones8", [E, P])
        blockdiag = sb("blockdiag", [P, H])
        iota8 = sb("iota8", [P, E])
        minus_half = sb("minus_half", [P, NB * TC])
        e_const = sb("e_const", [P, TC])

        NROW = 12 + 2 * E * FC + 1 + L
        rows = sb("rows", [NROW, P])
        cols = sb("cols", [P, NROW])
        cols_regrouped = sb("cols_regrouped", [P, NROW])
        LN1W, LN1B, LN2W, LN2B, BQ, BK, B1, BV = 0, 2, 4, 6, 8, 10, 12, NROW - 1 - L
        bias_row = sb("bias_row", [P, 1 + L, P])
        gate_bias = sb("gate_bias", [P, L, E])
        gate_sb = sb("gate_sb", [P, L, E])
        wq_sb = sb("wq_sb", [P, L, P])
        wk_sb = sb("wk_sb", [P, L, P])
        wv_sb = sb("wv_sb", [P, L, P])
        wo_sb = sb("wo_sb", [P, L, P])
        w_outer = sb("w_outer", [P, 2, P])
        wo_gated = sb("wo_gated", [P, P])
        tril_rows = sb("tril_rows", [P, HD])
        tril_block = sb("tril_block", [P, P])
        w1_sb = sb("w1_sb", [P, E, FF])
        w2_sb = sb("w2_sb", [P, E, FC, P])
        b2_sb = sb("b2_sb", [E, P])
        cond = sb("cond", [NB, P])
        cond_a = sb("cond_a", [NB, P])
        cond_b = sb("cond_b", [NB, P])
        condT = sb("condT", [P, NB])
        mod_cols = sb("mod_cols", [P, 2, NB])
        modB = sb("modB", [P, NB, 4, P])

        stats = sb("stats", [P, TC, 6])
        mean_var = sb("mean_var", [P, TC, 2])
        var_eps = sb("var_eps", [P, TC])
        rstd = sb("rstd", [P, TC])
        xn = sb("xn", [P, TC, P])
        hT = sb("hT", [P, S])
        q_f = sb("q_f", [P, S])
        k_f = sb("k_f", [P, S])
        q_parts = sb("q_parts", [P, 3, S], BF16)
        k_parts = sb("k_parts", [P, 3, S], BF16)
        stacks = sb("stacks", [P, 6, PAIRS, S], BF16)
        Qs = [[stacks[:, 2 * n + a] for a in range(2)] for n in range(2)]
        Ks = [stacks[:, 4 + n] for n in range(2)]
        Vt = [sb(f"Vt{n}", [P, TC, H, 32]) for n in range(2)]
        CAUSAL_AT = [HG * sum(S - P * j for j in range(c)) for c in range(TC + 1)]
        work_all = sb("work", [P, CAUSAL_AT[TC]])
        work = work_all[:, 0:2 * HG * S].rearrange("p (n s) -> p n s", s=S)

        def probs(ph, step):
            c = step % TC
            if ph.causal:
                return work_all[:, CAUSAL_AT[c]:CAUSAL_AT[c + 1]].rearrange("p (h s) -> p h s", h=HG)
            return work[:, step % 2 * HG:(step % 2 + 1) * HG, :]

        flat = work_all
        wmod_sb = flat[:, 0:6 * P]
        w_raw = flat[:, 6 * P:8 * P].rearrange("p (n d) -> p n d", n=2)
        batch_row = flat[0:NB, 8 * P:16 * P].rearrange("p (b d) -> p b d", b=NB)
        mod_row = flat[0:NB, 16 * P:20 * P].rearrange("p (n d) -> p n d", n=4)
        mod_tmp = flat[0:NB, 20 * P:22 * P].rearrange("p (n d) -> p n d", n=2)
        mod_tmp2 = flat[0:NB, 22 * P:24 * P].rearrange("p (n d) -> p n d", n=2)
        wqk_raw = flat[:, 24 * P:28 * P].rearrange("p (n d) -> p n d", n=4)
        tril_raw = flat[:, 28 * P:29 * P]
        rows_regrouped = flat[0:NROW, 29 * P:30 * P]
        row_max = sb("row_max", [P, UNITS])
        shift_tok = [sb(f"shift_tok{n}", [P, TC, 2, HG], BF16) for n in range(2)]
        shift = [sb(f"shift{n}", [2 * HG, S], BF16) for n in range(2)]
        av_sb = [sb(f"av_sb{n}", [P, S]) for n in range(2)]
        recip = sb("recip", [P, TC, HG])
        y_sb = sb("y_sb", [P, TC, P])
        yT = sb("yT", [P, S])
        bias_gated = sb("bias_gated", [P, P])
        stats2 = sb("stats2", [P, TC, 6])
        mean_var2 = sb("mean_var2", [P, TC, 2])
        var_eps2 = sb("var_eps2", [P, TC])
        rstd2 = sb("rstd2", [P, TC])

        hid = [work[:, n * FC:(n + 1) * FC, :] for n in range(2)]
        logits = sb("logits", [P, TC, E])
        top8 = sb("top8", [P, TC, 8])
        top_idx = sb("top_idx", [P, TC, 8], U32)
        top_idxf = sb("top_idxf", [P, TC, 2])
        gap = sb("gap", [P, TC])
        gap_exp = sb("gap_exp", [P, TC])
        denom = sb("denom", [P, TC])
        weight = sb("weight", [P, TC, 2])
        pick = [sb(f"pick{n}", [P, TC, E]) for n in range(4)]
        combine = sb("combine", [P, TC, E])
        combineT = av_sb[0][0:E, :]
        seq_xn = [xn, y_sb]
        stats_all = sb("stats_all", [P, NB * TC, 6])
        mv_all = sb("mv_all", [P, NB * TC, 2])
        ve_all = sb("ve_all", [P, NB * TC])
        rstd_all = sb("rstd_all", [P, NB * TC])
        hsum = sb("hsum", [P, NB])
        seq_both = sb("seq_both", [NB, 2, NB, 2])
        seqB = sb("seqB", [P, 2 * NB])
        seq_idx = sb("seq_idx", [P, 2 * NB], I32)
        NSLOT = 4
        w1_slot = [w1_sb[:, n, :] for n in range(NSLOT)]
        w2_slot = [w2_sb[:, n, :, :] for n in range(NSLOT)]
        b1_slot = [sb(f"b1_slot{n}", [P, FC]) for n in range(NSLOT)]
        b2_slot = [Vt[0][:, 0, 4 * n:4 * n + 4, :].rearrange("p h d -> p (h d)") for n in range(NSLOT)]
        hT_all = stacks[:, 0:2].rearrange("p a b s -> p (a b s)").bitcast(F32)

        q_dram = nc.dram_tensor("q_parts_dram", [2, NPROD, P // 2, S], BF16, kind="Internal").ap()
        k_dram = nc.dram_tensor("k_parts_dram", [2, NPROD, P // 2, S], BF16, kind="Internal").ap()

        banks = [psum(f"bank{n}") for n in range(8)]
        AV = banks[5]
        MA, MB = banks[6], banks[7]
        HB = banks[0:4]
        YB = banks[4:6]

        EARLY_LOADS = 16 * (2 + HD + 9)
        LATE_LOADS = 16 * (1 + 2 * L + 6)
        DVE_SILU = 2 * len(Vt) + 2 + 3
        DVE_CONDT = DVE_SILU + 4
        DVE_MODCOL = DVE_CONDT + 4
        DVE_MODROW = DVE_MODCOL + 10
        DVE_WEIGHTS = DVE_MODROW + 4
        ACT_MODB = 3 + NB
        s_ld = sem("early_loaded")
        s_late = sem("late_loaded")
        s_cond = sem("cond_loaded")
        s_x0 = sem("x_first_loaded")
        s_x1 = sem("x_second_loaded")
        s_x = sem("x_loaded")
        s_w = sem("expert_weights_loaded")
        s_pool0 = sem("pool_setup_chain")
        s_const = sem("constants_built")
        s_dve0 = sem("dve_setup_chain")
        s_pe0 = sem("pe_setup")
        s_act0 = sem("act_setup")
        s_own_pool = sem("pool_own")
        s_own_dve = sem("dve_own")
        s_own_sp = sem("sp_own")

        def attention_names(tag, more=()):
            names = ("stats_done", "rstd_chain", "xn_ready", "xT_ready", "hT_ready", "q_proj", "k_proj", "v_proj",
                     "qf_ready", "q_copied", "kf_ready", "k_copied", "q_split_chain", "k_split_chain", "q_split",
                     "k_split", "q_spilled", "k_spilled", "q_stacked", "k_stacked", "v_ready", "scores_q", "max_done",
                     "shift_half", "shift_split", "max_T", "shift_copied", "shift_rows0", "shift_rows1", "scores_k",
                     "exp_done", "masked", "av_done", "av_copied", "heads_sel", "recip_done", "y_ready", "yT_done",
                     "yT_copied", "out_proj", "bias_added", "residual_done", "mv_chain") + more
            return {n: sem(f"{tag}_{n}") for n in names}

        outer = Phase(attention_names("o", ("wo_gated", "bias_gated", "stats2_done", "tail_chain", "tail_normed",
                                            "tail_scaled", "tail_done", "mv2_chain")),
                      first_batch=0, causal=False, own_k=False, stream=xr,
                      wq=tril_block[:, :], wk=None, wv=w_outer[:, 0, :], bq=None, bk=None, bv=cols[:, BV:BV + 1],
                      hw=None, hb=None, n=None)
        layer_sems = attention_names("l")
        layer = [Phase(layer_sems, first_batch=n * NB, causal=True, own_k=True, stream=yr,
                       wq=wq_sb[:, n, :], wk=wk_sb[:, n, :], wv=wv_sb[:, n, :],
                       bq=cols_regrouped[:, BQ + n:BQ + n + 1], bk=cols_regrouped[:, BK + n:BK + n + 1],
                       bv=cols[:, BV + 1 + n:BV + 2 + n],
                       hw=cols[:, LN1W + n:LN1W + n + 1], hb=cols[:, LN1B + n:LN1B + n + 1], n=n) for n in range(2)]
        tok = {n: sem(f"t_{n}") for n in (
            "stats_done", "mv_chain", "rstd_chain", "xn_ready", "xT_ready", "hT_ready", "logits_ready", "logits_copied",
            "gap_ready", "gap_exp", "gate_chain", "combine_ready", "combine_T", "combineT_copied", "b2_ready",
            "b2_added", "hidden", "gelu_done", "expert_out", "accumulated")}
        seq = {n: sem(f"s_{n}") for n in (
            "mv_chain", "aggregated", "rstd_chain", "rstd_ready", "xn_ready", "xT_ready", "hT_ready", "logits_ready",
            "gate_chain", "gap_ready", "gap_exp", "both_ready", "both_B", "picked", "loaded0", "loaded1", "loaded2",
            "loaded3", "hidden", "gelu_done", "expert_out",
            "b2_added", "accumulated", "gated", "added", "stored")}

        seq_loaded = [seq["loaded0"], seq["loaded1"], seq["loaded2"], seq["loaded3"]]
        SLOT_DMAS = 4

        def rows_shifted(ph, g):
            return (ph.s["shift_rows0"], ph.s["shift_rows1"])[g % 2]

        def tokens(stream, b, c=None):
            if c is None:
                return stream[:, bass.ds(b * S, S)].rearrange("p (c d) -> p c d", c=TC)
            return stream[:, bass.ds(b * S + c * P, P)]

        def batches(eng, ph, body):
            n = ph.first_batch
            body(n, 0, False, True, True)
            with eng.Fori(0, (NB - 4) // 2) as j:
                body(j * 2 + (n + 1), 1, True, True, True)
                body(j * 2 + (n + 2), 0, True, True, True)
            body(n + NB - 3, 1, True, True, True)
            body(n + NB - 2, 0, True, True, True)
            body(n + NB - 1, 1, True, True, False)
            body(n + NB, 0, True, False, False)

        def second_pass(i, q, prev, cur, k, lag):
            if k < lag:
                return i - 1, 1 - q, k + STEPS - lag, prev
            return i, q, k - lag, cur

        def first_banks(ph):
            return 3

        def bank_q(ph, v):
            return banks[v % first_banks(ph)]

        def bank_k(ph, u):
            return banks[first_banks(ph) + u % (5 - first_banks(ph))]

        def handed_over(eng, ph, b, *counts):
            if ph is layer[0] and isinstance(b, int) and b == 0:
                for name, count in counts:
                    eng.wait_ge(outer.s[name], count)

        def weigh_lag(ph):
            return LAG + 2 if ph.causal else LAG + 1

        def select_step(ph):
            return weigh_lag(ph) - LAG

        def first_chunk(ph, k):
            return TC - 1 - k % TC if ph.causal else k % TC

        def first_width(ph, c):
            return (c + 1) * P if ph.causal else S

        def second_low(ph, c):
            return c * P if ph.causal else 0

        block = ctx.enter_context(nc.Block())

        @block.sync
        def _(sp):
            def load(dst, src, s=s_ld, **kw):
                sp.dma_start(dst, src, **kw).then_inc(s, 16)

            def load_x(b, s):
                sp.dma_start(xr[:, b * S:(b + 1) * S].rearrange("p (c d) -> p c d", c=TC),
                             x_in[b].rearrange("(c p) d -> p c d", p=P)).then_inc(s, 16)

            load_x(0, s_x0)
            load(cond[:, :], c_in, s_cond)
            load(wmod_sb[:, :], wmod, s_cond)
            load(w_raw[:, 0, :], Wv)
            load(w_raw[:, 1, :], Wo)
            sp.wait_ge(s_const, 1)
            for r in range(HD):
                load(tril_rows[r::HD, 0:r + 1],
                     params[:, r * (r + 1) // 2:r * (r + 1) // 2 + r + 1], allow_slow_non_contiguous=(r == 0))
            for n, v in enumerate((ln1_w, ln1_b, ln2_w, ln2_b, bq, bk)):
                load(rows[2 * n:2 * n + 2, :], v)
            load(rows[B1:BV, :], e_b1.rearrange("l e (f p) -> (l e f) p", p=P))
            load(rows[BV:BV + 1, :], bv.unsqueeze(0))
            load(rows[BV + 1:NROW, :], bv2)
            load_x(1, s_x1)
            load(bias_row[:, 0, :], bo.partition_broadcast(P), s_late)
            for n in range(L):
                load(bias_row[:, 1 + n, :], bo2[n].partition_broadcast(P), s_late)
                load(gate_bias[:, n, :], gate_b[n].partition_broadcast(P), s_late)
            load(gate_sb[:, :, :], gate_w.rearrange("l d e -> d l e"), s_late)
            load(wqk_raw[:, 0:L, :], wq.rearrange("l d e -> d l e"), s_late)
            load(wqk_raw[:, L:2 * L, :], wk.rearrange("l d e -> d l e"), s_late)
            load(wv_sb[:, :, :], wv.rearrange("l d e -> d l e"), s_late)
            load(wo_sb[:, :, :], wo.rearrange("l d e -> d l e"), s_late)
            load(b2_sb[:, :], e_b2[0], s_late)

            def spill(ph, b, parts, dram, runs, split, spilled):
                sp.wait_ge(split, b + 1)
                sp.sem_inc(s_own_sp, 1)
                for a in range(2):
                    half = slice(64 * a, 64 * (a + 1))
                    for place, part, n, same in runs:
                        if same:
                            src = parts[half, part:part + 1, :].to_broadcast([64, n, S])
                        else:
                            src = parts[half, part:part + n, :]
                        sp.dma_start(dram[a, place:place + n].rearrange("r c n -> c r n"), src).then_inc(spilled, 16)

            def stack(ph, b, dst, dram, spilled, done):
                sp.wait_ge(spilled, (b + 1) * (16 * SPILL_DMAS))
                sp.sem_inc(s_own_sp, 1)
                wait(sp, ph.s["scores_k"], (b - 1) * UNITS)
                for a in range(2):
                    sp.dma_start(dst[a][64 * a:64 * a + KROWS, :, :],
                                 dram[a].rearrange("r (d p) n -> (r d) p n", d=HD)).then_inc(done, 16)

            def spill_q(ph, b):
                spill(ph, b, q_parts, q_dram, Q_RUNS, ph.s["q_split"], ph.s["q_spilled"])

            def spill_k(ph, b):
                if ph.own_k:
                    spill(ph, b, k_parts, k_dram, K_RUNS, ph.s["k_split"], ph.s["k_spilled"])
                else:
                    spill(ph, b, q_parts, k_dram, K_RUNS, ph.s["q_split"], ph.s["k_spilled"])

            def stack_q(ph, b, q):
                stack(ph, b, Qs[q], q_dram, ph.s["q_spilled"], ph.s["q_stacked"])

            def stack_k(ph, b, q):
                stack(ph, b, [Ks[q]] * 2, k_dram, ph.s["k_spilled"], ph.s["k_stacked"])

            def shift_rows(ph, b, q, g):
                sp.wait_ge(ph.s["shift_copied"], b * G + g + 1)
                sp.sem_inc(s_own_sp, 1)
                for n in range(HG):
                    sp.dma_start(Qs[q][n % 2][SHIFT_ROW:SHIFT_ROW + 2, 2 * g + n // 2, :], shift[g % 2][n::HG, :])\
                        .then_inc(rows_shifted(ph, g), 16)

            def attention(ph):
                def ready(piece, b, q):
                    if piece == "spill_q":
                        spill_q(ph, b)
                    if piece == "spill_k":
                        spill_k(ph, b)
                    if piece == "stack_q":
                        handed_over(sp, ph, b, ("scores_k", (NB - 1) * UNITS))
                        stack_q(ph, b, q)
                    if piece == "stack_k":
                        stack_k(ph, b, q)

                def run(follow=None):
                    def next_ready(piece, i, q, cur, nxt):
                        if nxt:
                            ready(piece, i + 1, 1 - q)
                        elif cur and follow:
                            follow(piece)

                    def body(i, q, prev, cur, nxt):
                        if prev:
                            shift_rows(ph, i - 1, 1 - q, 3)
                        if cur:
                            shift_rows(ph, i, q, 0)
                        next_ready("spill_q", i, q, cur, nxt)
                        if cur:
                            shift_rows(ph, i, q, 1)
                        next_ready("stack_q", i, q, cur, nxt)
                        next_ready("spill_k", i, q, cur, nxt)
                        next_ready("stack_k", i, q, cur, nxt)
                        if cur:
                            shift_rows(ph, i, q, 2)
                    batches(sp, ph, body)

                return ready, run

            ready_outer, run_outer = attention(outer)
            ready0, run0 = attention(layer[0])
            ready1, run1 = attention(layer[1])
            for piece in ("spill_q", "stack_q", "spill_k", "stack_k"):
                ready_outer(piece, 0, 0)
            for b in range(2, NB):
                load_x(b, s_x)
            sp.dma_start(w1_sb[:, :, :], e_w1[0].rearrange("e d f -> d e f")).then_inc(s_w, 16)
            sp.dma_start(w2_sb[:, :, :, :], e_w2[0].rearrange("e (f p) d -> p e f d", p=P)).then_inc(s_w, 16)
            run_outer(lambda piece, b=0: ready0(piece, b, b % 2))
            run0()
            for piece in ("spill_q", "stack_q", "spill_k", "stack_k"):
                ready1(piece, NB, 0)
            run1()

            sp.wait_ge(seq["picked"], 1)

            def fill_slots(j):
                for slot in range(NSLOT):
                    n = j * NSLOT + slot
                    sp.sem_inc(s_own_sp, 1)
                    e = sp.value_load(seq_idx[0:1, bass.ds(n, 1)], min_val=0, max_val=E - 1)
                    wait(sp, seq["accumulated"], n - NSLOT + 1)
                    sp.wait_ge(seq["picked"], 1)
                    for dst, src in (
                        (w1_slot[slot], e_w1[1, bass.ds(e, 1), :, :].rearrange("o d f -> (o d) f")),
                        (w2_slot[slot], e_w2[1, bass.ds(e, 1), :, :].rearrange("o (f p) d -> p (o f) d", p=P)),
                        (b1_slot[slot][:, :], cols[:, bass.ds(e * FC + (B1 + E * FC), FC)]),
                        (b2_slot[slot], e_b2[1, bass.ds(e, 1), :].rearrange("o d -> (o d)").partition_broadcast(P)),
                    ):
                        sp.dma_start(dst, src).then_inc(seq_loaded[slot], 16)

            fill_slots(0)
            with sp.Fori(1, NB // 2) as j:
                fill_slots(j)

        @block.gpsimd
        def _(pool):
            chain = [0]

            def link(ins):
                chain[0] += 1
                ins.then_inc(s_pool0, 1)
                pool.wait_ge(s_pool0, chain[0])

            link(pool.memset(tril_rows[:, :], 0.0))
            pool.memset(ones8[:, :], 1.0).then_inc(s_const, 1)
            for t in (ident, identb, mask_q, head_sel, batch_row):
                link(pool.memset(t[:], 0.0))
            link(pool.memset(blockdiag[:, :], 1.0))

            def select(t, pattern, op, fill, base, mult):
                link(pool.affine_select(out=t, in_=t, compare_op=op, fill=fill, base=base, pattern=pattern,
                                        channel_multiplier=mult))

            select(ident[:, :], [[-1, P]], ALU.not_equal, 1.0, 0, 1)
            select(blockdiag[:, :], [[-HD, H]], ALU.is_ge, 0.0, 0, 1)
            select(blockdiag[:, :], [[HD, H]], ALU.is_ge, 0.0, HD - 1, -1)
            select(batch_row[:, :, :], [[-1, NB], [0, P]], ALU.not_equal, 1.0, 0, 1)
            select(identb[:, :], [[-1, P]], ALU.not_equal, 1.0, 0, 1)
            select(mask_q[:, S - P:S], [[-1, P]], ALU.is_ge, NEG, 0, 1)
            select(head_sel[:, 0:32].rearrange("p (j d) -> p j d", j=HG), [[-32, HG], [-1, HD]], ALU.not_equal, 1.0, 0, 1)
            select(head_sel[:, 32:36], [[-32, HG]], ALU.not_equal, 1.0, -HD, 1)
            link(pool.memset(minus_half[:, :], -0.5))
            link(pool.memset(e_const[:, :], E_CONST))
            link(pool.memset(wo_gated[:, :], 0.0))
            pool.memset(rstd2[:, :], 0.0).then_inc(outer.s["tail_done"], 1)
            pool.iota(iota8[:, :], pattern=[[1, E]], base=0, channel_multiplier=0,
                      allow_small_or_imprecise_dtypes=True).then_inc(s_const, 1)
            pool.wait_ge(s_const, 2)

            def wait(eng, sem_, value):
                if isinstance(value, int):
                    if value > 0:
                        eng.wait_ge(sem_, value)
                    return
                eng.wait_ge(sem_, value)
                eng.sem_inc(s_own_pool, 1)

            def normalise(piece, dst, src, mv, s_stats, s_chain, done, ve, rs, n):
                if piece == 0:
                    wait(pool, s_stats, n + 1)
                    pool.tensor_scalar(ve[:, :], mv[:, :, 1], EPS, None, ALU.add).then_inc(s_chain, 1)
                    wait(pool, s_chain, n * 3 + 1)
                    pool.tensor_tensor(rs[:, :], ve[:, :], minus_half[:, 0:TC], ALU.pow).then_inc(s_chain, 1)
                elif piece == 1:
                    pool.tensor_tensor(dst, src, mv[:, :, 0:1].to_broadcast([P, TC, P]), ALU.subtract).then_inc(s_chain, 1)
                else:
                    wait(pool, s_chain, n * 3 + 3)
                    pool.tensor_tensor(dst, dst, rs[:, :].unsqueeze(2).to_broadcast([P, TC, P]), ALU.mult).then_inc(done, 1)

            def split(piece, full, parts, s_full, s_high, s_chain, done, b):
                if piece == 0:
                    wait(pool, s_full, b + 1)
                    wait(pool, s_high, b + 1)
                    pool.tensor_tensor(full[:, :], full[:, :], parts[:, 0, :], ALU.subtract).then_inc(s_chain, 1)
                elif piece == 1:
                    wait(pool, s_chain, b * 2 + 1)
                    pool.tensor_scalar(parts[:, 1, :], full[:, :], 1.0, None, ALU.mult).then_inc(s_chain, 1)
                else:
                    wait(pool, s_chain, b * 2 + 2)
                    pool.tensor_tensor(parts[:, 2, :], full[:, :], parts[:, 1, :], ALU.subtract).then_inc(done, 1)

            def attention(ph):
                s = ph.s

                def prep(b, piece):
                    if piece == 1:
                        wait(pool, s["xT_ready"], b)
                    normalise(piece, xn[:, :, :], tokens(ph.stream, b - ph.first_batch), mean_var, s["stats_done"],
                              s["rstd_chain"], s["xn_ready"], var_eps, rstd, b)

                def bias(b, q):
                    wait(pool, s["xn_ready"], b + 1)
                    if ph is outer:
                        ga = modB[:, bass.ds(b, 1), 0, :]
                        wait(pool, s["bias_added"], b)
                        pool.tensor_tensor(bias_gated[:, :].unsqueeze(1), bias_row[:, 0, :].unsqueeze(1), ga,
                                           ALU.mult).then_inc(s["bias_gated"], 1)
                        wait(pool, s["bias_gated"], b + 1)
                        row = bias_gated[:, :]
                    else:
                        row = bias_row[:, 1 + ph.n, :]
                    t = tokens(ph.stream, b - ph.first_batch)
                    pool.tensor_tensor(t, t, row.unsqueeze(1).to_broadcast([P, TC, P]), ALU.add).then_inc(s["bias_added"], 1)

                def gate_wo(b):
                    wait(pool, s["out_proj"], b)
                    pool.tensor_tensor(wo_gated[:, :].unsqueeze(1), w_outer[:, 1, :].unsqueeze(1),
                                       modB[:, bass.ds(b, 1), 0, :], ALU.mult).then_inc(s["wo_gated"], 1)

                def tail(b):
                    t = tokens(yr, b)
                    for piece in range(3):
                        normalise(piece, t, tokens(xr, b), mean_var2, s["stats2_done"], s["tail_chain"],
                                  s["tail_normed"], var_eps2, rstd2, b)
                    wait(pool, s["tail_normed"], b + 1)
                    pool.tensor_tensor(t, t, modB[:, bass.ds(b, 1), 2, :].to_broadcast([P, TC, P]), ALU.mult)\
                        .then_inc(s["tail_scaled"], 1)
                    wait(pool, s["tail_scaled"], b + 1)
                    pool.tensor_tensor(t, t, modB[:, bass.ds(b, 1), 1, :].to_broadcast([P, TC, P]), ALU.add)\
                        .then_inc(s["tail_done"], 1)

                def split_q(b, piece):
                    split(piece, q_f, q_parts, s["qf_ready"], s["q_copied"], s["q_split_chain"], s["q_split"], b)

                def split_k(b, piece):
                    split(piece, k_f, k_parts, s["kf_ready"], s["k_copied"], s["k_split_chain"], s["k_split"], b)

                def mask(b, step):
                    wait(pool, s["exp_done"], b * UNITS + (step + 1) * HG)
                    block_ = probs(ph, step)[:, :, 0:P]
                    pool.affine_select(out=block_, in_=block_, compare_op=ALU.is_ge, fill=0.0, base=0,
                                       pattern=[[0, HG], [1, P]], channel_multiplier=-1).then_inc(s["masked"], 1)

                def ready(piece, b, q):
                    what, n = piece
                    if what == "xn":
                        handed_over(pool, ph, b, ("xT_ready", NB))
                        prep(b, n)
                    if what == "q":
                        split_q(b, n)
                    if what == "k" and ph.own_k:
                        split_k(b, n)

                def run(follow=None):
                    def next_ready(piece, i, q, cur, nxt):
                        if nxt:
                            ready(piece, i + 1, 1 - q)
                        elif cur and follow:
                            follow(piece)

                    def after_next(piece, i, q, cur):
                        if cur and not (isinstance(i, int) and i >= ph.first_batch + NB - 2):
                            ready(piece, i + 2, q)
                        elif cur and follow:
                            follow(piece, i - (ph.first_batch + NB - 2))

                    def body(i, q, prev, cur, nxt):
                        for k in range(STEPS):
                            b, _, step, on = second_pass(i, q, prev, cur, k, LAG)
                            if on and ph.causal:
                                mask(b, step)
                            if k == 2 and cur:
                                bias(i, q)
                            if 3 <= k < 6:
                                next_ready(("q", k - 3), i, q, cur, nxt)
                            if 6 <= k < 9:
                                next_ready(("k", k - 6), i, q, cur, nxt)
                            if 12 <= k < 15:
                                after_next(("xn", k - 12), i, q, cur)
                        if prev and ph is outer:
                            tail(i - 1)
                        if cur and ph is outer:
                            gate_wo(i)
                    batches(pool, ph, body)

                return ready, run

            READY = [(what, n) for what in ("xn", "q", "k") for n in range(3)]
            ready_outer, run_outer = attention(outer)
            ready0, run0 = attention(layer[0])
            ready1, run1 = attention(layer[1])
            for piece in READY:
                ready_outer(piece, 0, 0)
            for piece in READY[0:3]:
                ready_outer(piece, 1, 1)
            link(pool.memset(stacks[:, 2:4], 0.0))
            link(pool.memset(Ks[1][:], 1.0))
            pool.wait_ge(s_act0, ACT_MODB)
            pool.wait_ge(s_late, LATE_LOADS)
            run_outer(lambda piece, b=0: ready0(piece, b, b % 2))
            wait(pool, outer.s["residual_done"], NB)
            run0()
            wait(pool, layer[0].s["residual_done"], NB)

            def tok_prep(b):
                wait(pool, tok["xT_ready"], b)
                for piece in range(3):
                    normalise(piece, y_sb[:, :, :], tokens(yr, b), mean_var2, tok["stats_done"], tok["rstd_chain"],
                              tok["xn_ready"], var_eps2, rstd2, b)

            def tok_gap(b):
                wait(pool, tok["gap_ready"], b + 1)
                pool.tensor_tensor(gap_exp[:, :], e_const[:, :], gap[:, :], ALU.pow).then_inc(tok["gap_exp"], 1)

            tok_prep(0)
            tok_gap(0)
            with pool.Fori(0, NB - 1) as i:
                tok_prep(i + 1)
                tok_gap(i + 1)
            for piece in READY:
                ready1(piece, NB, 0)
            for piece in READY[0:3]:
                ready1(piece, NB + 1, 1)
            wait(pool, tok["accumulated"], NB * E)
            run1()
            wait(pool, layer[1].s["residual_done"], 2 * NB)

            wait(pool, seq["aggregated"], NB * TC)
            pool.tensor_scalar(ve_all[:, :], mv_all[:, :, 1], EPS, None, ALU.add).then_inc(seq["rstd_chain"], 1)
            wait(pool, seq["rstd_chain"], 1)
            pool.tensor_tensor(rstd_all[:, :], ve_all[:, :], minus_half[:, :], ALU.pow).then_inc(seq["rstd_ready"], 1)
            wait(pool, seq["gap_ready"], 1)
            pool.tensor_tensor(gap_exp[0:NB, 0:1], e_const[0:NB, 0:1], gap[0:NB, 0:1], ALU.pow).then_inc(seq["gap_exp"], 1)

            def finish(b):
                wait(pool, seq["accumulated"], b * 2 + 2)
                t = tokens(yr, b)
                pool.tensor_tensor(t, t, modB[:, bass.ds(b, 1), 3, :].to_broadcast([P, TC, P]), ALU.mult)\
                    .then_inc(seq["gated"], 1)
                wait(pool, seq["gated"], b + 1)
                o = q_f[:, :].rearrange("p (c d) -> p c d", c=TC)
                wait(pool, seq["stored"], b * 16)
                pool.tensor_tensor(o, t, tokens(xr, b), ALU.add).then_inc(seq["added"], 1)
                wait(pool, seq["added"], b + 1)
                pool.dma_start(out[bass.ds(b, 1), :, :].rearrange("o (c p) d -> p (o c) d", p=P), o).then_inc(seq["stored"], 16)

            finish(0)
            with pool.Fori(1, NB) as b:
                finish(b)
            wait(pool, seq["stored"], NB * 16)

        @block.scalar
        def _(act):
            act.wait_ge(s_cond, 32)
            act.activation(cond_a[:, :], cond[:, :], ACT.Exp, scale=-1.0).then_inc(s_act0, 1)
            for n in range(2):
                act.wait_ge(s_pe0, 3 + 2 * n)
                act.activation(w_outer[:, n, :], (MA, MB)[n][:, 0:P], ACT.Copy).then_inc(s_act0, 1)
            def attention(ph):
                s = ph.s

                def copy_hT(b):
                    act.wait_ge(s["xT_ready"], b + 1)
                    wait(act, s["v_proj"], b)
                    if ph is outer:
                        sc = mod_cols[:, 1, bass.ds(b, 1)]
                        bi = mod_cols[:, 0, bass.ds(b, 1)]
                    else:
                        sc, bi = ph.hw, ph.hb
                    act.activation(hT[:, :], MB[:, :], ACT.Identity, bias=bi, scale=sc).then_inc(s["hT_ready"], 1)

                def copy_full(b, bank, full, bias, s_proj, s_full, s_split):
                    act.wait_ge(s_proj, b + 1)
                    wait(act, s_split, b)
                    if bias is None:
                        ins = act.activation(full[:, :], bank[:, :], ACT.Copy)
                    else:
                        ins = act.activation(full[:, :], bank[:, :], ACT.Identity, bias=bias)
                    ins.then_inc(s_full, 1)

                def copy_high(b, bank, parts, bias, s_high, stacked):
                    for sem_ in stacked:
                        wait(act, sem_, b * (16 * STACK_DMAS))
                    if bias is None:
                        ins = act.activation(parts[:, 0, :], bank[:, :], ACT.Copy)
                    else:
                        ins = act.activation(parts[:, 0, :], bank[:, :], ACT.Identity, bias=bias)
                    ins.then_inc(s_high, 1)

                def exp(b, step, n):
                    u = step * HG + n
                    act.wait_ge(s["scores_k"], b * UNITS + u + 1)
                    wait(act, s["av_done"], b * STEPS + step + 1 - (TC if ph.causal else 2))
                    w = S - second_low(ph, step % TC)
                    act.activation(probs(ph, step)[:, n, :], bank_k(ph, u)[:, 0:w], ACT.Exp, scale=SCALE)\
                        .then_inc(s["exp_done"], 1)

                def copy_av(b, g):
                    act.wait_ge(s["av_done"], b * STEPS + TC * (g + 1))
                    wait(act, s["heads_sel"], b * G + g if g else b * G - 1)
                    act.activation(av_sb[g % 2][:, :], AV[:, :], ACT.Copy).then_inc(s["av_copied"], 1)

                def copy_v(b, q):
                    act.wait_ge(s["v_proj"], b + 1)
                    wait(act, s["av_done"], (b - 1) * STEPS)
                    act.activation(Vt[q][:, :, :, 0:HD].rearrange("p c h d -> p (c h) d"),
                                   MA[:, :].rearrange("p (n d) -> p n d", d=HD), ACT.Copy).then_inc(s["v_ready"], 1)

                def copy_yT(b):
                    act.wait_ge(s["yT_done"], b + 1)
                    act.activation(yT[:, :], MB[:, :], ACT.Identity, bias=ph.bv).then_inc(s["yT_copied"], 1)

                sel = select_step(ph)

                def ready(piece, b, q):
                    if piece == "hT":
                        handed_over(act, ph, b, ("v_proj", NB))
                        copy_hT(b)
                    if piece == "q_full":
                        handed_over(act, ph, b, ("q_split", NB))
                        copy_full(b, MA, q_f, ph.bq, s["q_proj"], s["qf_ready"], s["q_split"])
                    if piece == "q_high":
                        handed_over(act, ph, b, ("q_stacked", NB * 16 * STACK_DMAS), ("k_stacked", NB * 16 * STACK_DMAS))
                        copy_high(b, MA, q_parts, ph.bq, s["q_copied"],
                                  [s["q_stacked"]] if ph.own_k else [s["q_stacked"], s["k_stacked"]])
                    if piece == "k_full" and ph.own_k:
                        copy_full(b, MB, k_f, ph.bk, s["k_proj"], s["kf_ready"], s["k_split"])
                    if piece == "k_high" and ph.own_k:
                        copy_high(b, MB, k_parts, ph.bk, s["k_copied"], [s["k_stacked"]])
                    if piece == "v":
                        handed_over(act, ph, b, ("av_done", (NB - 1) * STEPS))
                        copy_v(b, q)

                def run(follow=None):
                    def next_ready(piece, i, q, cur, nxt):
                        if nxt:
                            ready(piece, i + 1, 1 - q)
                        elif cur and follow:
                            follow(piece)

                    def body(i, q, prev, cur, nxt):
                        for k in range(STEPS):
                            b, _, step, on = second_pass(i, q, prev, cur, k, LAG)
                            for n in range(HG):
                                if on:
                                    exp(b, step, n)
                                if n == 1 and k == 1:
                                    next_ready("hT", i, q, cur, nxt)
                                if n == 1 and k == 2:
                                    next_ready("q_full", i, q, cur, nxt)
                                if n == 3 and k == 2:
                                    next_ready("q_high", i, q, cur, nxt)
                                if n == 1 and k == 4:
                                    next_ready("k_full", i, q, cur, nxt)
                                if n == 3 and k == 4:
                                    next_ready("k_high", i, q, cur, nxt)
                                if n == 1 and k == weigh_lag(ph) + 1:
                                    next_ready("v", i, q, cur, nxt)
                                if n == 1 and k == LAG + sel + 2 and prev:
                                    copy_yT(i - 1)
                            b, _, step, on = second_pass(i, q, prev, cur, k, weigh_lag(ph))
                            if on and step % TC == TC - 1:
                                copy_av(b, step // TC)
                    batches(act, ph, body)

                return ready, run

            READY = ("hT", "q_full", "q_high", "k_full", "k_high", "v")
            ready_outer, run_outer = attention(outer)
            ready0, run0 = attention(layer[0])
            ready1, run1 = attention(layer[1])
            act.wait_ge(s_dve0, DVE_MODCOL)
            for piece in READY:
                ready_outer(piece, 0, 0)
            for b in range(NB):
                act.wait_ge(s_pe0, 8 + b)
                act.activation(modB[:, b, :, :].rearrange("p a d -> p (a d)"), banks[1 + b % 4][:, :], ACT.Copy)\
                    .then_inc(s_act0, 1)
            run_outer(lambda piece, b=0: ready0(piece, b, b % 2))
            act.wait_ge(outer.s["residual_done"], NB)
            run0()
            act.wait_ge(layer[0].s["residual_done"], NB)

            def tok_hT(b):
                act.wait_ge(tok["xT_ready"], b + 1)
                wait(act, tok["hidden"], b * E * FC)
                act.activation(yT[:, :], MA[:, :], ACT.Identity, bias=cols[:, LN2B:LN2B + 1],
                               scale=cols[:, LN2W:LN2W + 1]).then_inc(tok["hT_ready"], 1)

            def tok_experts(b, follow=None):
                for e in range(E):
                    if follow and e == 5:
                        follow("hT")
                    if follow and e == 6:
                        follow("q_full")
                        follow("q_high")
                        follow("k_full")
                        follow("k_high")
                    if follow and e == 7:
                        follow("v")
                    for f in range(FC):
                        u = e * FC + f
                        act.wait_ge(tok["hidden"], b * (E * FC) + u + 1)
                        if f == 0:
                            wait(act, tok["expert_out"], b * E + e - 1)
                        act.activation(hid[e % 2][:, f, :], HB[f][:, :], ACT.Gelu,
                                       bias=cols[:, B1 + u:B1 + u + 1]).then_inc(tok["gelu_done"], 1)

            tok_hT(0)
            tok_experts(0)
            tok_hT(1)
            with act.Fori(1, NB - 1) as i:
                tok_experts(i)
                tok_hT(i + 1)
            tok_experts(NB - 1, lambda piece, b=0: ready1(piece, NB + b, b % 2))
            act.wait_ge(tok["accumulated"], NB * E)
            run1()
            act.wait_ge(layer[1].s["residual_done"], 2 * NB)

            for b in range(NB):
                act.wait_ge(seq["xT_ready"], b + 1)
                act.activation(hT_all[:, b * S:(b + 1) * S], (MA, MB)[b % 2][:, :], ACT.Identity, bias=cols[:, LN2B + 1:LN2B + 2],
                               scale=cols[:, LN2W + 1:LN2W + 2], accum_out=hsum[:, b:b + 1]).then_inc(seq["hT_ready"], 1)

            def seq_experts(j):
                for slot in range(NSLOT):
                    n = j * NSLOT + slot
                    act.wait_ge(seq_loaded[slot], (j + 1) * (16 * SLOT_DMAS))
                    wait(act, seq["expert_out"], n - 1)
                    for f in range(FC):
                        act.wait_ge(seq["hidden"], n * FC + f + 1)
                        act.activation(hid[slot % 2][:, f, :], HB[f][:, :], ACT.Gelu,
                                       bias=b1_slot[slot][:, f:f + 1]).then_inc(seq["gelu_done"], 1)

            seq_experts(0)
            with act.Fori(1, NB // 2) as j:
                seq_experts(j)

        @block.vector
        def _(dve):
            chain = [0]

            def link(ins):
                chain[0] += 1
                ins.then_inc(s_dve0, 1)
                dve.wait_ge(s_dve0, chain[0])

            def regroup(dst, src):
                return dve.tensor_copy(dst.rearrange("x (a d p) -> x p a d", a=2, d=HD),
                                       src.rearrange("x (p a d) -> x p a d", a=2, d=HD))

            def settled(sem_, value):
                dve.wait_ge(sem_, value)
                dve.sem_inc(s_own_dve, 1)

            def statistics(piece, stream, b, st, mv, s_chain, done, n, st_free=False):
                if piece < TC:
                    if piece == 0 and not st_free and not (isinstance(n, int) and n == 0):
                        settled(done, n)
                    dve.bn_stats(st[:, piece, :], tokens(stream, b, piece)).then_inc(s_chain, 1)
                else:
                    settled(s_chain, (n + 1) * TC)
                    for c in range(TC):
                        ins = dve.bn_aggr(mv[:, c, :], st[:, c, :])
                    ins.then_inc(done, 1)

            for t in Vt:
                link(dve.memset(t[:], 0.0))
                link(dve.memset(t[:, :, :, HD:HD + 1], 1.0))
            dve.wait_ge(s_x0, 16)
            for piece in range(TC + 1):
                statistics(piece, xr, 0, stats, mean_var, outer.s["mv_chain"], outer.s["stats_done"], 0)
            link(dve.memset(stacks[:, 0:2], 0.0))
            link(dve.memset(Ks[0][:], 1.0))
            dve.wait_ge(s_act0, 1)
            dve.wait_ge(s_cond, 32)
            link(dve.tensor_scalar(cond_b[:, :], cond_a[:, :], 1.0, None, ALU.add))
            link(dve.reciprocal(cond_a[:, :], cond_b[:, :]))
            link(dve.tensor_tensor(cond_b[:, :], cond_a[:, :], cond[:, :], ALU.mult))
            assert chain[0] == DVE_SILU
            dve.wait_ge(s_const, 2)
            dve.wait_ge(s_ld, EARLY_LOADS)
            link(dve.tensor_tensor(tril_raw.rearrange("p (h j) -> p h j", h=H),
                                   tril_rows[:, :].unsqueeze(1).to_broadcast([P, H, HD]),
                                   blockdiag[:, :].unsqueeze(2).to_broadcast([P, H, HD]), ALU.mult))
            dve.wait_ge(s_pe0, 1)
            link(dve.tensor_copy(condT[:, :], MA[:, 0:NB]))
            for dst, src in ((tril_block[:, :], tril_raw), (rows_regrouped, rows[:, :])):
                link(regroup(dst, src))
            assert chain[0] == DVE_CONDT
            dve.wait_ge(s_pe0, 2)
            link(dve.tensor_copy(cols[:, :], MB[:, 0:NROW]))
            dve.wait_ge(s_pe0, 4)
            link(dve.tensor_copy(cols_regrouped[:, :], MB[:, 256:256 + NROW]))
            dve.wait_ge(s_pe0, 6)
            link(dve.tensor_copy(mod_cols[:, 0, :], MA[:, 384:384 + NB]))
            link(dve.tensor_scalar(mod_cols[:, 1, :], MA[:, 384 + NB:384 + 2 * NB], 1.0, None, ALU.add))
            assert chain[0] == DVE_MODCOL
            dve.wait_ge(s_pe0, 7)
            link(dve.tensor_copy(mod_row[:, 1:3, :].rearrange("b a d -> b (a d)"), banks[0][0:NB, P:3 * P]))
            for n in range(2):
                src = banks[0][0:NB, 0:P] if n == 0 else banks[0][0:NB, 3 * P:4 * P]
                link(dve.tensor_scalar(mod_tmp[:, n, :], src, 0.0, 2.0, ALU.is_ge, ALU.mult))
                link(dve.tensor_scalar(mod_tmp2[:, n, :], src, -1.0, None, ALU.mult))
                link(dve.scalar_tensor_tensor(mod_tmp2[:, n, :], src, 0.25, mod_tmp2[:, n, :], ALU.max, ALU.max))
                link(dve.scalar_tensor_tensor(mod_row[:, 3 * n, :], mod_tmp[:, n, :], 1.0, mod_tmp2[:, n, :],
                                              ALU.subtract, ALU.mult))
            link(dve.tensor_scalar(mod_row[:, 2, :], mod_row[:, 2, :], 1.0, None, ALU.add))
            assert chain[0] == DVE_MODROW
            dve.wait_ge(s_late, LATE_LOADS)
            for dst, src in ((wq_sb[:, 0, :], wqk_raw[:, 0, :]), (wq_sb[:, 1, :], wqk_raw[:, 1, :]),
                             (wk_sb[:, 0, :], wqk_raw[:, 2, :]), (wk_sb[:, 1, :], wqk_raw[:, 3, :])):
                link(regroup(dst, src))
            assert chain[0] == DVE_WEIGHTS

            def attention(ph):
                s = ph.s

                def sequence_stats(b):
                    settled(s["residual_done"], b + 1)
                    for c in range(TC):
                        dve.bn_stats(stats_all[:, bass.ds((b - ph.first_batch) * TC + c, 1), :].rearrange("p o s -> p (o s)"),
                                     tokens(yr, b - ph.first_batch, c)).then_inc(seq["mv_chain"], 1)

                STATS_STEPS = (3, 5, 6, 7, 9)

                def stats_of(b, piece):
                    if piece == 0 and ph is outer:
                        if isinstance(b, int) and b == 1:
                            dve.wait_ge(s_x1, 16)
                        else:
                            dve.wait_ge(s_x, 16 * (NB - 2))
                    if piece == TC:
                        wait(dve, s["xn_ready"], b)
                    statistics(piece, ph.stream, b - ph.first_batch, stats, mean_var, s["mv_chain"], s["stats_done"], b)

                def maxima(i, k, n):
                    v = k * HG + n
                    if v % 16 == 0:
                        wait(dve, s["shift_split"], i * G + k // TC - G + 1)
                    dve.wait_ge(s["scores_q"], i * UNITS + v + 1)
                    c = first_chunk(ph, k)
                    w, at = first_width(ph, c), HG * (k // TC * TC + c) + n
                    if ph.causal:
                        dve.sem_inc(s_own_dve, 1)
                        dve.tensor_tensor_reduce(bank_q(ph, v)[:, 0:w], bank_q(ph, v)[:, 0:w], mask_q[:, S - w:S], 1.0, NEG,
                                                 ALU.add, ALU.max, row_max[:, at:at + 1]).then_inc(s["max_done"], 1)
                    else:
                        dve.tensor_reduce(row_max[:, at:at + 1], bank_q(ph, v)[:, 0:w], AX_X, ALU.max)\
                            .then_inc(s["max_done"], 1)

                def split_max(b, g):
                    m = b * G + g
                    dve.wait_ge(s["max_done"], b * UNITS + 16 * (g + 1))
                    wait(dve, s["max_T"], m - 1)
                    t = shift_tok[g % 2]
                    rm = row_max[:, 16 * g:16 * g + 16].rearrange("p (c h) -> p c h", h=HG)
                    dve.tensor_scalar(t[:, :, 0, :], rm, -1.0, None, ALU.mult).then_inc(s["shift_half"], 1)
                    dve.wait_ge(s["shift_half"], m + 1)
                    dve.scalar_tensor_tensor(t[:, :, 1, :], rm, -1.0, t[:, :, 0, :], ALU.mult, ALU.subtract)\
                        .then_inc(s["shift_split"], 1)

                def copy_shift(b, g):
                    dve.wait_ge(s["max_T"], b * G + g + 1)
                    wait(dve, rows_shifted(ph, g), (b * (G // 2) + g // 2) * (16 * SHIFT_DMAS))
                    dve.tensor_copy(shift[g % 2][:, :], MA[:, :].bitcast(BF16)[0:2 * HG, 0:S]).then_inc(s["shift_copied"], 1)

                def normalise_heads(b, g):
                    dve.wait_ge(s["heads_sel"], b * G + g + 1)
                    m = MB[:, 0:TC * 36].rearrange("p (c n) -> p c n", c=TC)
                    dve.reciprocal(recip[:, :, :], m[:, :, 32:36]).then_inc(s["recip_done"], 1)
                    dve.wait_ge(s["recip_done"], b * G + g + 1)
                    if g == 0:
                        wait(dve, s["yT_done"], b)
                    dve.tensor_tensor(y_sb[:, :, 32 * g:32 * g + 32].rearrange("p c (h d) -> p c h d", d=HD),
                                      m[:, :, 0:32].rearrange("p c (h d) -> p c h d", d=HD),
                                      recip[:, :, :].unsqueeze(3).to_broadcast([P, TC, HG, HD]), ALU.mult)\
                        .then_inc(s["y_ready"], 1)

                def residual(b):
                    dve.wait_ge(s["out_proj"], b + 1)
                    dve.wait_ge(s["bias_added"], b + 1)
                    t = tokens(ph.stream, b - ph.first_batch)
                    dve.tensor_tensor(t, MA[:, :].rearrange("p (c d) -> p c d", c=TC), t, ALU.add)\
                        .then_inc(s["residual_done"], 1)

                def tail_stats(b):
                    dve.wait_ge(s["residual_done"], b + 1)
                    settled(s["tail_done"], b + 1)
                    for piece in range(TC + 1):
                        statistics(piece, xr, b, stats2, mean_var2, s["mv2_chain"], s["stats2_done"], b, st_free=True)

                sel = select_step(ph)

                def ready(piece, b, q):
                    if piece == 0:
                        handed_over(dve, ph, b, ("xn_ready", NB), ("stats_done", NB))
                        if ph is layer[0] and isinstance(b, int) and b < 2:
                            dve.wait_ge(outer.s["tail_done"], b + 2)
                    stats_of(b, piece)

                def run(follow=None):
                    def after_next(piece, i, q, cur):
                        if cur and not (isinstance(i, int) and i >= ph.first_batch + NB - 2):
                            ready(piece, i + 2, q)
                        elif cur and follow:
                            follow(piece, i - (ph.first_batch + NB - 2))

                    def body(i, q, prev, cur, nxt):
                        for k in range(STEPS):
                            if k == 0 and prev:
                                split_max(i - 1, G - 1)
                            elif k and k % TC == 0 and cur:
                                split_max(i, k // TC - 1)
                            for n in range(HG):
                                if cur:
                                    maxima(i, k, n)
                                if n == 0 and k in STATS_STEPS:
                                    after_next(STATS_STEPS.index(k), i, q, cur)
                                if n == 1 and k == 0 and prev:
                                    copy_shift(i - 1, G - 1)
                                elif n == 1 and k and k % TC == 0 and cur:
                                    copy_shift(i, k // TC - 1)
                            if prev and k % TC == sel and k <= sel + 2 * TC:
                                normalise_heads(i - 1, k // TC + 1)
                            if k == LAG + sel + 2 and prev:
                                residual(i - 1)
                            if k == LAG + sel + 3 and prev and ph is layer[1]:
                                sequence_stats(i - 1)
                            if k == LAG + sel + 3 and prev and ph is outer:
                                tail_stats(i - 1)
                            if k == sel + LAG + TC and cur:
                                normalise_heads(i, 0)
                    batches(dve, ph, body)

                return ready, run

            ready_outer, run_outer = attention(outer)
            for piece in range(TC + 1):
                ready_outer(piece, 1, 1)
            ready0, run0 = attention(layer[0])
            ready1, run1 = attention(layer[1])
            run_outer(lambda piece, b=0: ready0(piece, b, b % 2))
            dve.wait_ge(outer.s["tail_done"], NB + 1)
            run0()
            dve.wait_ge(layer[0].s["residual_done"], NB)

            def tok_stats(b):
                wait(dve, tok["xn_ready"], b)
                for piece in range(TC + 1):
                    statistics(piece, yr, b, stats2, mean_var2, tok["mv_chain"], tok["stats_done"], b)

            GC = 2 * TC + 8

            def tok_gate_a(b):
                dve.wait_ge(tok["logits_ready"], b + 1)
                dve.tensor_tensor(logits[:, :, :], MB[:, 0:TC * E].rearrange("p (c e) -> p c e", c=TC),
                                  gate_bias[:, 0, :].unsqueeze(1).to_broadcast([P, TC, E]), ALU.add)\
                    .then_inc(tok["logits_copied"], 1)
                settled(tok["logits_copied"], b + 1)
                for c in range(TC):
                    dve.max(top8[:, c, :], logits[:, c, :]).then_inc(tok["gate_chain"], 1)
                settled(tok["gate_chain"], b * GC + TC)
                for c in range(TC):
                    dve.max_index(top_idx[:, c, :], top8[:, c, :], logits[:, c, :]).then_inc(tok["gate_chain"], 1)
                dve.tensor_tensor(gap[:, :], top8[:, :, 1], top8[:, :, 0], ALU.subtract).then_inc(tok["gap_ready"], 1)

            def tok_gate_b(b):
                s_, n = tok["gate_chain"], [b * GC + 2 * TC]

                def step(ins):
                    n[0] = n[0] + 1
                    ins.then_inc(s_, 1)
                    dve.wait_ge(s_, n[0])

                dve.wait_ge(s_, n[0])
                step(dve.tensor_copy(top_idxf[:, :, :], top_idx[:, :, 0:2]))
                dve.wait_ge(tok["gap_exp"], b + 1)
                step(dve.tensor_scalar(denom[:, :], gap_exp[:, :], 1.0, None, ALU.add))
                step(dve.reciprocal(weight[:, :, 0], denom[:, :]))
                step(dve.tensor_tensor(weight[:, :, 1], weight[:, :, 0], gap_exp[:, :], ALU.mult))
                for m in range(2):
                    step(dve.tensor_tensor(pick[m][:, :, :], iota8[:, :].unsqueeze(1).to_broadcast([P, TC, E]),
                                           top_idxf[:, :, m:m + 1].to_broadcast([P, TC, E]), ALU.is_equal))
                    step(dve.tensor_tensor(pick[2 + m][:, :, :], pick[m][:, :, :],
                                           weight[:, :, m:m + 1].to_broadcast([P, TC, E]), ALU.mult))
                wait(dve, tok["combine_T"], b)
                wait(dve, tok["accumulated"], b * E)
                dve.tensor_tensor(combine[:, :, :], pick[2][:, :, :], pick[3][:, :, :], ALU.add)\
                    .then_inc(tok["combine_ready"], 1)
                dve.wait_ge(tok["combine_ready"], b + 1)

            def tok_combineT(b):
                dve.wait_ge(tok["combine_T"], b + 1)
                wait(dve, tok["b2_ready"], b)
                dve.tensor_copy(combineT[:, :], MA[0:E, :]).then_inc(tok["combineT_copied"], 1)

            def tok_b2(b):
                dve.wait_ge(tok["b2_ready"], b + 1)
                dve.wait_ge(tok["accumulated"], b * E + 3)
                t = tokens(yr, b)
                dve.tensor_tensor(t, MB[:, :].rearrange("p (c d) -> p c d", c=TC), t, ALU.add).then_inc(tok["b2_added"], 1)

            def tok_accumulate(b, e):
                dve.wait_ge(tok["expert_out"], b * E + e + 1)
                if e > 0:
                    dve.wait_ge(tok["accumulated"], b * E + e)
                if e == 3:
                    dve.wait_ge(tok["b2_added"], b + 1)
                for c in range(TC):
                    t = tokens(yr, b, c)
                    ins = dve.scalar_tensor_tensor(t, YB[e % 2][:, c * P:(c + 1) * P], combine[:, c, e:e + 1], t,
                                                   ALU.mult, ALU.add)
                ins.then_inc(tok["accumulated"], 1)

            def tok_body(i, prev, nxt, follow=None):
                if prev:
                    tok_accumulate(i - 1, E - 1)
                tok_gate_b(i)
                tok_combineT(i)
                for e in range(1, E):
                    tok_accumulate(i, e - 1)
                    if e == 1 and nxt:
                        tok_stats(i + 1)
                    if e == 3:
                        tok_b2(i)
                    if e in (2, 4) and follow:
                        dve.wait_ge(tok["accumulated"], 2 * E)
                        for piece in range(TC + 1):
                            follow(piece, e // 2 - 1)
                if nxt:
                    tok_gate_a(i + 1)

            tok_stats(0)
            tok_gate_a(0)
            tok_body(0, False, True)
            with dve.Fori(1, NB - 1) as i:
                tok_body(i, True, True)
            tok_body(NB - 1, True, False, lambda piece, b=0: ready1(piece, NB + b, b % 2))
            tok_accumulate(NB - 1, E - 1)
            dve.wait_ge(tok["accumulated"], NB * E)
            run1()
            dve.wait_ge(layer[1].s["residual_done"], 2 * NB)

            dve.wait_ge(seq["mv_chain"], NB * TC)
            for n in range(NB * TC):
                dve.bn_aggr(mv_all[:, n, :], stats_all[:, n, :]).then_inc(seq["aggregated"], 1)
            dve.wait_ge(seq["rstd_ready"], 1)
            for b in range(NB):
                wait(dve, seq["xT_ready"], b - 1)
                for c in range(TC):
                    n = b * TC + c
                    ins = dve.tensor_scalar(seq_xn[b % 2][:, c, :], yr[:, n * P:(n + 1) * P], mv_all[:, n, 0:1],
                                            rstd_all[:, n:n + 1], ALU.subtract, ALU.mult)
                ins.then_inc(seq["xn_ready"], 1)
            dve.wait_ge(seq["logits_ready"], 1)
            dve.scalar_tensor_tensor(logits[0:NB, 0, :], MA[0:NB, 0:E], 1.0 / S, gate_bias[0:NB, 1, :], ALU.mult, ALU.add)\
                .then_inc(seq["gate_chain"], 1)
            dve.wait_ge(seq["gate_chain"], 1)
            dve.max(top8[0:NB, 0, :], logits[0:NB, 0, :]).then_inc(seq["gate_chain"], 1)
            dve.wait_ge(seq["gate_chain"], 2)
            dve.max_index(top_idx[0:NB, 0, :], top8[0:NB, 0, :], logits[0:NB, 0, :]).then_inc(seq["gate_chain"], 1)
            dve.tensor_tensor(gap[0:NB, 0:1], top8[0:NB, 0, 1:2], top8[0:NB, 0, 0:1], ALU.subtract).then_inc(seq["gap_ready"], 1)
            dve.wait_ge(seq["gate_chain"], 3)
            dve.tensor_copy(top_idxf[0:NB, 0, :], top_idx[0:NB, 0, 0:2]).then_inc(seq["gate_chain"], 1)
            dve.wait_ge(seq["gap_exp"], 1)
            dve.tensor_scalar(denom[0:NB, 0:1], gap_exp[0:NB, 0:1], 1.0, None, ALU.add).then_inc(seq["gate_chain"], 1)
            dve.wait_ge(seq["gate_chain"], 5)
            dve.reciprocal(weight[0:NB, 0, 0:1], denom[0:NB, 0:1]).then_inc(seq["gate_chain"], 1)
            dve.wait_ge(seq["gate_chain"], 6)
            dve.tensor_tensor(weight[0:NB, 0, 1:2], weight[0:NB, 0, 0:1], gap_exp[0:NB, 0:1], ALU.mult)\
                .then_inc(seq["gate_chain"], 1)
            dve.wait_ge(seq["gate_chain"], 7)
            for m, src in enumerate((weight, top_idxf)):
                dve.tensor_tensor(seq_both[:, m, :, :], src[0:NB, 0, :].unsqueeze(1).to_broadcast([NB, NB, 2]),
                                  ident[0:NB, 0:NB].unsqueeze(2).to_broadcast([NB, NB, 2]), ALU.mult).then_inc(seq["both_ready"], 1)
            dve.wait_ge(seq["both_B"], 1)
            dve.tensor_copy(seq_idx[0:1, :], MB[0:1, 2 * NB:4 * NB]).then_inc(seq["picked"], 1)
            dve.tensor_copy(seqB[:, :], MB[:, 0:2 * NB]).then_inc(seq["gate_chain"], 1)
            dve.wait_ge(seq["gate_chain"], 8)

            def seq_apply(j):
                for slot in range(NSLOT):
                    n = j * NSLOT + slot
                    b = j * 2 + slot // 2
                    w = seqB[:, bass.ds(n, 1)]
                    dve.wait_ge(seq_loaded[slot], (j + 1) * (16 * SLOT_DMAS))
                    wait(dve, seq["accumulated"], n)
                    for c in range(TC):
                        t = tokens(yr, b, c)
                        ins = dve.scalar_tensor_tensor(t, b2_slot[slot][:, :], w, t, ALU.mult, ALU.add)
                    ins.then_inc(seq["b2_added"], 1)
                    dve.wait_ge(seq["b2_added"], n + 1)
                    dve.wait_ge(seq["expert_out"], n + 1)
                    for c in range(TC):
                        t = tokens(yr, b, c)
                        ins = dve.scalar_tensor_tensor(t, YB[slot % 2][:, c * P:(c + 1) * P], w, t, ALU.mult, ALU.add)
                    ins.then_inc(seq["accumulated"], 1)

            seq_apply(0)
            with dve.Fori(1, NB // 2) as j:
                seq_apply(j)

        @block.tensor
        def _(pe):
            pe.wait_ge(s_const, 2)
            pe.wait_ge(s_dve0, DVE_SILU)
            pe.transpose(MA[:, 0:NB], cond_b[:, :], ident[0:NB, 0:NB]).then_inc(s_pe0, 1)
            pe.wait_ge(s_ld, EARLY_LOADS)
            pe.transpose(MB[:, 0:NROW], rows[:, :], ident[0:NROW, 0:NROW]).then_inc(s_pe0, 1)
            pe.wait_ge(s_dve0, DVE_CONDT)
            pe.transpose(MA[:, 0:P], w_raw[:, 0, :], ident[:, :]).then_inc(s_pe0, 1)
            pe.wait_ge(s_dve0, DVE_CONDT + 1)
            pe.transpose(MB[:, 256:256 + NROW], rows_regrouped, ident[0:NROW, 0:NROW]).then_inc(s_pe0, 1)
            pe.wait_ge(s_dve0, DVE_CONDT + 2)
            pe.transpose(MB[:, 0:P], w_raw[:, 1, :], ident[:, :]).then_inc(s_pe0, 1)
            pe.wait_ge(s_act0, 2)
            for m in range(2):
                ins = pe.matmul(MA[:, 384 + m * NB:384 + (m + 1) * NB], wmod_sb[:, m * P:(m + 1) * P], condT[:, :],
                                start=True, stop=True)
            ins.then_inc(s_pe0, 1)
            pe.matmul(banks[0][0:NB, :], condT[:, :], wmod_sb[:, 2 * P:6 * P], start=True, stop=True).then_inc(s_pe0, 1)

            def spread_modulation():
                pe.wait_ge(s_dve0, DVE_MODROW)
                for b in range(NB):
                    if b >= 4:
                        pe.wait_ge(s_act0, ACT_MODB - NB + b - 3)
                    pe.matmul(banks[1 + b % 4][:, :], batch_row[:, b, :], mod_row[:, :, :].rearrange("b a d -> b (a d)"),
                              start=True, stop=True).then_inc(s_pe0, 1)
                pe.wait_ge(s_act0, ACT_MODB)
                pe.wait_ge(s_dve0, DVE_WEIGHTS)
                pe.wait_ge(s_late, LATE_LOADS)

            def transposed(bank, src, chunks=TC, rows_=P):
                for c in range(chunks):
                    ins = pe.transpose(bank[0:rows_, c * P:(c + 1) * P], src[:, c, :], ident[:, :])
                return ins

            freed = {"A": (s_dve0, DVE_MODCOL), "B": (s_act0, 3)}

            def take(bank):
                wait(pe, *freed[bank])

            def attention(ph):
                s = ph.s
                def max_T(b, g):
                    take("A")
                    pe.wait_ge(s["shift_split"], b * G + g + 1)
                    for c in range(TC):
                        ins = pe.transpose(MA[:, :].bitcast(BF16)[0:2 * HG, c * P:(c + 1) * P],
                                           shift_tok[g % 2][:, c, :, :].rearrange("p a h -> p (a h)"), identb[:, :])
                    ins.then_inc(s["max_T"], 1)
                    freed["A"] = (s["shift_copied"], b * G + g + 1)

                def normed_T(b):
                    take("B")
                    pe.wait_ge(s["xn_ready"], b + 1)
                    transposed(MB, xn).then_inc(s["xT_ready"], 1)
                    freed["B"] = (s["hT_ready"], b + 1)

                def project_q(b):
                    take("A")
                    pe.wait_ge(s["hT_ready"], b + 1)
                    pe.matmul(MA[:, :], ph.wq, hT[:, :], start=True, stop=True).then_inc(s["q_proj"], 1)
                    freed["A"] = (s["q_copied"], b + 1)

                def project_k(b):
                    take("B")
                    pe.wait_ge(s["hT_ready"], b + 1)
                    pe.matmul(MB[:, :], ph.wk, hT[:, :], start=True, stop=True).then_inc(s["k_proj"], 1)
                    freed["B"] = (s["k_copied"], b + 1)

                def project_v(b):
                    take("A")
                    pe.wait_ge(s["hT_ready"], b + 1)
                    for c in range(TC):
                        ins = pe.matmul(MA[:, c * P:(c + 1) * P], hT[:, c * P:(c + 1) * P], ph.wv, start=True, stop=True)
                    ins.then_inc(s["v_proj"], 1)
                    freed["A"] = (s["v_ready"], b + 1)

                def select_heads(b, g):
                    take("B")
                    pe.wait_ge(s["av_copied"], b * G + g + 1)
                    for c in range(TC):
                        ins = pe.matmul(MB[:, c * 36:(c + 1) * 36], av_sb[g % 2][:, c * P:(c + 1) * P], head_sel[:, :],
                                        start=True, stop=True)
                    ins.then_inc(s["heads_sel"], 1)
                    freed["B"] = (s["y_ready"], b * G + g + 1)

                def heads_T(b):
                    take("B")
                    pe.wait_ge(s["y_ready"], b * G + G)
                    transposed(MB, y_sb).then_inc(s["yT_done"], 1)
                    freed["B"] = (s["yT_copied"], b + 1)

                def project_out(b, q):
                    take("A")
                    pe.wait_ge(s["yT_copied"], b + 1)
                    if ph is outer:
                        pe.wait_ge(s["wo_gated"], b + 1)
                        w = wo_gated[:, :]
                    else:
                        w = wo_sb[:, ph.n, :]
                    for c in range(TC):
                        ins = pe.matmul(MA[:, c * P:(c + 1) * P], yT[:, c * P:(c + 1) * P], w, start=True, stop=True)
                    ins.then_inc(s["out_proj"], 1)
                    freed["A"] = (s["residual_done"], b + 1)

                def first(i, q, k, n):
                    g, c = k // TC, first_chunk(ph, k)
                    v, h = k * HG + n, g * HG + n
                    w = first_width(ph, c)
                    if v == 0:
                        pe.wait_ge(s["q_stacked"], (i + 1) * (16 * STACK_DMAS))
                        pe.wait_ge(s["k_stacked"], (i + 1) * (16 * STACK_DMAS))
                    wait(pe, s["max_done"], i * UNITS + max(0, v + 1 - first_banks(ph)))
                    pe.matmul(bank_q(ph, v)[:, 0:w], Qs[q][h % 2][0:SHIFT_ROW, h // 2, c * P:(c + 1) * P],
                              Ks[q][0:SHIFT_ROW, h // 2, 0:w], start=True, stop=True).then_inc(s["scores_q"], 1)

                def second(b, q, step, n):
                    g, c = step // TC, step % TC
                    u, h = step * HG + n, g * HG + n
                    lo = second_low(ph, c)
                    if c == 0 and n == 0:
                        pe.wait_ge(rows_shifted(ph, g), (b * (G // 2) + g // 2 + 1) * (16 * SHIFT_DMAS))
                    wait(pe, s["exp_done"], b * UNITS + max(0, u + 1 - (5 - first_banks(ph))))
                    pe.matmul(bank_k(ph, u)[:, 0:S - lo], Ks[q][:, h // 2, c * P:(c + 1) * P],
                              Qs[q][h % 2][:, h // 2, lo:S], start=True, stop=True).then_inc(s["scores_k"], 1)

                def weigh(b, q, step):
                    g, c = step // TC, step % TC
                    lo = second_low(ph, c)
                    pe.wait_ge(s["exp_done"], b * UNITS + (step + 1) * HG)
                    if ph.causal:
                        pe.wait_ge(s["masked"], b * STEPS + step + 1)
                    if step == 0:
                        pe.wait_ge(s["v_ready"], b + 1)
                    if c == 0:
                        wait(pe, s["av_copied"], b * G + g)
                    for n in range(HG):
                        ins = pe.matmul(AV[32 * n:32 * n + 32, lo:S], Vt[q][:, c, g * HG + n, :],
                                        probs(ph, step)[:, n, :], start=(c == 0), stop=(c == TC - 1))
                    ins.then_inc(s["av_done"], 1)

                sel = select_step(ph)

                def ready(piece, b, q):
                    if piece == "xT":
                        normed_T(b)
                    if piece == "q":
                        project_q(b)
                    if piece == "k" and ph.own_k:
                        project_k(b)
                    if piece == "v":
                        project_v(b)

                def run(follow=None):
                    def next_ready(piece, i, q, cur, nxt):
                        if nxt:
                            ready(piece, i + 1, 1 - q)
                        elif cur and follow:
                            follow(piece)

                    def body(i, q, prev, cur, nxt):
                        if prev:
                            freed["A"] = (s["shift_copied"], (i - 1) * G + G - 1)
                            freed["B"] = (s["y_ready"], (i - 1) * G + 1)
                        for k in range(STEPS):
                            b2, q2, step2, on2 = second_pass(i, q, prev, cur, k, LAG)
                            b3, q3, step3, on3 = second_pass(i, q, prev, cur, k, weigh_lag(ph))
                            for n in range(HG):
                                if on2:
                                    second(b2, q2, step2, n)
                                if cur:
                                    first(i, q, k, n)
                                if n == 1:
                                    if on3:
                                        weigh(b3, q3, step3)
                                    if k == 0 and prev:
                                        max_T(i - 1, G - 1)
                                    elif k and k % TC == 0 and cur:
                                        max_T(i, k // TC - 1)
                            if k == 0:
                                next_ready("xT", i, q, cur, nxt)
                            if k == 1:
                                next_ready("q", i, q, cur, nxt)
                            if prev and k % TC == sel and k <= sel + 2 * TC:
                                select_heads(i - 1, k // TC + 1)
                            if k == 3:
                                next_ready("k", i, q, cur, nxt)
                            if k == weigh_lag(ph):
                                next_ready("v", i, q, cur, nxt)
                            if k == LAG + sel + 1 and prev:
                                heads_T(i - 1)
                            if k == LAG + sel + 2 and prev:
                                project_out(i - 1, 1 - q)
                            if k == sel + LAG + TC and cur:
                                select_heads(i, 0)
                    batches(pe, ph, body)

                return ready, run

            READY = ("xT", "q", "k", "v")
            ready_outer, run_outer = attention(outer)
            ready0, run0 = attention(layer[0])
            ready1, run1 = attention(layer[1])
            for piece in READY:
                ready_outer(piece, 0, 0)
            spread_modulation()
            run_outer(lambda piece, b=0: ready0(piece, b, b % 2))
            pe.wait_ge(outer.s["residual_done"], NB)
            run0()
            pe.wait_ge(layer[0].s["residual_done"], NB)
            pe.wait_ge(s_w, 32)

            def tok_normed_T(b):
                pe.wait_ge(tok["xn_ready"], b + 1)
                wait(pe, tok["combineT_copied"], b)
                transposed(MA, y_sb).then_inc(tok["xT_ready"], 1)

            def tok_logits(b):
                pe.wait_ge(tok["hT_ready"], b + 1)
                wait(pe, tok["b2_added"], b)
                for c in range(TC):
                    ins = pe.matmul(MB[:, c * E:(c + 1) * E], yT[:, c * P:(c + 1) * P], gate_sb[:, 0, :],
                                    start=True, stop=True)
                ins.then_inc(tok["logits_ready"], 1)

            def expert_up(sems, n, w1, x):
                for f in range(FC):
                    wait(pe, sems["gelu_done"], n * FC + f - FC + 1)
                    pe.matmul(HB[f][:, :], w1[:, f * P:(f + 1) * P], x, start=True, stop=True).then_inc(sems["hidden"], 1)

            def expert_down(sems, n, par, w2):
                pe.wait_ge(sems["gelu_done"], n * FC + FC)
                wait(pe, sems["accumulated"], n - 1)
                for c in range(TC):
                    for f in range(FC):
                        ins = pe.matmul(YB[par][:, c * P:(c + 1) * P], hid[par][:, f, c * P:(c + 1) * P], w2[:, f, :],
                                        start=(f == 0), stop=(f == FC - 1))
                ins.then_inc(sems["expert_out"], 1)

            def tok_body(i, prev, nxt, follow=None):
                for e in range(E):
                    if e == 0:
                        pe.wait_ge(tok["hT_ready"], i + 1)
                    expert_up(tok, i * E + e, w1_sb[:, e, :], yT[:, :])
                    if e == 1:
                        pe.wait_ge(tok["combine_ready"], i + 1)
                        transposed(MA, combine, rows_=E).then_inc(tok["combine_T"], 1)
                    if e == 2:
                        pe.wait_ge(tok["combineT_copied"], i + 1)
                        pe.wait_ge(tok["logits_copied"], i + 1)
                        for c in range(TC):
                            ins = pe.matmul(MB[:, c * P:(c + 1) * P], combineT[:, c * P:(c + 1) * P], b2_sb[:, :],
                                            start=True, stop=True)
                        ins.then_inc(tok["b2_ready"], 1)
                    if e == E - 1 and nxt:
                        tok_normed_T(i + 1)
                    if e == 4 and follow:
                        freed["A"], freed["B"] = (tok["combineT_copied"], NB), (tok["b2_added"], NB)
                        follow("xT")
                    if e == 5 and follow:
                        follow("q")
                        follow("k")
                    if e == 6 and follow:
                        follow("v")
                    if e:
                        expert_down(tok, i * E + e - 1, (e - 1) % 2, w2_sb[:, e - 1, :, :])
                    elif prev:
                        expert_down(tok, i * E - 1, (E - 1) % 2, w2_sb[:, E - 1, :, :])
                if nxt:
                    tok_logits(i + 1)

            tok_normed_T(0)
            tok_logits(0)
            tok_body(0, False, True)
            with pe.Fori(1, NB - 1) as i:
                tok_body(i, True, True)
            tok_body(NB - 1, True, False, lambda piece, b=0: ready1(piece, NB + b, b % 2))
            expert_down(tok, NB * E - 1, (E - 1) % 2, w2_sb[:, E - 1, :, :])
            pe.wait_ge(tok["accumulated"], NB * E)
            run1()
            pe.wait_ge(layer[1].s["residual_done"], 2 * NB)

            for b in range(NB):
                pe.wait_ge(seq["xn_ready"], b + 1)
                wait(pe, seq["hT_ready"], b - 1)
                transposed((MA, MB)[b % 2], seq_xn[b % 2]).then_inc(seq["xT_ready"], 1)
            pe.wait_ge(seq["hT_ready"], NB)
            pe.matmul(MA[0:NB, 0:E], hsum[:, :], gate_sb[:, 1, :], start=True, stop=True).then_inc(seq["logits_ready"], 1)
            pe.wait_ge(seq["both_ready"], 2)
            pe.matmul(MB[:, 0:4 * NB], ones8[:, :], seq_both[:, :, :, :].rearrange("p m b k -> p (m b k)"),
                      start=True, stop=True).then_inc(seq["both_B"], 1)

            def seq_body(j):
                for slot in range(NSLOT):
                    n = j * NSLOT + slot
                    pe.wait_ge(seq_loaded[slot], (j + 1) * (16 * SLOT_DMAS))
                    expert_up(seq, n, w1_slot[slot], hT_all[:, bass.ds((j * 2 + slot // 2) * S, S)])
                    if slot or not isinstance(j, int):
                        expert_down(seq, n - 1, (slot - 1) % 2, w2_slot[(slot - 1) % NSLOT])

            seq_body(0)
            with pe.Fori(1, NB // 2) as j:
                seq_body(j)
            expert_down(seq, 2 * NB - 1, (NSLOT - 1) % 2, w2_slot[NSLOT - 1])


_INS = ['L0_attn_x', 'L0_attn_params', 'L0_attn_Wv', 'L0_attn_bv', 'L0_attn_Wo', 'L0_attn_bo', 'L0_ffn_ln1_w',
        'L0_ffn_ln1_b', 'L0_ffn_ln2_w', 'L0_ffn_ln2_b', 'L0_ffn_wq', 'L0_ffn_wk', 'L0_ffn_wv', 'L0_ffn_wo',
        'L0_ffn_bq', 'L0_ffn_bk', 'L0_ffn_bv', 'L0_ffn_bo', 'L0_ffn_gate_w', 'L0_ffn_gate_b', 'L0_ffn_e_w1',
        'L0_ffn_e_b1', 'L0_ffn_e_w2', 'L0_ffn_e_b2', 'L0_c', 'L0_wmod']
_OUTS = [((8, 512, 128), 'float32')]


def kernel(**inputs):
    import numpy as _np
    import concourse.bacc as _bacc
    from concourse import mybir as _mybir
    from concourse.bass_utils import run_bass_kernel_spmd as _run

    nc = _bacc.Bacc("TRN2", target_bir_lowering=False, num_devices=1)
    arrays, args = {}, []
    for name in _INS:
        a = _np.ascontiguousarray(inputs[name])
        arrays[f"in_{name}_dram"] = a
        args.append(nc.dram_tensor(f"in_{name}_dram", a.shape, _mybir.dt.from_np(a.dtype), kind="ExternalInput").ap())
    for i, (shape, dtype) in enumerate(_OUTS):
        dt = _mybir.dt.from_np(_np.dtype(dtype))
        args.append(nc.dram_tensor(f"out_{i}_dram", shape, dt, kind="ExternalOutput").ap())
    adaln_block(nc, *args)
    r = _run(nc, [arrays], core_ids=[0])
    got = tuple(r.results[0][f"out_{i}_dram"] for i in range(len(_OUTS)))
    return got[0]
```
